# Optimizing a Trainium2 kernel written in Bass

```python
import numpy as np
import jax
import jax.numpy as jnp

def _softmax(x, axis=-1):
    return jax.nn.softmax(x, axis=axis)

def _gelu(x):
    return jax.nn.gelu(x, approximate=True)

def _silu(x):
    return jax.nn.silu(x)

def _sigmoid(x):
    return jax.nn.sigmoid(x)

def _layernorm(x, axis=-1, eps=1e-05):
    m = jnp.mean(x, axis=axis, keepdims=True)
    v = jnp.var(x, axis=axis, keepdims=True)
    return (x - m) / jnp.sqrt(v + eps)

def _scatter_add(tgt, idx, src, axis=0):
    return tgt.at[idx].add(src)

def _segment_sum(src, seg, n):
    return jax.ops.segment_sum(src, seg, n)
kernel_name = 'mk_gnn_resnorm_d4_gnn_r64_4a9d79'

def setup_inputs(seed: int=0):
    np.random.seed(seed)
    _w = jnp.asarray

    def _rec_inputs():
        import jax
        import jax.numpy as jnp
        _gk = jax.random.key(seed)
        x = -0.0005121 + 1.001 * jax.random.normal(jax.random.fold_in(_gk, 1), (100000, 160), jnp.float32)
        src = jax.random.randint(jax.random.fold_in(_gk, 2), (25000,), 0, 100000, jnp.int32)
        dst = jnp.minimum((100000 * jax.random.uniform(jax.random.fold_in(_gk, 3), (25000,)) ** 2.0).astype(jnp.int32), 99999)
        _o = jnp.argsort(dst, stable=True)
        src = src[_o]
        dst = dst[_o]
        edge_attr_16 = jax.random.uniform(jax.random.fold_in(_gk, 12), (25000, 16), jnp.float32, 0.0, 1)
        edge_attr_4 = 0.000898722 + 1.00012 * jax.random.normal(jax.random.fold_in(_gk, 13), (25000, 4), jnp.float32)
        edge_attr_8 = 0.000735704 + 1.0001 * jax.random.normal(jax.random.fold_in(_gk, 14), (25000, 8), jnp.float32)
        node_vec1 = jax.random.uniform(jax.random.fold_in(_gk, 16), (100000, 1), jnp.float32, 0.0, 1)
        return (x, src, dst, edge_attr_16, edge_attr_4, edge_attr_8, node_vec1)
    x, src, dst, edge_attr_16, edge_attr_4, edge_attr_8, node_vec1 = _rec_inputs()

    def _L0_gnn_setup():
        import jax, jax.numpy as jnp
        import numpy as np
        N, E = (20000, 5000)
        CS, CV = (64, 32)
        AS_, AV, H = (16, 8, 4)
        NB = 16
        SQRT3 = 1.7320508075688772
        SQRT2 = 1.4142135623730951
        EPS = 1e-05

        def _cg_tp(s, v, y0, y1, w_ss, w_sv, w_vs, w_vv0, w_vv1):
            out_s = jnp.concatenate([w_ss * s * y0[:, None], w_vv0 * (jnp.einsum('eci,ei->ec', v, y1) / SQRT3)], axis=-1)
            out_v = jnp.concatenate([(w_sv * s)[:, :, None] * y1[:, None, :], (w_vs * jnp.ones_like(v[..., 0]))[..., None] * v * y0[:, None, None], (w_vv1 * jnp.ones_like(v[..., 0]))[..., None] * (jnp.cross(v, y1[:, None, :]) / SQRT2)], axis=1)
            return (out_s, out_v)

        def _equiv_layernorm(s, v, gamma_s, beta_s, gamma_v):
            mu = jnp.mean(s, axis=-1, keepdims=True)
            var = jnp.var(s, axis=-1, keepdims=True)
            s_n = (s - mu) * jax.lax.rsqrt(var + EPS) * gamma_s + beta_s
            rms = jnp.sqrt(jnp.mean(jnp.sum(v * v, axis=-1), axis=-1, keepdims=True) + EPS)
            v_n = v / rms[..., None] * gamma_v[None, :, None]
            return (s_n, v_n)
        key = jax.random.key(seed)
        ks = jax.random.split(key, 26)

        def rn(k, shape, fan):
            return jax.random.normal(k, shape, jnp.float32) / np.sqrt(fan)
        D1S, D1V = (CS + CV, CS + 2 * CV)
        WN = 2 * CS + 3 * CV
        inp = {'node': jax.random.normal(ks[0], (N, CS + 3 * CV), jnp.float32), 'edge_index': jax.random.randint(ks[1], (2, E), 0, N, jnp.int64 if jax.config.jax_enable_x64 else jnp.int32), 'rbf': jax.random.uniform(ks[2], (E, NB), jnp.float32), 'rsh': jax.random.normal(ks[3], (E, 4), jnp.float32), 'gamma_s': jnp.ones((CS,), jnp.float32), 'beta_s': jnp.zeros((CS,), jnp.float32), 'gamma_v': jnp.ones((CV,), jnp.float32), 'Ws_src': rn(ks[4], (CS, CS), CS), 'Wv_src': rn(ks[5], (CV, CV), CV), 'Ws_dst': rn(ks[6], (CS, CS), CS), 'Wv_dst': rn(ks[7], (CV, CV), CV), 'W_rbf': rn(ks[8], (NB, WN), NB), 'W_alpha': rn(ks[9], (D1S, H * AS_), D1S), 'alpha_dot': rn(ks[10], (1, H, AS_), AS_), 'Ws_val': rn(ks[11], (D1S, CS), D1S), 'Wv_val': rn(ks[12], (D1V, CV), D1V), 'Wg': rn(ks[13], (CS, CV), CS), 'w2_ss': rn(ks[14], (CS,), 1), 'w2_sv': rn(ks[15], (CS,), 1), 'w2_vs': rn(ks[16], (CV,), 1), 'w2_vv0': rn(ks[17], (CV,), 1), 'w2_vv1': rn(ks[18], (CV,), 1), 'Ws_vlin': rn(ks[19], (D1S, H * AS_), D1S), 'Wv_vlin': rn(ks[20], (D1V, H * AV), D1V), 'Wps': rn(ks[21], (H * AS_, CS), H * AS_), 'Wpv': rn(ks[22], (H * AV, CV), H * AV)}
        return inp
    _L0_gnn_all = _L0_gnn_setup()
    _L0_gnn_in = {k: v for k, v in _L0_gnn_all.items() if k in ('gamma_s', 'beta_s', 'gamma_v', 'Ws_src', 'Wv_src', 'Ws_dst', 'Wv_dst', 'W_rbf', 'W_alpha', 'alpha_dot', 'Ws_val', 'Wv_val', 'Wg', 'w2_ss', 'w2_sv', 'w2_vs', 'w2_vv0', 'w2_vv1', 'Ws_vlin', 'Wv_vlin', 'Wps', 'Wpv')}
    del _L0_gnn_all

    def _L1_gnn_setup():
        import jax, jax.numpy as jnp
        import numpy as np
        N_NODES = 10000
        N_EDGES = 5000
        NUM_NEIGHBORS = 32.0
        INV_SQRT3 = 1.0 / np.sqrt(3.0)

        def _fctp_scalar_attr(xs, xv, Ws, Wv, a):
            out_s = xs @ Ws * (a / np.sqrt(xs.shape[1]))[:, None]
            out_v = jnp.einsum('nuc,uw->nwc', xv, Wv) * (a / np.sqrt(xv.shape[1]))[:, None, None]
            return (out_s, out_v)
        key = jax.random.key(seed)
        ks = jax.random.split(key, 16)
        f32 = jnp.float32
        return {'node_input': jax.random.normal(ks[0], (N_NODES, 160), f32), 'node_attr': jnp.ones((N_NODES, 1), f32), 'edge_attr': jax.random.normal(ks[1], (N_EDGES, 4), f32), 'edge_scalar_attr': jax.random.normal(ks[2], (N_EDGES, 8), f32), 'Wsc0': jax.random.normal(ks[3], (64, 64), f32), 'Wsc1': jax.random.normal(ks[4], (32, 32), f32), 'Wl1_0': jax.random.normal(ks[5], (64, 64), f32), 'Wl1_1': jax.random.normal(ks[6], (32, 32), f32), 'Wfc1': jax.random.normal(ks[7], (8, 64), f32), 'Wfc2': jax.random.normal(ks[8], (64, 64), f32), 'Wfc3': jax.random.normal(ks[9], (64, 192), f32), 'Wl2_s': jax.random.normal(ks[10], (96, 64), f32), 'Wl2_v': jax.random.normal(ks[11], (96, 32), f32), 'Wa': jax.random.normal(ks[12], (96, 1), f32), 'edge_src': jax.random.randint(ks[13], (N_EDGES,), 0, N_NODES), 'edge_dst': jax.random.randint(ks[14], (N_EDGES,), 0, N_NODES)}
    _L1_gnn_all = _L1_gnn_setup()
    _L1_gnn_in = {k: v for k, v in _L1_gnn_all.items() if k in ('Wsc0', 'Wsc1', 'Wl1_0', 'Wl1_1', 'Wfc1', 'Wfc2', 'Wfc3', 'Wl2_s', 'Wl2_v', 'Wa')}
    del _L1_gnn_all

    def _L2_gnn_setup():
        import jax, jax.numpy as jnp
        import numpy as np
        N = 20000
        E = 5000
        MUL0 = 64
        MUL1 = 32
        FC_IN = 16
        FC_H = 64
        WNUM = 192
        key = jax.random.key(seed)
        ks = jax.random.split(key, 16)
        return {'x': jax.random.normal(ks[0], (N, MUL0 + 3 * MUL1), jnp.float32), 'node_attr': jnp.ones((N, 1), jnp.float32), 'edge_scalars': jax.random.normal(ks[1], (E, FC_IN), jnp.float32), 'edge_attr_sh': jax.random.normal(ks[2], (E, 4), jnp.float32), 'edge_src': jax.random.randint(ks[3], (E,), 0, N), 'edge_dst': jax.random.randint(ks[4], (E,), 0, N), 'Wfc1': jax.random.normal(ks[5], (FC_IN, FC_H), jnp.float32), 'Wfc2': jax.random.normal(ks[6], (FC_H, WNUM), jnp.float32), 'Wsc0': jax.random.normal(ks[7], (MUL0, MUL0), jnp.float32), 'Wsc1': jax.random.normal(ks[8], (MUL1, MUL1), jnp.float32), 'Wl1_0': jax.random.normal(ks[9], (MUL0, MUL0), jnp.float32), 'Wl1_1': jax.random.normal(ks[10], (MUL1, MUL1), jnp.float32), 'Wl2_s': jax.random.normal(ks[11], (MUL0 + MUL1, MUL0), jnp.float32), 'Wl2_v': jax.random.normal(ks[12], (MUL0 + MUL1, MUL1), jnp.float32), 'Wa': 0.1 * jax.random.normal(ks[13], (MUL0 + MUL1, 1), jnp.float32)}
    _L2_gnn_all = _L2_gnn_setup()
    _L2_gnn_in = {k: v for k, v in _L2_gnn_all.items() if k in ('Wfc1', 'Wfc2', 'Wsc0', 'Wsc1', 'Wl1_0', 'Wl1_1', 'Wl2_s', 'Wl2_v', 'Wa')}
    del _L2_gnn_all

    def _L3_gnn_setup():
        import jax, jax.numpy as jnp
        import numpy as np
        N_NODES = 100000
        N_EDGES = 12500
        MUL_S = 64
        MUL_V = 32
        DIM = MUL_S + 3 * MUL_V
        EDGE_SCALAR_DIM = 16
        ISQ3 = 1.0 / np.sqrt(3.0)
        ISQ2 = 1.0 / np.sqrt(2.0)

        def _forward(x, edge_index, edge_feat, edge_scalars, W_ss, W_sv, W_vs, W_vv, W_rad, b_rad, L_s, L_v):
            src, dst = (edge_index[0], edge_index[1])
            n = x.shape[0]
            xs = x[:, :MUL_S]
            xv = x[:, MUL_S:].reshape(n, MUL_V, 3)
            xs_e = xs[src]
            xv_e = xv[src]
            es = edge_feat[:, 0]
            ev = edge_feat[:, 1:4]
            out_s = (jnp.einsum('eu,uo->eo', xs_e * es[:, None], W_ss) / np.sqrt(MUL_S) + jnp.einsum('eud,ed,uo->eo', xv_e, ev, W_vv) * ISQ3 / np.sqrt(MUL_V)) * ISQ2
            out_v = (jnp.einsum('eu,ed,uv->evd', xs_e, ev, W_sv) * ISQ3 / np.sqrt(MUL_S) + jnp.einsum('eud,e,uv->evd', xv_e, es, W_vs) * ISQ3 / np.sqrt(MUL_V)) * ISQ2
            messages = jnp.concatenate([out_s, out_v.reshape(-1, 3 * MUL_V)], axis=1)
            scale = jax.nn.sigmoid(edge_scalars @ W_rad.T + b_rad)
            messages = messages * scale
            agg = jax.ops.segment_sum(messages, dst, num_segments=n)
            h = x + agg
            hs = h[:, :MUL_S]
            hv = h[:, MUL_S:].reshape(n, MUL_V, 3)
            ys = hs @ L_s / np.sqrt(MUL_S)
            yv = jnp.einsum('nud,uv->nvd', hv, L_v) / np.sqrt(MUL_V)
            return jnp.concatenate([ys, yv.reshape(n, 3 * MUL_V)], axis=1)
        key = jax.random.key(seed)
        ks = jax.random.split(key, 12)
        x = jax.random.normal(ks[0], (N_NODES, DIM), dtype=jnp.float32)
        edge_index = jax.random.randint(ks[1], (2, N_EDGES), 0, N_NODES, dtype=jnp.int64)
        edge_feat = jax.random.normal(ks[2], (N_EDGES, 4), dtype=jnp.float32)
        edge_scalars = jax.random.normal(ks[3], (N_EDGES, EDGE_SCALAR_DIM), dtype=jnp.float32)
        W_ss = jax.random.normal(ks[4], (MUL_S, MUL_S), dtype=jnp.float32)
        W_sv = jax.random.normal(ks[5], (MUL_S, MUL_V), dtype=jnp.float32)
        W_vs = jax.random.normal(ks[6], (MUL_V, MUL_V), dtype=jnp.float32)
        W_vv = jax.random.normal(ks[7], (MUL_V, MUL_S), dtype=jnp.float32)
        W_rad = jax.random.normal(ks[8], (DIM, EDGE_SCALAR_DIM), dtype=jnp.float32) / np.sqrt(EDGE_SCALAR_DIM)
        b_rad = jax.random.normal(ks[9], (DIM,), dtype=jnp.float32) * 0.1
        L_s = jax.random.normal(ks[10], (MUL_S, MUL_S), dtype=jnp.float32)
        L_v = jax.random.normal(ks[11], (MUL_V, MUL_V), dtype=jnp.float32)
        return {'x': x, 'edge_index': edge_index, 'edge_feat': edge_feat, 'edge_scalars': edge_scalars, 'W_ss': W_ss, 'W_sv': W_sv, 'W_vs': W_vs, 'W_vv': W_vv, 'W_rad': W_rad, 'b_rad': b_rad, 'L_s': L_s, 'L_v': L_v}
    _L3_gnn_all = _L3_gnn_setup()
    _L3_gnn_in = {k: v for k, v in _L3_gnn_all.items() if k in ('W_ss', 'W_sv', 'W_vs', 'W_vv', 'W_rad', 'b_rad', 'L_s', 'L_v')}
    del _L3_gnn_all
    return {'x': x, 'src': src, 'dst': dst, 'edge_attr_16': edge_attr_16, 'edge_attr_4': edge_attr_4, 'edge_attr_8': edge_attr_8, 'node_vec1': node_vec1, 'L0_gnn_gamma_s': _L0_gnn_in['gamma_s'], 'L0_gnn_beta_s': _L0_gnn_in['beta_s'], 'L0_gnn_gamma_v': _L0_gnn_in['gamma_v'], 'L0_gnn_Ws_src': _L0_gnn_in['Ws_src'], 'L0_gnn_Wv_src': _L0_gnn_in['Wv_src'], 'L0_gnn_Ws_dst': _L0_gnn_in['Ws_dst'], 'L0_gnn_Wv_dst': _L0_gnn_in['Wv_dst'], 'L0_gnn_W_rbf': _L0_gnn_in['W_rbf'], 'L0_gnn_W_alpha': _L0_gnn_in['W_alpha'], 'L0_gnn_alpha_dot': _L0_gnn_in['alpha_dot'], 'L0_gnn_Ws_val': _L0_gnn_in['Ws_val'], 'L0_gnn_Wv_val': _L0_gnn_in['Wv_val'], 'L0_gnn_Wg': _L0_gnn_in['Wg'], 'L0_gnn_w2_ss': _L0_gnn_in['w2_ss'], 'L0_gnn_w2_sv': _L0_gnn_in['w2_sv'], 'L0_gnn_w2_vs': _L0_gnn_in['w2_vs'], 'L0_gnn_w2_vv0': _L0_gnn_in['w2_vv0'], 'L0_gnn_w2_vv1': _L0_gnn_in['w2_vv1'], 'L0_gnn_Ws_vlin': _L0_gnn_in['Ws_vlin'], 'L0_gnn_Wv_vlin': _L0_gnn_in['Wv_vlin'], 'L0_gnn_Wps': _L0_gnn_in['Wps'], 'L0_gnn_Wpv': _L0_gnn_in['Wpv'], 'L1_gnn_Wsc0': _L1_gnn_in['Wsc0'], 'L1_gnn_Wsc1': _L1_gnn_in['Wsc1'], 'L1_gnn_Wl1_0': _L1_gnn_in['Wl1_0'], 'L1_gnn_Wl1_1': _L1_gnn_in['Wl1_1'], 'L1_gnn_Wfc1': _L1_gnn_in['Wfc1'], 'L1_gnn_Wfc2': _L1_gnn_in['Wfc2'], 'L1_gnn_Wfc3': _L1_gnn_in['Wfc3'], 'L1_gnn_Wl2_s': _L1_gnn_in['Wl2_s'], 'L1_gnn_Wl2_v': _L1_gnn_in['Wl2_v'], 'L1_gnn_Wa': _L1_gnn_in['Wa'], 'L2_gnn_Wfc1': _L2_gnn_in['Wfc1'], 'L2_gnn_Wfc2': _L2_gnn_in['Wfc2'], 'L2_gnn_Wsc0': _L2_gnn_in['Wsc0'], 'L2_gnn_Wsc1': _L2_gnn_in['Wsc1'], 'L2_gnn_Wl1_0': _L2_gnn_in['Wl1_0'], 'L2_gnn_Wl1_1': _L2_gnn_in['Wl1_1'], 'L2_gnn_Wl2_s': _L2_gnn_in['Wl2_s'], 'L2_gnn_Wl2_v': _L2_gnn_in['Wl2_v'], 'L2_gnn_Wa': _L2_gnn_in['Wa'], 'L3_gnn_W_ss': _L3_gnn_in['W_ss'], 'L3_gnn_W_sv': _L3_gnn_in['W_sv'], 'L3_gnn_W_vs': _L3_gnn_in['W_vs'], 'L3_gnn_W_vv': _L3_gnn_in['W_vv'], 'L3_gnn_W_rad': _L3_gnn_in['W_rad'], 'L3_gnn_b_rad': _L3_gnn_in['b_rad'], 'L3_gnn_L_s': _L3_gnn_in['L_s'], 'L3_gnn_L_v': _L3_gnn_in['L_v']}

def reference(x, src, dst, edge_attr_16, edge_attr_4, edge_attr_8, node_vec1, L0_gnn_gamma_s, L0_gnn_beta_s, L0_gnn_gamma_v, L0_gnn_Ws_src, L0_gnn_Wv_src, L0_gnn_Ws_dst, L0_gnn_Wv_dst, L0_gnn_W_rbf, L0_gnn_W_alpha, L0_gnn_alpha_dot, L0_gnn_Ws_val, L0_gnn_Wv_val, L0_gnn_Wg, L0_gnn_w2_ss, L0_gnn_w2_sv, L0_gnn_w2_vs, L0_gnn_w2_vv0, L0_gnn_w2_vv1, L0_gnn_Ws_vlin, L0_gnn_Wv_vlin, L0_gnn_Wps, L0_gnn_Wpv, L1_gnn_Wsc0, L1_gnn_Wsc1, L1_gnn_Wl1_0, L1_gnn_Wl1_1, L1_gnn_Wfc1, L1_gnn_Wfc2, L1_gnn_Wfc3, L1_gnn_Wl2_s, L1_gnn_Wl2_v, L1_gnn_Wa, L2_gnn_Wfc1, L2_gnn_Wfc2, L2_gnn_Wsc0, L2_gnn_Wsc1, L2_gnn_Wl1_0, L2_gnn_Wl1_1, L2_gnn_Wl2_s, L2_gnn_Wl2_v, L2_gnn_Wa, L3_gnn_W_ss, L3_gnn_W_sv, L3_gnn_W_vs, L3_gnn_W_vv, L3_gnn_W_rad, L3_gnn_b_rad, L3_gnn_L_s, L3_gnn_L_v):
    import jax
    import jax.numpy as jnp

    def _L0_gnn_ref(node, rbf, rsh, gamma_s, beta_s, gamma_v, Ws_src, Wv_src, Ws_dst, Wv_dst, W_rbf, W_alpha, alpha_dot, Ws_val, Wv_val, Wg, w2_ss, w2_sv, w2_vs, w2_vv0, w2_vv1, Ws_vlin, Wv_vlin, Wps, Wpv, edge_index):
        import jax, jax.numpy as jnp
        import numpy as np
        N, E = (20000, 5000)
        CS, CV = (64, 32)
        AS_, AV, H = (16, 8, 4)
        NB = 16
        SQRT3 = 1.7320508075688772
        SQRT2 = 1.4142135623730951
        EPS = 1e-05

        def _cg_tp(s, v, y0, y1, w_ss, w_sv, w_vs, w_vv0, w_vv1):
            out_s = jnp.concatenate([w_ss * s * y0[:, None], w_vv0 * (jnp.einsum('eci,ei->ec', v, y1) / SQRT3)], axis=-1)
            out_v = jnp.concatenate([(w_sv * s)[:, :, None] * y1[:, None, :], (w_vs * jnp.ones_like(v[..., 0]))[..., None] * v * y0[:, None, None], (w_vv1 * jnp.ones_like(v[..., 0]))[..., None] * (jnp.cross(v, y1[:, None, :]) / SQRT2)], axis=1)
            return (out_s, out_v)

        def _equiv_layernorm(s, v, gamma_s, beta_s, gamma_v):
            mu = jnp.mean(s, axis=-1, keepdims=True)
            var = jnp.var(s, axis=-1, keepdims=True)
            s_n = (s - mu) * jax.lax.rsqrt(var + EPS) * gamma_s + beta_s
            rms = jnp.sqrt(jnp.mean(jnp.sum(v * v, axis=-1), axis=-1, keepdims=True) + EPS)
            v_n = v / rms[..., None] * gamma_v[None, :, None]
            return (s_n, v_n)
        n = node.shape[0]
        e = rsh.shape[0]
        s = node[:, :CS]
        v = node[:, CS:].reshape(n, CV, 3)
        s_n, v_n = _equiv_layernorm(s, v, gamma_s, beta_s, gamma_v)
        src, dst = (edge_index[0], edge_index[1])
        msg_s = (s_n @ Ws_src)[src] + (s_n @ Ws_dst)[dst]
        msg_v = jnp.einsum('ncx,cd->ndx', v_n, Wv_src)[src] + jnp.einsum('ncx,cd->ndx', v_n, Wv_dst)[dst]
        y0, y1 = (rsh[:, 0], rsh[:, 1:4])
        w1 = rbf @ W_rbf
        m1_s, m1_v = _cg_tp(msg_s, msg_v, y0, y1, w1[:, :CS], w1[:, CS:2 * CS], w1[:, 2 * CS:2 * CS + CV], w1[:, 2 * CS + CV:2 * CS + 2 * CV], w1[:, 2 * CS + 2 * CV:])
        a = (m1_s @ W_alpha).reshape(e, H, AS_)
        a = jnp.where(a > 0, a, 0.2 * a)
        a = jnp.sum(a * alpha_dot, axis=-1, keepdims=True)
        amax = jax.ops.segment_max(a, dst, num_segments=n)
        amax = jnp.where(jnp.isfinite(amax), amax, 0.0)
        ex = jnp.exp(a - amax[dst])
        den = jax.ops.segment_sum(ex, dst, num_segments=n)
        alpha = ex / (den[dst] + 1e-16)
        val_s = m1_s @ Ws_val
        val_v = jnp.einsum('ecx,cd->edx', m1_v, Wv_val)
        val_v = val_v * jax.nn.sigmoid(val_s @ Wg)[..., None]
        val_s = jax.nn.sigmoid(val_s)
        m2_s, m2_v = _cg_tp(val_s, val_v, y0, y1, w2_ss, w2_sv, w2_vs, w2_vv0, w2_vv1)
        hs = (m2_s @ Ws_vlin).reshape(e, H, AS_)
        hv = jnp.einsum('ecx,cd->edx', m2_v, Wv_vlin).reshape(e, H, AV, 3)
        h = jnp.concatenate([hs, hv.reshape(e, H, AV * 3)], axis=-1)
        agg = jax.ops.segment_sum(alpha * h, dst, num_segments=n)
        agg_s = agg[:, :, :AS_].reshape(n, H * AS_)
        agg_v = agg[:, :, AS_:].reshape(n, H * AV, 3)
        out = node + jnp.concatenate([agg_s @ Wps, jnp.einsum('ncx,cd->ndx', agg_v, Wpv).reshape(n, CV * 3)], axis=-1)
        return out

    def _L1_gnn_ref(node_input, node_attr, edge_attr, edge_scalar_attr, Wsc0, Wsc1, Wl1_0, Wl1_1, Wfc1, Wfc2, Wfc3, Wl2_s, Wl2_v, Wa, edge_src, edge_dst):
        import jax, jax.numpy as jnp
        import numpy as np
        N_NODES = 10000
        N_EDGES = 5000
        NUM_NEIGHBORS = 32.0
        INV_SQRT3 = 1.0 / np.sqrt(3.0)

        def _fctp_scalar_attr(xs, xv, Ws, Wv, a):
            out_s = xs @ Ws * (a / np.sqrt(xs.shape[1]))[:, None]
            out_v = jnp.einsum('nuc,uw->nwc', xv, Wv) * (a / np.sqrt(xv.shape[1]))[:, None, None]
            return (out_s, out_v)
        N = node_input.shape[0]
        a = node_attr[:, 0]
        xs = node_input[:, :64]
        xv = node_input[:, 64:].reshape(N, 32, 3)
        sc_s, sc_v = _fctp_scalar_attr(xs, xv, Wsc0, Wsc1, a)
        f_s, f_v = _fctp_scalar_attr(xs, xv, Wl1_0, Wl1_1, a)
        h = jax.nn.gelu(edge_scalar_attr @ Wfc1 / np.sqrt(8.0))
        h = jax.nn.gelu(h @ Wfc2 / np.sqrt(64.0))
        w = h @ Wfc3 / np.sqrt(64.0)
        w0, w1, w2, w3 = (w[:, :64], w[:, 64:128], w[:, 128:160], w[:, 160:192])
        gs = f_s[edge_src]
        gv = f_v[edge_src]
        y0 = edge_attr[:, 0]
        y1 = edge_attr[:, 1:4]
        mid0 = w0 * gs * y0[:, None]
        mid1 = w3 * jnp.einsum('euc,ec->eu', gv, y1) * INV_SQRT3
        mid2 = (w1 * gs)[:, :, None] * y1[:, None, :]
        mid3 = w2[:, :, None] * gv * y0[:, None, None]
        inv = 1.0 / np.sqrt(NUM_NEIGHBORS)
        seg = lambda x: jax.ops.segment_sum(x, edge_dst, num_segments=N) * inv
        ns0, ns1, nv2, nv3 = (seg(mid0), seg(mid1), seg(mid2), seg(mid3))
        mid_s = jnp.concatenate([ns0, ns1], axis=1)
        mid_v = jnp.concatenate([nv2, nv3], axis=1)
        out_s = mid_s @ Wl2_s * (a / np.sqrt(96.0))[:, None]
        out_v = jnp.einsum('nuc,uw->nwc', mid_v, Wl2_v) * (a / np.sqrt(96.0))[:, None, None]
        alpha = mid_s @ Wa * (a / np.sqrt(96.0))[:, None]
        res_s = sc_s + alpha * out_s
        res_v = sc_v + alpha[:, :, None] * out_v
        return jnp.concatenate([res_s, res_v.reshape(N, 96)], axis=1)

    def _L2_gnn_ref(x, node_attr, edge_scalars, edge_attr_sh, edge_src, edge_dst, Wfc1, Wfc2, Wsc0, Wsc1, Wl1_0, Wl1_1, Wl2_s, Wl2_v, Wa):
        import jax, jax.numpy as jnp
        import numpy as np
        N = 20000
        E = 5000
        MUL0 = 64
        MUL1 = 32
        FC_IN = 16
        FC_H = 64
        WNUM = 192
        n = x.shape[0]
        x0 = x[:, :MUL0]
        x1 = x[:, MUL0:].reshape(n, MUL1, 3)
        a = node_attr
        h = jax.nn.silu(edge_scalars @ (Wfc1 / jnp.sqrt(jnp.float32(FC_IN))))
        w = h @ (Wfc2 / jnp.sqrt(jnp.float32(FC_H)))
        w0 = w[:, :64]
        w1 = w[:, 64:128]
        w2 = w[:, 128:160]
        w3 = w[:, 160:192]
        inv8 = 1.0 / jnp.sqrt(jnp.float32(MUL0))
        inv32 = 1.0 / jnp.sqrt(jnp.float32(MUL1))
        sc = jnp.concatenate([x0 @ Wsc0 * a * inv8, (jnp.einsum('num,uv->nvm', x1, Wsc1) * a[..., None] * inv32).reshape(n, 3 * MUL1)], axis=1)
        f0 = x0 @ Wl1_0 * a * inv8
        f1 = jnp.einsum('num,uv->nvm', x1, Wl1_1) * a[..., None] * inv32
        e0 = f0[edge_src]
        e1 = f1[edge_src]
        sh0 = edge_attr_sh[:, :1]
        sh1 = edge_attr_sh[:, 1:4]
        mid0 = w0 * e0 * sh0
        mid1 = w3 * jnp.einsum('eum,em->eu', e1, sh1) / jnp.sqrt(3.0)
        mid2 = w1[:, :, None] * e0[:, :, None] * sh1[:, None, :]
        mid3 = w2[:, :, None] * e1 * sh0[:, :, None]
        cnt = jnp.clip(jax.ops.segment_sum(jnp.ones(edge_dst.shape, x.dtype), edge_dst, num_segments=n), 1.0)

        def smean(v):
            s = jax.ops.segment_sum(v, edge_dst, num_segments=n)
            return s / cnt.reshape((n,) + (1,) * (v.ndim - 1))
        n0, n1 = (smean(mid0), smean(mid1))
        n2, n3 = (smean(mid2), smean(mid3))
        scal = jnp.concatenate([n0, n1], axis=1)
        vec = jnp.concatenate([n2, n3], axis=1)
        inv96 = 1.0 / jnp.sqrt(jnp.float32(MUL0 + MUL1))
        alpha = scal @ Wa * a * inv96
        out_s = scal @ Wl2_s * a * inv96
        out_v = jnp.einsum('num,uv->nvm', vec, Wl2_v) * a[..., None] * inv96
        conv = jnp.concatenate([out_s, out_v.reshape(n, 3 * MUL1)], axis=1)
        return sc + alpha * conv

    def _L3_gnn_ref(x, edge_index, edge_feat, edge_scalars, W_ss, W_sv, W_vs, W_vv, W_rad, b_rad, L_s, L_v):
        import jax, jax.numpy as jnp
        import numpy as np
        N_NODES = 100000
        N_EDGES = 12500
        MUL_S = 64
        MUL_V = 32
        DIM = MUL_S + 3 * MUL_V
        EDGE_SCALAR_DIM = 16
        ISQ3 = 1.0 / np.sqrt(3.0)
        ISQ2 = 1.0 / np.sqrt(2.0)

        def _forward(x, edge_index, edge_feat, edge_scalars, W_ss, W_sv, W_vs, W_vv, W_rad, b_rad, L_s, L_v):
            src, dst = (edge_index[0], edge_index[1])
            n = x.shape[0]
            xs = x[:, :MUL_S]
            xv = x[:, MUL_S:].reshape(n, MUL_V, 3)
            xs_e = xs[src]
            xv_e = xv[src]
            es = edge_feat[:, 0]
            ev = edge_feat[:, 1:4]
            out_s = (jnp.einsum('eu,uo->eo', xs_e * es[:, None], W_ss) / np.sqrt(MUL_S) + jnp.einsum('eud,ed,uo->eo', xv_e, ev, W_vv) * ISQ3 / np.sqrt(MUL_V)) * ISQ2
            out_v = (jnp.einsum('eu,ed,uv->evd', xs_e, ev, W_sv) * ISQ3 / np.sqrt(MUL_S) + jnp.einsum('eud,e,uv->evd', xv_e, es, W_vs) * ISQ3 / np.sqrt(MUL_V)) * ISQ2
            messages = jnp.concatenate([out_s, out_v.reshape(-1, 3 * MUL_V)], axis=1)
            scale = jax.nn.sigmoid(edge_scalars @ W_rad.T + b_rad)
            messages = messages * scale
            agg = jax.ops.segment_sum(messages, dst, num_segments=n)
            h = x + agg
            hs = h[:, :MUL_S]
            hv = h[:, MUL_S:].reshape(n, MUL_V, 3)
            ys = hs @ L_s / np.sqrt(MUL_S)
            yv = jnp.einsum('nud,uv->nvd', hv, L_v) / np.sqrt(MUL_V)
            return jnp.concatenate([ys, yv.reshape(n, 3 * MUL_V)], axis=1)
        return _forward(x, edge_index, edge_feat, edge_scalars, W_ss, W_sv, W_vs, W_vv, W_rad, b_rad, L_s, L_v)
    edge_index = jnp.stack([src, dst])
    x = _layernorm(x + _L0_gnn_ref(x, edge_attr_16, edge_attr_4, L0_gnn_gamma_s, L0_gnn_beta_s, L0_gnn_gamma_v, L0_gnn_Ws_src, L0_gnn_Wv_src, L0_gnn_Ws_dst, L0_gnn_Wv_dst, L0_gnn_W_rbf, L0_gnn_W_alpha, L0_gnn_alpha_dot, L0_gnn_Ws_val, L0_gnn_Wv_val, L0_gnn_Wg, L0_gnn_w2_ss, L0_gnn_w2_sv, L0_gnn_w2_vs, L0_gnn_w2_vv0, L0_gnn_w2_vv1, L0_gnn_Ws_vlin, L0_gnn_Wv_vlin, L0_gnn_Wps, L0_gnn_Wpv, edge_index), axis=-1)
    x = _layernorm(x + _L1_gnn_ref(x, node_vec1, edge_attr_4, edge_attr_8, L1_gnn_Wsc0, L1_gnn_Wsc1, L1_gnn_Wl1_0, L1_gnn_Wl1_1, L1_gnn_Wfc1, L1_gnn_Wfc2, L1_gnn_Wfc3, L1_gnn_Wl2_s, L1_gnn_Wl2_v, L1_gnn_Wa, src, dst), axis=-1)
    x = _layernorm(x + _L2_gnn_ref(x, node_vec1, edge_attr_16, edge_attr_4, src, dst, L2_gnn_Wfc1, L2_gnn_Wfc2, L2_gnn_Wsc0, L2_gnn_Wsc1, L2_gnn_Wl1_0, L2_gnn_Wl1_1, L2_gnn_Wl2_s, L2_gnn_Wl2_v, L2_gnn_Wa), axis=-1)
    x = _layernorm(x + _L3_gnn_ref(x, edge_index, edge_attr_4, edge_attr_16, L3_gnn_W_ss, L3_gnn_W_sv, L3_gnn_W_vs, L3_gnn_W_vv, L3_gnn_W_rad, L3_gnn_b_rad, L3_gnn_L_s, L3_gnn_L_v), axis=-1)
    return x

_drawn_inputs = setup_inputs


def setup_inputs(seed=0):
    import zlib

    import numpy as np

    out = dict(_drawn_inputs(seed))
    spreads = {'L0_gnn_gamma_s': (1.0, 0.6), 'L0_gnn_beta_s': (0.0, 0.8), 'L0_gnn_gamma_v': (1.0, 0.6)}
    factors = {'edge_attr_8': 8.0,
     'L0_gnn_Wv_dst': 2.682,
     'L0_gnn_W_alpha': 6.161,
     'L0_gnn_alpha_dot': 6.067,
     'L0_gnn_Wg': 2.685,
     'L0_gnn_w2_vv1': 3.256,
     'L1_gnn_Wl1_0': 8.0,
     'L1_gnn_Wl1_1': 8.0,
     'L1_gnn_Wfc1': 8.0,
     'L1_gnn_Wfc2': 8.0,
     'L1_gnn_Wfc3': 8.0,
     'L1_gnn_Wl2_s': 8.0,
     'L1_gnn_Wl2_v': 8.0,
     'L1_gnn_Wa': 8.0,
     'L2_gnn_Wfc1': 8.0,
     'L2_gnn_Wfc2': 8.0,
     'L2_gnn_Wl1_0': 8.0,
     'L2_gnn_Wl1_1': 8.0,
     'L2_gnn_Wl2_s': 8.0,
     'L2_gnn_Wl2_v': 8.0,
     'L2_gnn_Wa': 8.0,
     'L3_gnn_b_rad': 8.0}
    for name, (base, spread) in spreads.items():
        noise = np.random.default_rng([zlib.crc32(name.encode()), seed]).standard_normal(out[name].shape)
        drawn = base * np.exp(spread * noise) if base else spread * noise
        out[name] = jnp.asarray(drawn.astype(out[name].dtype))
    for name, factor in factors.items():
        out[name] = (out[name] * factor).astype(out[name].dtype)
    return out
```

```python
from contextlib import ExitStack, contextmanager

import numpy as np

import concourse.bass as bass
from concourse import mybir

F32 = mybir.dt.float32
I32 = mybir.dt.int32
ALU = mybir.AluOpType
ACT = mybir.ActivationFunctionType
AX = mybir.AxisListType

P = 128
CS, CV = 64, 32
C = CS + 3 * CV
EPS = 1e-5
PAIR = 2
BODY = 2 * PAIR
NEG = -1.0e30
ROW = C + 2
MW = 13
M_YA, M_Y, M_DST, M_REP, M_LAST = 0, 4, 10, 11, 12
W96 = CS + CV


def cm(ap):
    return ap.rearrange("p (u c) -> p c u", c=3)


@contextmanager
def phase(nc):
    with nc.cleanup_on_exit():
        with ExitStack() as ctx:
            yield ctx


class Alloc:
    def __init__(self, nc, ctx, name):
        self.nc, self.ctx, self.name = nc, ctx, name

    def sb(self, name, shape, dt=F32):
        return self.ctx.enter_context(self.nc.sbuf_tensor(f"{self.name}_{name}", shape, dt))

    def ps(self, name, shape):
        return self.ctx.enter_context(self.nc.psum_tensor(f"{self.name}_{name}", shape, F32))

    def sem(self, name):
        return self.nc.alloc_semaphore(name=f"{self.name}_{name}")

    def sems(self, name, n=2):
        return [self.sem(f"{name}{b}") for b in range(n)]

    def sbs(self, name, shape, dt=F32):
        return [self.sb(f"{name}{b}", shape, dt) for b in range(2)]


def free(eng, sem, value):
    if not (isinstance(value, int) and value == 0):
        eng.wait_ge(sem, value)


def ready(eng, sems, i, b):
    eng.wait_ge(sems[b], i + 1)


def apart(eng, sem, value, passed):
    eng.wait_ge(sem, value).then_inc(passed, 1)


def before(eng, sems, i, b):
    free(eng, sems[1 - b], i + b)



def load_weights(nc, ctx, d):
    A = Alloc(nc, ctx, "w")
    w = {}
    loads, scales, colscales = [], [], []

    def tile(name, shape):
        w[name] = A.sb(name, shape)
        return w[name]

    def block(name, ws, wv, fs, fv):
        m = tile(name + "_m", [P, P])
        r = tile(name + "_r", [CV, CV])
        loads.append((m[0:CS, 0:CS], d[ws]))
        loads.append((m[64:96, 64:96], d[wv]))
        loads.append((m[96:128, 96:128], d[wv]))
        loads.append((r[:, :], d[wv]))
        scales.append((r[:, :], fv))
        scales.append((m[0:CS, 0:CS], fs))
        scales.append((m[64:128, 64:128], fv))

    i8, i32 = 1 / 8.0, 1 / np.sqrt(32.0)
    block("sc1", "L1_gnn_Wsc0", "L1_gnn_Wsc1", i8, i32)
    block("sc2", "L2_gnn_Wsc0", "L2_gnn_Wsc1", i8, i32)
    block("sc3", "L3_gnn_L_s", "L3_gnn_L_v", i8, i32)
    block("f1", "L1_gnn_Wl1_0", "L1_gnn_Wl1_1", i8, i32)
    block("f2", "L2_gnn_Wl1_0", "L2_gnn_Wl1_1", i8, i32)
    block("src", "L0_gnn_Ws_src", "L0_gnn_Wv_src", 1.0, 1.0)
    block("dst", "L0_gnn_Ws_dst", "L0_gnn_Wv_dst", 1.0, 1.0)
    block("out0", "L0_gnn_Wps", "L0_gnn_Wpv", 1.0, 1.0)

    def plain(name, src, rows, cols, f=1.0):
        t = tile(name, [rows, cols])
        loads.append((t[:, :], d[src]))
        if f != 1.0:
            scales.append((t[:, :], f))
        return t

    plain("fc1_1", "L1_gnn_Wfc1", 8, 64)
    plain("fc1_2", "L1_gnn_Wfc2", 64, 64)
    t = plain("fc1_3", "L1_gnn_Wfc3", 64, 192)
    scales.append((t[:, 160:192], 1 / np.sqrt(3.0)))
    plain("fc2_1", "L2_gnn_Wfc1", 16, 64)
    t = plain("fc2_3", "L2_gnn_Wfc2", 64, 192)
    scales.append((t[:, 160:192], 1 / np.sqrt(3.0)))
    for l, f in ((1, 1 / np.sqrt(32.0) / np.sqrt(96.0)), (2, 1 / np.sqrt(96.0))):
        plain(f"os{l}", f"L{l}_gnn_Wl2_s", W96, CS, f)
        plain(f"ov{l}", f"L{l}_gnn_Wl2_v", W96, CV, f)
        t = tile(f"oa{l}", [W96 + 1, 2])
        loads.append((t[0:W96, 0:1], d[f"L{l}_gnn_Wa"]))
        scales.append((t[0:W96, 0:1], f))
    plain("rbf", "L0_gnn_W_rbf", 16, 224)
    scales.append((w["rbf"][:, 160:192], 1 / np.sqrt(3.0)))
    scales.append((w["rbf"][:, 192:224], 1 / np.sqrt(2.0)))
    va = tile("va", [W96, 160])
    loads.append((va[:, 0:64], d["L0_gnn_Ws_val"]))
    loads.append((va[:, 64:128], d["L0_gnn_W_alpha"]))
    plain("valT", "ws_valT", 64, W96)
    plain("wg", "L0_gnn_Wg", 64, CV)
    plain("wvval", "L0_gnn_Wv_val", P, CV)
    adot = tile("adot", [P, 64])
    loads.append((adot[:, :], d["L0_gnn_alpha_dot"].partition_broadcast(P)))
    hm = tile("h_m", [P, 224])
    hr = tile("h_r", [64, 128])
    loads.append((hm[0:64, 0:64], d["L0_gnn_Ws_vlin"][0:64, :]))
    loads.append((hm[0:64, 64:96], d["L0_gnn_Wv_vlin"][0:64, :]))
    for g in range(2):
        loads.append((hm[64 + 32 * g:96 + 32 * g, 96 + 64 * g:128 + 64 * g], d["L0_gnn_Wv_vlin"][64:96, :]))
        loads.append((hm[64 + 32 * g:96 + 32 * g, 128 + 64 * g:160 + 64 * g], d["L0_gnn_Wv_vlin"][96:128, :]))
    loads.append((hr[0:32, 0:32], d["L0_gnn_Wv_vlin"][64:96, :]))
    loads.append((hr[0:32, 32:64], d["L0_gnn_Wv_vlin"][96:128, :]))
    loads.append((hr[32:64, 64:128], d["L0_gnn_Ws_vlin"][64:96, :]))
    cols = tile("cols", [P, 12])

    def col(c, at, src, n):
        loads.append((cols[at:at + n, c:c + 1], d[src]))

    col(0, 0, "L0_gnn_w2_ss", 64)
    col(1, 0, "L0_gnn_w2_sv", 64)
    for at in (64, 96):
        col(2, at, "L0_gnn_w2_vs", 32)
        col(3, at, "L0_gnn_w2_vv1", 32)
    col(4, 0, "L0_gnn_w2_vs", 32)
    col(5, 0, "L0_gnn_w2_vv1", 32)
    col(6, 32, "L0_gnn_w2_vv0", 32)
    col(7, 0, "L0_gnn_gamma_s", 64)
    col(7, 64, "L0_gnn_gamma_v", 32)
    col(7, 96, "L0_gnn_gamma_v", 32)
    col(8, 0, "L0_gnn_gamma_v", 32)
    col(9, 0, "L0_gnn_beta_s", 64)
    colscales += [(hm[0:64, 0:64], cols[0:64, 0:1], 1.0), (hm[0:64, 64:96], cols[0:64, 1:2], 1.0)]
    for g in range(2):
        a, b = 64 + 32 * g, 96 + 32 * g
        colscales.append((hm[a:b, 96 + 64 * g:128 + 64 * g], cols[a:b, 2:3], 1.0))
        colscales.append((hm[a:b, 128 + 64 * g:160 + 64 * g], cols[a:b, 3:4], 1 / np.sqrt(2.0)))
    colscales.append((hr[0:32, 0:32], cols[0:32, 4:5], 1.0))
    colscales.append((hr[0:32, 32:64], cols[0:32, 5:6], 1 / np.sqrt(2.0)))
    colscales.append((hr[32:64, 64:128], cols[32:64, 6:7], 1 / np.sqrt(3.0)))
    raw_src, raw_dst = plain("ws_src", "L0_gnn_Ws_src", 64, 64), plain("ws_dst", "L0_gnn_Ws_dst", 64, 64)
    for n in ("src", "dst"):
        colscales.append((w[n + "_m"][:, :], cols[:, 7:8], 1.0))
        colscales.append((w[n + "_r"][:, :], cols[0:CV, 8:9], 1.0))
    g_m, g_r = tile("g_m", [P, 288]), tile("g_r", [CV, W96])
    i2, i3 = 1 / np.sqrt(2.0), 1 / np.sqrt(3.0)
    loads.append((g_m[0:64, 0:64], d["L3_gnn_W_ss"]))
    loads.append((g_m[0:64, 64:96], d["L3_gnn_W_sv"]))
    scales += [(g_m[0:64, 0:64], i2 * i8), (g_m[0:64, 64:96], i2 * i3 * i8)]
    for g in range(2):
        a, c = 64 + 32 * g, 96 * (g + 1)
        loads.append((g_m[a:a + 32, c:c + 64], d["L3_gnn_W_vv"]))
        loads.append((g_m[a:a + 32, c + 64:c + 96], d["L3_gnn_W_vs"]))
        scales.append((g_m[a:a + 32, c:c + 96], i2 * i3 * i32))
    loads.append((g_r[:, 0:64], d["L3_gnn_W_vv"]))
    loads.append((g_r[:, 64:96], d["L3_gnn_W_vs"]))
    scales.append((g_r[:, :], i2 * i3 * i32))
    plain("rad", "w_rad_ext", 17, C)
    ident = tile("ident", [P, P])
    ones = tile("ones", [1, P])
    bias = tile("bias", [1, P])
    eps = tile("eps", [P, 2])
    big = [w[n] for n in w if n.endswith("_m") or n.endswith("_r")]
    with phase(nc) as pctx:
        A = Alloc(nc, pctx, "setup")
        N = d["xa"].shape[0]
        slots = A.sb("slots", [P, (N + P - 1) // P], I32)
        pw = A.ps("pw", [W96, 512])

        zeroed, ident_done, weights_in = A.sem("zeroed"), A.sem("ident_done"), A.sem("weights_in")
        scaled, products, slots_set = A.sem("scaled"), A.sem("products"), A.sem("slots_set")
        slots_out = A.sem("slots_out")
        with nc.Block() as block:
            @block.gpsimd
            def _(pool):
                for t in big:
                    last = pool.memset(t[:, :], 0.0)
                last.then_inc(zeroed, 1)
                pool.memset(ident[:, :], 0.0).then_inc(ident_done, 1)
                pool.wait_ge(ident_done, 1)
                pool.affine_select(out=ident[:, :], in_=ident[:, :], compare_op=ALU.not_equal, fill=1.0,
                                   base=0, pattern=[[-1, P]], channel_multiplier=1).then_inc(ident_done, 1)
                pool.wait_ge(ident_done, 2)

            @block.sync
            def _(sp):
                sp.wait_ge(zeroed, 1)
                for dst, src in loads:
                    sp.dma_start(dst, src).then_inc(weights_in, 16)
                sp.wait_ge(slots_set, 1)
                full = slots.shape[1]
                rows = N // full
                sp.dma_start(d["slot"][0:rows * full, :].rearrange("(p k) c -> p (k c)", k=full),
                             slots[0:rows, :]).then_inc(slots_out, 16)
                if N % full:
                    sp.dma_start(d["slot"][rows * full:N, :].rearrange("(p k) c -> p (k c)", p=1),
                                 slots[0:1, 0:N % full]).then_inc(slots_out, 16)
                    sp.wait_ge(slots_out, 32)
                else:
                    sp.wait_ge(slots_out, 16)

            @block.vector
            def _(dve):
                dve.memset(slots[:, :], d["E_pad"] + 1).then_inc(slots_set, 1)
                dve.memset(ones[:, :], 1.0)
                dve.memset(eps[:, 0:1], EPS)
                dve.memset(eps[:, 1:2], EPS / 4)
                dve.memset(bias[:, :], 0.0)
                for l in (1, 2):
                    dve.memset(w[f"oa{l}"][0:W96, 1:2], 0.0)
                    dve.memset(w[f"oa{l}"][W96:W96 + 1, 0:1], 0.0)
                    dve.memset(w[f"oa{l}"][W96:W96 + 1, 1:2], 1.0)
                dve.wait_ge(weights_in, 16 * len(loads))
                for k, (ap, f) in enumerate(scales):
                    dve.tensor_scalar(ap, ap, float(f), None, ALU.mult).then_inc(scaled, 1)
                dve.wait_ge(scaled, len(scales))
                for ap, c, f in colscales:
                    dve.tensor_scalar(ap, ap, c, float(f), ALU.mult, ALU.mult).then_inc(scaled, 1)
                dve.wait_ge(scaled, len(scales) + len(colscales))
                dve.wait_ge(products, 1)
                dve.tensor_copy(w["va"][:, 128:160], pw[:, 0:CV]).then_inc(scaled, 1)
                dve.tensor_copy(bias[0:1, 0:CS], pw[0:1, 128:128 + CS]).then_inc(scaled, 1)
                dve.wait_ge(scaled, len(scales) + len(colscales) + 2)

            @block.tensor
            def _(pe):
                pe.wait_ge(weights_in, 16 * len(loads))
                pe.matmul(pw[:, 0:CV], w["valT"][:, :], w["wg"][:, :], start=True, stop=True)
                pe.matmul(pw[0:1, 128:192], cols[0:64, 9:10], raw_src[:, :], start=True, stop=False)
                pe.matmul(pw[0:1, 128:192], cols[0:64, 9:10], raw_dst[:, :], start=False, stop=True).then_inc(products, 1)
    return w



def tiles_of(ap, at, g):
    return ap[bass.ds(at, g * P), :].rearrange("(g p) c -> p g c", p=P)


def last_edges(dve, out, ends, flag, big, done, value):
    dve.tensor_tensor(flag, ends[:, :, 0], ends[:, :, 1], ALU.not_equal).then_inc(done, 1)
    dve.wait_ge(done, value + 1)
    dve.scalar_tensor_tensor(flag, ends[:, :, 0], float(-big), flag, ALU.add, ALU.mult).then_inc(done, 1)
    dve.wait_ge(done, value + 2)
    return dve.tensor_scalar(out, flag, float(big), None, ALU.add)


def chain(nc, w, d, name, G, iters, sources):
    N, NT = d["xa"].shape[0], d["NT"]
    step = 2 * G * P
    big = 2 * N
    with phase(nc) as ctx:
        A = Alloc(nc, ctx, name)
        xin = A.sbs("xin", [P, G, C + 1])
        st, mv = A.sbs("st", [P, G, 6]), A.sbs("mv", [P, G, 2])
        rs, nb, ac, sd = (A.sbs(n, [P, G]) for n in ("rs", "nb", "ac", "sd"))
        xs = [A.sbs(f"x{l}", [P, G, C]) for l in (1, 2, 3)]
        pre = A.sbs("pre", [P, G, C])
        tm, tr = A.sbs("tm", [P, G * P]), A.sbs("tr", [CV, G * P])
        p_t = [A.ps(f"pt{b}", [P, 512]) for b in range(2)]
        p_r = [A.ps(f"pr{b}", [P, 512]) for b in range(2)]
        p_y = [A.ps(f"py{b}", [P, G, 256]) for b in range(2)]

        x_in = A.sems("x_in")
        stats, aggr, scl, nbd = A.sems("stats"), A.sems("aggr"), A.sems("scl"), A.sems("nbd")
        roots, passed = A.sems("roots"), A.sem("passed")
        x_ready = [A.sems(f"x{l}_ready") for l in (1, 2, 3)]
        turned, turned_out, y_done, pre_done = (A.sems("turned"), A.sems("turned_out"), A.sems("y_done"),
                                                A.sems("pre_done"))
        if sources:
            meta, eint, yin = A.sbs("meta", [P, G, MW]), A.sbs("eint", [P, G, 4], I32), A.sbs("yin", [P, G, 4])
            lst = A.sbs("lst", [P, G])
            rep = A.sbs("rep", [P, G], I32)
            e_in, rep_in, meta_set = A.sems("e_in"), A.sems("rep_in"), A.sems("meta_set")
            lst_done, stored = A.sems("lst_done"), A.sems("stored")
        else:
            ob = A.sbs("ob", [P, G, C])
            o_ready, o_stored = A.sems("o_ready"), A.sems("o_stored")
            ids, ends = A.sb("ids", [P, NT, 2], I32), A.sb("ends", [P, NT, 2], I32)
            endf, ring = A.sb("endf", [P, NT]), A.sbs("ring", [P, 1, 2], I32)
            ends_in, ids_done = A.sem("ends_in"), A.sem("ids_done")
            ring_in, ring_used = A.sems("ring_in"), A.sems("ring_used")
        layers = 2 if sources else 3

        with nc.Block() as block:
            @block.sync
            def _(sp):
                if sources:
                    def body(i):
                        for b in range(2):
                            at = (2 * i + b) * G * P
                            free(sp, stored[b], 80 * i)
                            sp.dma_start(eint[b][:, :, :], tiles_of(d["eint"], at, G)).then_inc(e_in[b], 16)
                            sp.dma_start(yin[b][:, :, :], tiles_of(d["y"], at, G)).then_inc(e_in[b], 16)
                        for b in range(2):
                            at = (2 * i + b) * G * P
                            ready(sp, meta_set, i, b)
                            sp.dma_start(tiles_of(d["meta"], at, G), meta[b][:, :, :]).then_inc(stored[b], 16)
                            sp.dma_start(tiles_of(d["B0"], at, G), xin[b][:, :, :]).then_inc(stored[b], 16)
                        for l in range(3):
                            for b in range(2):
                                ready(sp, x_ready[l], i, b)
                                sp.dma_start(tiles_of(d[f"B{l + 1}"], (2 * i + b) * G * P, G),
                                             xs[l][b][:, :, :]).then_inc(stored[b], 16)

                    body(0)
                    with sp.Fori(1, iters) as i:
                        body(i)
                    for b in range(2):
                        sp.wait_ge(stored[b], 80 * iters)
                    return

                sp.dma_start(ends[:, :, :], d["ends"]).then_inc(ends_in, 16)
                sp.dma_start(ids[:, :, :], d["edge_ids"]).then_inc(ends_in, 16)

                def nodes(i, row):
                    for b in range(2):
                        free(sp, x_ready[0][b], i)
                        sp.dma_start(xin[b][:, :, :], d["xa"][bass.ds(row + b * G * P, G * P), :]
                                     .rearrange("(p g) c -> p g c", g=G)).then_inc(x_in[b], 16)

                def slots(i):
                    for b in range(2):
                        free(sp, ring_used[b], 16 * i)
                        sp.dma_start(ring[b][:, :, :], ids[:, bass.ds(2 * i + b, 1), :]).then_inc(ring_in[b], 16)

                def outs(i, row):
                    for b in range(2):
                        ready(sp, o_ready, i, b)
                        sp.dma_start(d["out"][bass.ds(row + b * G * P, G * P), :]
                                     .rearrange("(p g) c -> p g c", g=G), ob[b][:, :, :]).then_inc(o_stored[b], 16)

                nodes(0, 0)
                sp.wait_ge(ids_done, 3)
                slots(0)
                with sp.Fori(1, iters - 1) as i:
                    nodes(i, i * step)
                    slots(i)
                    outs(i - 1, (i - 1) * step)
                nodes(iters - 1, N - step)
                slots(iters - 1)
                outs(iters - 2, (iters - 2) * step)
                for b in range(2):
                    sp.wait_ge(o_stored[b], 16 * (iters - 1))
                outs(iters - 1, N - step)
                for b in range(2):
                    sp.wait_ge(o_stored[b], 16 * iters)

            @block.gpsimd
            def _(pool):
                top = pool.to_reg(N - 1)

                def body(i):
                    for b in range(2):
                        if not sources:
                            apart(pool, ring_in[b], 16 * i + 16, passed)
                            pool.indirect_dma_start(
                                d["slot"], bass.IndirectOffsetOnAxis(ap=ring[b][:, 0, 0:1], axis=0),
                                ring[b][:, 0, 1:2], None, bounds_check=top,
                                oob_is_err=False).then_inc(ring_used[b], 16)
                        else:
                            apart(pool, e_in[b], 32 * i + 32, passed)
                            for k in range(G):
                                pool.indirect_dma_start(
                                    xin[b][:, k, :], None, d["xa"],
                                    bass.IndirectOffsetOnAxis(ap=eint[b][:, k, 0:1], axis=0),
                                    bounds_check=top, oob_is_err=False).then_inc(x_in[b], 16)
                                pool.indirect_dma_start(
                                    rep[b][:, k:k + 1], None, d["slot"],
                                    bass.IndirectOffsetOnAxis(ap=eint[b][:, k, 0:1], axis=0),
                                    bounds_check=top, oob_is_err=False).then_inc(rep_in[b], 16)

                body(0)
                with pool.Fori(1, iters) as i:
                    body(i)
                for b in range(2):
                    if not sources:
                        pool.wait_ge(ring_used[b], 16 * iters)

            @block.vector
            def _(dve):
                if not sources:
                    dve.wait_ge(ends_in, 32)
                    last_edges(dve, ids[:, :, 0], ends, endf[:, :], big, ids_done, 0).then_inc(ids_done, 1)

                def statistics(i, l, src):
                    n = i * (layers + 1) + l
                    for b in range(2):
                        if l == 0:
                            dve.wait_ge(x_in[b], 16 * (G if sources else 1) * (i + 1))
                        else:
                            dve.wait_ge(pre_done[b], i * layers + l)
                        for k in range(G):
                            ins = dve.bn_stats(st[b][:, k, :], src[b][:, k, 0:C])
                        ins.then_inc(stats[b], 1)
                    for b in range(2):
                        apart(dve, stats[b], n + 1, passed)
                        for k in range(G):
                            ins = dve.bn_aggr(mv[b][:, k, :], st[b][:, k, :])
                        ins.then_inc(aggr[b], 1)
                    for b in range(2):
                        dve.wait_ge(roots[b], n + 1)
                        dve.reciprocal(rs[b][:, :], sd[b][:, :]).then_inc(scl[b], 1)
                    return n

                def body(i):
                    n = statistics(i, 0, xin)
                    for b in range(2):
                        dve.tensor_copy(ac[b][:, :], xin[b][:, :, C])
                        if sources:
                            dve.wait_ge(e_in[b], 32 * i + 32)
                            dve.wait_ge(rep_in[b], 16 * G * (i + 1))
                            dve.tensor_tensor(meta[b][:, :, M_YA:M_YA + 4], yin[b][:, :, :],
                                              xin[b][:, :, C:C + 1].to_broadcast([P, G, 4]), ALU.mult)
                            dve.tensor_copy(meta[b][:, :, M_Y:M_Y + 4], yin[b][:, :, :])
                            dve.tensor_copy(meta[b][:, :, M_Y + 4:M_Y + 6], yin[b][:, :, 1:3])
                            mint = meta[b][:, :, :].bitcast(I32)
                            dve.tensor_copy(mint[:, :, M_DST:M_DST + 1], eint[b][:, :, 1:2])
                            dve.tensor_copy(mint[:, :, M_REP], rep[b][:, :])
                            last_edges(dve, mint[:, :, M_LAST], eint[b][:, :, 1:3], lst[b][:, :], big,
                                       lst_done[b], 2 * i).then_inc(meta_set[b], 1)
                    for b in range(2):
                        dve.wait_ge(scl[b], n + 1)
                        for k in range(G):
                            dve.tensor_scalar(xs[0][b][:, k, 0:CS], xin[b][:, k, 0:CS], mv[b][:, k, 0:1],
                                              rs[b][:, k:k + 1], ALU.subtract, ALU.mult)
                            ins = dve.tensor_scalar(xs[0][b][:, k, CS:C].rearrange("p (c u) -> p c u", c=3),
                                                    cm(xin[b][:, k, CS:C]), mv[b][:, k, 0:1],
                                                    rs[b][:, k:k + 1], ALU.subtract, ALU.mult)
                        ins.then_inc(x_ready[0][b], 1)
                    for l in range(layers):
                        for b in range(2):
                            dve.wait_ge(y_done[b], i * layers + l + 1)
                            if l:
                                dve.wait_ge(x_ready[l][b], i + 1)
                            for k in range(G):
                                if l < 2:
                                    ins = dve.scalar_tensor_tensor(pre[b][:, k, :], p_y[b][:, k, 0:C],
                                                                   ac[b][:, k:k + 1], xs[l][b][:, k, :],
                                                                   ALU.mult, ALU.add)
                                else:
                                    ins = dve.tensor_tensor(pre[b][:, k, :], p_y[b][:, k, 0:C],
                                                            xs[l][b][:, k, :], ALU.add)
                            ins.then_inc(pre_done[b], 1)
                        n = statistics(i, l + 1, pre)
                        for b in range(2):
                            dve.wait_ge(scl[b], n + 1)
                            dve.scalar_tensor_tensor(nb[b][:, :], mv[b][:, :, 0], -1.0, rs[b][:, :],
                                                     ALU.mult, ALU.mult).then_inc(nbd[b], 1)

                body(0)
                with dve.Fori(1, iters) as i:
                    body(i)

            @block.scalar
            def _(act):
                def deviations(i, l, eps):
                    for b in range(2):
                        act.wait_ge(aggr[b], i * (layers + 1) + l + 1)
                        act.activation(sd[b][:, :], mv[b][:, :, 1], ACT.Sqrt, bias=eps).then_inc(roots[b], 1)

                def body(i):
                    deviations(i, 0, w["eps"][:, 1:2])
                    for l in range(layers):
                        for b in range(2):
                            act.wait_ge(turned[b], i * layers + l + 1)
                            act.activation(tm[b][:, :], p_t[b][:, 0:G * P], ACT.Copy)
                            act.activation(tr[b][:, :], p_r[b][0:CV, 0:G * P], ACT.Copy).then_inc(turned_out[b], 1)
                        deviations(i, l + 1, w["eps"][:, 0:1])
                        for b in range(2):
                            act.wait_ge(nbd[b], i * layers + l + 1)
                            for k in range(G):
                                sc, bi = rs[b][:, k:k + 1], nb[b][:, k:k + 1]
                                if l < 2:
                                    ins = act.activation(xs[l + 1][b][:, k, :], pre[b][:, k, :], ACT.Identity,
                                                         bias=bi, scale=sc)
                                else:
                                    if k == 0:
                                        free(act, o_stored[b], 16 * i)
                                    act.activation(ob[b][:, k, 0:CS], pre[b][:, k, 0:CS], ACT.Identity,
                                                   bias=bi, scale=sc)
                                    ins = act.activation(cm(ob[b][:, k, CS:C]),
                                                         pre[b][:, k, CS:C].rearrange("p (c u) -> p c u", c=3),
                                                         ACT.Identity, bias=bi, scale=sc)
                            ins.then_inc((x_ready[l + 1] if l < 2 else o_ready)[b], 1)

                body(0)
                with act.Fori(1, iters) as i:
                    body(i)

            @block.tensor
            def _(pe):
                def body(i):
                    for l in range(layers):
                        wm, wr = w[f"sc{l + 1}_m"], w[f"sc{l + 1}_r"]
                        for b in range(2):
                            ready(pe, x_ready[l], i, b)
                            for k in range(G):
                                pe.transpose(p_t[b][:, k * P:(k + 1) * P], xs[l][b][:, k, 0:P], w["ident"][:, :])
                                ins = pe.transpose(p_r[b][0:CV, k * P:(k + 1) * P], xs[l][b][:, k, P:C],
                                                   w["ident"][:, :])
                            ins.then_inc(turned[b], 1)
                        for b in range(2):
                            pe.wait_ge(turned_out[b], i * layers + l + 1)
                            for k in range(G):
                                pe.matmul(p_y[b][:, k, 0:P], tm[b][:, k * P:(k + 1) * P], wm[:, :],
                                          start=True, stop=True)
                                ins = pe.matmul(p_y[b][:, k, P:C], tr[b][:, k * P:(k + 1) * P],
                                                wr[:, :], start=True, stop=True)
                            ins.then_inc(y_done[b], 1)

                body(0)
                with pe.Fori(1, iters) as i:
                    body(i)



def vecs(ap):
    return ap.rearrange("p k (c u) -> p k c u", c=3)


def spread(ap, shape):
    return ap.to_broadcast(shape)


def edge_rows(nc, ap, at, n):
    return ap[:, bass.ds(at, n)]


def attend0(nc, w, d):
    NT, N = d["NT"], d["xa"].shape[0]
    iters = NT // BODY
    K = PAIR
    with phase(nc) as ctx:
        A = Alloc(nc, ctx, "att")
        xr = A.sbs("xr", [P, 2 * K, C + 1])
        meta, eint = A.sbs("meta", [P, K, MW]), A.sbs("eint", [P, K, 4], I32)
        attr, drow = A.sbs("attr", [16, K * P]), A.sbs("drow", [4, K * P + 2], I32)
        st, mv, sq = A.sbs("st", [P, 2 * K, 6]), A.sbs("mv", [P, 2 * K, 2]), A.sbs("sq", [P, 2 * K, 96])
        ss, sd, rs = (A.sbs(n, [P, 2 * K] + r) for n, r in (("ss", []), ("sd", [2]), ("rs", [2])))
        xn = A.sbs("xn", [P, 2 * K, C])
        tm, tr = A.sbs("tm", [P, 2 * K * P]), A.sbs("tr", [CV, 2 * K * P])
        msg = A.sbs("msg", [P, K, CS + 5 * CV])
        ws, t1, t2, q = A.sbs("ws", [P, K, 128]), A.sbs("t1", [P, K, 96]), A.sbs("t2", [P, K, 96]), A.sbs("q", [P, K, 96])
        wv, cr, dt = A.sbs("wv", [P, K, CV]), A.sbs("cr", [P, K, 96]), A.sbs("dt", [P, K, CV])
        m1 = A.sbs("m1", [P, K, 480])
        m1t = A.sbs("m1t", [P, K, 512])
        val, gate, al = A.sbs("val", [P, K, 192]), A.sbs("gate", [P, K, CV]), A.sbs("al", [P, K, 64])
        la, lb, q2, sc = A.sbs("la", [P, K, 64]), A.sbs("lb", [P, K, 64]), A.sbs("q2", [P, K, 96]), A.sbs("sc", [P, K, 4])
        vt, vr, at4 = A.sbs("vt", [P, K * P]), A.sbs("vr", [64, K * P]), A.sbs("at4", [4, K * P])
        e5 = A.sbs("e5", [P, K, 160])
        h1, c1, p1, e1, e2, c2, e3 = (A.sbs(n, [P, K, 64 if n == "h1" else 96])
                                      for n in ("h1", "c1", "p1", "e1", "e2", "c2", "e3"))
        h = A.sbs("h", [P, K, C])
        pen, pen2, mrun = A.sbs("pen", [4, K * P]), A.sbs("pen2", [4, K * P]), A.sbs("mrun", [4, K * P])

        b_t, b_r, b_m = A.ps("b_t", [P, 512]), A.ps("b_r", [P, 512]), A.ps("b_m", [P, K, 256])
        b_w = [A.ps(f"b_w{b}", [P, K, 256]) for b in range(2)]
        b_u = A.ps("b_u", [P, K, 512])

        in_, meta_in, d_in, d0_out = (A.sems(n) for n in ("in", "meta_in", "d_in", "d0_out"))
        stats, squares, aggr, roots, scl = (A.sems(n) for n in ("stats", "squares", "aggr", "roots", "scl"))
        xn_s, xn_v, turned, turned_out = (A.sems(n) for n in ("xn_s", "xn_v", "turned", "turned_out"))
        msg_done, msg_out, p_a, p_b, m1_ready = (A.sems(n) for n in ("msg_done", "msg_out", "p_a", "p_b", "m1_ready"))
        m1_turned, m1_out, va_done, acts = (A.sems(n) for n in ("m1_turned", "m1_out", "va_done", "acts"))
        c_a, c_b, c_ready, v_turned, v_out = (A.sems(n) for n in ("c_a", "c_b", "c_ready", "v_turned", "v_out"))
        h_done, e_out, d_a, d_b, h_ready, stored = (A.sems(n) for n in ("h_done", "e_out", "d_a", "d_b", "h_ready", "stored"))
        start, passed = A.sem("start"), A.sem("passed")

        def pos(i, b):
            return (2 * i + b) * K * P

        with nc.Block() as block:
            @block.sync
            def _(sp):
                def early(i):
                    for b in range(2):
                        free(sp, msg_done[b], i)
                        free(sp, p_b[b], i)
                        free(sp, d_b[b], i)
                        at = pos(i, b)
                        sp.dma_start(xr[b][:, 0:K, :], tiles_of(d["B0"], at, K)).then_inc(in_[b], 16)
                        sp.dma_start(eint[b][:, :, :], tiles_of(d["eint"], at, K)).then_inc(in_[b], 16)
                        sp.dma_start(attr[b][:, :], d["attr16"][0:16, bass.ds(at, K * P)]).then_inc(in_[b], 16)
                        sp.dma_start(drow[b][:, :], d["dst_row"][0:1, bass.ds(at, K * P + 2)]
                                     .partition_broadcast(4)).then_inc(in_[b], 16)

                def late(i):
                    for b in range(2):
                        free(sp, h_ready[b], i)
                        sp.dma_start(meta[b][:, :, :], tiles_of(d["meta"], pos(i, b), K)).then_inc(meta_in[b], 16)

                def stores(i):
                    for b in range(2):
                        ready(sp, h_ready, i, b)
                        at = pos(i, b)
                        sp.dma_start(tiles_of(d["H0"], at, K), h[b][:, :, :]).then_inc(stored[b], 16)
                        sp.dma_start(d["A0"][:, bass.ds(at, K * P)], at4[b][:, :]).then_inc(stored[b], 16)
                        sp.dma_start(d["R0"][:, bass.ds(at, K * P)], mrun[b][:, :]).then_inc(stored[b], 16)

                early(0)
                late(0)
                with sp.Fori(1, iters) as i:
                    early(i)
                    stores(i - 1)
                    late(i)
                stores(iters - 1)
                for b in range(2):
                    sp.wait_ge(stored[b], 48 * iters)

            @block.gpsimd
            def _(pool):
                top = pool.to_reg(N - 1)
                def body(i):
                    for b in range(2):
                        free(pool, d0_out[b], 16 * i)
                        apart(pool, in_[b], 64 * i + 64, passed)
                        for k in range(K):
                            pool.indirect_dma_start(
                                xr[b][:, K + k, :], None, d["xa"],
                                bass.IndirectOffsetOnAxis(ap=eint[b][:, k, 3:4], axis=0),
                                bounds_check=top, oob_is_err=False).then_inc(d_in[b], 16)

                body(0)
                with pool.Fori(1, iters) as i:
                    body(i)

            @block.vector
            def _(dve):
                dve.memset(mrun[1][:, :], NEG).then_inc(start, 1)
                dve.wait_ge(start, 1)
                def body(i):
                    n = i + 1
                    for b in range(2):
                        dve.wait_ge(in_[b], 64 * n)
                        dve.wait_ge(d_in[b], 32 * n)
                        for k in range(2 * K):
                            ins = dve.bn_stats(st[b][:, k, :], xr[b][:, k, 0:CS])
                        ins.then_inc(stats[b], 1)
                    for b in range(2):
                        apart(dve, stats[b], n, passed)
                        for k in range(2 * K):
                            ins = dve.bn_aggr(mv[b][:, k, :], st[b][:, k, :])
                        ins.then_inc(aggr[b], 1)
                    for b in range(2):
                        dve.wait_ge(roots[b], n)
                        dve.reciprocal(rs[b][:, :, :], sd[b][:, :, :]).then_inc(scl[b], 1)
                    for b in range(2):
                        dve.wait_ge(scl[b], n)
                        for k in range(2 * K):
                            ins = dve.tensor_scalar(xn[b][:, k, 0:CS], xr[b][:, k, 0:CS], mv[b][:, k, 0:1],
                                                    rs[b][:, k, 0:1], ALU.subtract, ALU.mult)
                        ins.then_inc(xn_s[b], 1)
                    for b in range(2):
                        dve.wait_ge(meta_in[b], 16 * n)
                        dve.wait_ge(msg_done[b], n)
                        dve.wait_ge(msg_out[b], n)
                        y, W, m = meta[b], b_w[b], msg[b]
                        S3, S64 = [P, K, 3, CV], [P, K, 3, CS]
                        y0, yx = y[:, :, M_Y:M_Y + 1], y[:, :, M_Y + 1:M_Y + 4]
                        yx1, yx2 = y[:, :, M_Y + 2:M_Y + 5], y[:, :, M_Y + 3:M_Y + 6]

                        def over(ap, shape):
                            return ap.unsqueeze(3).to_broadcast(shape)

                        dve.tensor_tensor(ws[b][:, :, :].rearrange("p k (a u) -> p k a u", a=2),
                                          W[:, :, 0:128].rearrange("p k (a u) -> p k a u", a=2),
                                          m[:, :, 0:CS].unsqueeze(2).to_broadcast([P, K, 2, CS]), ALU.mult)
                        dve.tensor_tensor(vecs(t1[b][:, :, :]), vecs(m[:, :, 96:192]), over(yx2, S3), ALU.mult)
                        dve.tensor_tensor(vecs(t2[b][:, :, :]), vecs(m[:, :, 128:224]), over(yx1, S3), ALU.mult)
                        dve.tensor_tensor(vecs(q[b][:, :, :]), vecs(m[:, :, 64:160]), over(yx, S3), ALU.mult)
                        dve.tensor_tensor(wv[b][:, :, :], W[:, :, 128:160], y0.to_broadcast([P, K, CV]),
                                          ALU.mult).then_inc(p_a[b], 1)
                        dve.wait_ge(p_a[b], n)
                        dve.tensor_tensor(m1[b][:, :, 0:CS], ws[b][:, :, 0:CS], y0.to_broadcast([P, K, CS]), ALU.mult)
                        mx = m1[b][:, :, 96:480].rearrange("p k (c u) -> p k c u", c=3)
                        dve.tensor_tensor(mx[:, :, :, 0:CS], ws[b][:, :, 64:128].unsqueeze(2).to_broadcast(S64),
                                          over(yx, S64), ALU.mult)
                        dve.tensor_tensor(cr[b][:, :, :], t1[b][:, :, :], t2[b][:, :, :], ALU.subtract)
                        dve.tensor_tensor(mx[:, :, :, 64:96], vecs(m[:, :, 64:160]),
                                          wv[b][:, :, :].unsqueeze(2).to_broadcast(S3), ALU.mult)
                        dve.tensor_reduce(dt[b][:, :, :], q[b][:, :, :].rearrange("p k (c u) -> p k u c", c=3),
                                          AX.X, ALU.add).then_inc(p_b[b], 1)
                        dve.wait_ge(p_b[b], n)
                        dve.tensor_tensor(m1[b][:, :, CS:96], W[:, :, 160:192], dt[b][:, :, :], ALU.mult)
                        dve.tensor_tensor(mx[:, :, :, 96:128], W[:, :, 192:224].unsqueeze(2).to_broadcast(S3),
                                          vecs(cr[b][:, :, :]), ALU.mult).then_inc(m1_ready[b], 1)
                    for b in range(2):
                        y, W = meta[b], b_w[b]
                        S3 = [P, K, 3, CV]
                        yx = y[:, :, M_Y + 1:M_Y + 4]
                        dve.wait_ge(va_done[b], n)
                        dve.wait_ge(acts[b], n)
                        dve.tensor_tensor(vecs(val[b][:, :, 64:160]), vecs(W[:, :, 160:256]),
                                          gate[b][:, :, :].unsqueeze(2).to_broadcast(S3), ALU.mult)
                        dve.scalar_tensor_tensor(la[b][:, :, :], al[b][:, :, :], 0.2, al[b][:, :, :],
                                                 ALU.mult, ALU.max).then_inc(c_a[b], 1)
                        dve.wait_ge(c_a[b], n)
                        dve.tensor_tensor(vecs(q2[b][:, :, :]), vecs(val[b][:, :, 64:160]),
                                          yx.unsqueeze(3).to_broadcast(S3), ALU.mult)
                        dve.tensor_tensor(lb[b][:, :, :], la[b][:, :, :],
                                          w["adot"][:, :].unsqueeze(1).to_broadcast([P, K, 64]), ALU.mult).then_inc(c_b[b], 1)
                        dve.wait_ge(c_b[b], n)
                        dve.tensor_reduce(val[b][:, :, 160:192], q2[b][:, :, :].rearrange("p k (c u) -> p k u c", c=3),
                                          AX.X, ALU.add)
                        dve.tensor_reduce(sc[b][:, :, :], lb[b][:, :, :].rearrange("p k (h u) -> p k h u", h=4),
                                          AX.X, ALU.add).then_inc(c_ready[b], 1)
                    for b in range(2):
                        y = meta[b]
                        S3 = [P, K, 3, CV]
                        y0, yx = y[:, :, M_Y:M_Y + 1], y[:, :, M_Y + 1:M_Y + 4].unsqueeze(3).to_broadcast(S3)
                        yx1 = y[:, :, M_Y + 2:M_Y + 5].unsqueeze(3).to_broadcast(S3)
                        yx2 = y[:, :, M_Y + 3:M_Y + 6].unsqueeze(3).to_broadcast(S3)
                        dve.wait_ge(h_done[b], n)
                        dve.wait_ge(e_out[b], n)
                        free(dve, stored[b], 48 * i)
                        dve.tensor_tensor(h1[b][:, :, :], b_u[:, :, 0:CS], y0.to_broadcast([P, K, CS]), ALU.mult)
                        dve.tensor_tensor(vecs(c1[b][:, :, :]), b_u[:, :, 64:96].unsqueeze(2).to_broadcast(S3), yx, ALU.mult)
                        de = b_u[:, :, 96:288].rearrange("p k (c u) -> p k c u", c=3)
                        dve.tensor_tensor(vecs(p1[b][:, :, :]), de[:, :, :, 0:CV],
                                          y0.unsqueeze(3).to_broadcast(S3), ALU.mult)
                        dve.tensor_tensor(vecs(e1[b][:, :, :]), vecs(e5[b][:, :, 32:128]), yx2, ALU.mult)
                        dve.tensor_tensor(vecs(e2[b][:, :, :]), vecs(e5[b][:, :, 64:160]), yx1, ALU.mult)
                        dve.tensor_tensor(pen[b][:, :], drow[b][:, 1:K * P + 1], drow[b][:, 0:K * P],
                                          ALU.not_equal).then_inc(d_a[b], 1)
                        dve.wait_ge(d_a[b], n)
                        dve.tensor_tensor(h[b][:, :, 0:CS], b_u[:, :, 288:352], h1[b][:, :, :], ALU.add)
                        dve.tensor_tensor(c2[b][:, :, :], c1[b][:, :, :], p1[b][:, :, :], ALU.add)
                        dve.tensor_tensor(e3[b][:, :, :], e1[b][:, :, :], e2[b][:, :, :], ALU.subtract)
                        dve.tensor_scalar(pen2[b][:, :], pen[b][:, :], NEG, None, ALU.mult).then_inc(d_b[b], 1)
                        dve.wait_ge(d_b[b], n)
                        if b:
                            dve.wait_ge(h_ready[0], n)
                        dve.tensor_tensor(h[b][:, :, CS:C], c2[b][:, :, :], e3[b][:, :, :], ALU.add)
                        dve.tensor_tensor_scan(mrun[b][:, :], pen2[b][:, :], at4[b][:, :],
                                               mrun[1 - b][:, K * P - 1:K * P], ALU.add, ALU.max).then_inc(h_ready[b], 1)
                    dve.wait_ge(h_ready[1], n)

                body(0)
                with dve.Fori(1, iters) as i:
                    body(i)

            @block.scalar
            def _(act):
                def body(i):
                    n = i + 1
                    for b in range(2):
                        act.wait_ge(in_[b], 64 * n)
                        act.wait_ge(d_in[b], 32 * n)
                        act.dma_start(tiles_of(d["D0"], pos(i, b), K), xr[b][:, K:2 * K, :]).then_inc(d0_out[b], 16)
                        for k in range(2 * K):
                            ins = act.activation(sq[b][:, k, :], xr[b][:, k, CS:C], ACT.Square, accum_out=ss[b][:, k:k + 1])
                        ins.then_inc(squares[b], 1)
                    for b in range(2):
                        act.wait_ge(squares[b], n)
                        act.activation(sd[b][:, :, 1], ss[b][:, :], ACT.Sqrt, bias=w["eps"][:, 0:1], scale=1.0 / CV)
                        act.wait_ge(aggr[b], n)
                        act.activation(sd[b][:, :, 0], mv[b][:, :, 1], ACT.Sqrt, bias=w["eps"][:, 0:1]).then_inc(roots[b], 1)
                    for b in range(2):
                        act.wait_ge(scl[b], n)
                        for k in range(2 * K):
                            ins = act.activation(xn[b][:, k, CS:C].rearrange("p (c u) -> p c u", c=3), cm(xr[b][:, k, CS:C]),
                                                 ACT.Copy, scale=rs[b][:, k, 1:2])
                        ins.then_inc(xn_v[b], 1)
                    for b in range(2):
                        act.wait_ge(turned[b], n)
                        act.activation(tm[b][:, :], b_t[:, :], ACT.Copy)
                        act.activation(tr[b][:, :], b_r[0:CV, :], ACT.Copy).then_inc(turned_out[b], 1)
                    for b in range(2):
                        act.wait_ge(msg_done[b], n)
                        act.activation(msg[b][:, :, 0:C], b_m[:, :, 0:C], ACT.Copy)
                        act.activation(msg[b][:, :, C:C + 64], b_m[:, :, CS:CS + 64], ACT.Copy).then_inc(msg_out[b], 1)
                    for b in range(2):
                        act.wait_ge(m1_turned[b], n)
                        for k in range(K):
                            act.activation(m1t[b][0:96, k, 0:128], b_u[0:96, k, 0:128], ACT.Copy)
                            ins = act.activation(m1t[b][:, k, 128:512], b_u[:, k, 128:512], ACT.Copy)
                        ins.then_inc(m1_out[b], 1)
                    for b in range(2):
                        act.wait_ge(va_done[b], n)
                        act.activation(val[b][:, :, 0:CS], b_w[b][:, :, 0:CS], ACT.Sigmoid)
                        act.activation(gate[b][:, :, :], b_w[b][:, :, 128:160], ACT.Sigmoid)
                        act.activation(al[b][:, :, :], b_w[b][:, :, 64:128], ACT.Copy).then_inc(acts[b], 1)
                    for b in range(2):
                        act.wait_ge(v_turned[b], n)
                        free(act, stored[b], 48 * i)
                        act.activation(vt[b][:, :], b_t[:, 0:K * P], ACT.Copy)
                        act.activation(vr[b][:, :], b_r[0:64, 0:K * P], ACT.Copy)
                        act.activation(at4[b][:, :], b_r[0:4, K * P:2 * K * P], ACT.Copy).then_inc(v_out[b], 1)
                    for b in range(2):
                        act.wait_ge(h_done[b], n)
                        de = b_u[:, :, 96:288].rearrange("p k (c u) -> p k c u", c=3)
                        act.activation(vecs(e5[b][:, :, 0:96]), de[:, :, :, CV:2 * CV], ACT.Copy)
                        act.activation(e5[b][:, :, 96:160].rearrange("p k (c u) -> p k c u", c=2), de[:, :, 0:2, CV:2 * CV],
                                       ACT.Copy).then_inc(e_out[b], 1)

                body(0)
                with act.Fori(1, iters) as i:
                    body(i)
                for b in range(2):
                    act.wait_ge(d0_out[b], 16 * iters)

            @block.tensor
            def _(pe):
                ident = w["ident"]
                def body(i):
                    n = i + 1
                    for b in range(2):
                        pe.wait_ge(xn_s[b], n)
                        pe.wait_ge(xn_v[b], n)
                        if b:
                            pe.wait_ge(turned_out[0], n)
                        for k in range(2 * K):
                            pe.transpose(b_t[:, k * P:(k + 1) * P], xn[b][:, k, 0:P], ident[:, :])
                            ins = pe.transpose(b_r[0:CV, k * P:(k + 1) * P], xn[b][:, k, P:C], ident[:, :])
                        ins.then_inc(turned[b], 1)
                    for b in range(2):
                        pe.wait_ge(turned_out[b], n)
                        pe.wait_ge(in_[b], 64 * n)
                        if b:
                            pe.wait_ge(msg_out[0], n)
                        for k in range(K):
                            s, t = slice(k * P, (k + 1) * P), slice((K + k) * P, (K + k + 1) * P)
                            pe.matmul(b_m[:, k, 0:P], tm[b][:, s], w["src_m"][:, :], start=True, stop=False)
                            pe.matmul(b_m[:, k, 0:P], tm[b][:, t], w["dst_m"][:, :], start=False, stop=False)
                            pe.matmul(b_m[:, k, 0:P], w["ones"][:, :], w["bias"][:, :], start=False, stop=True)
                            pe.matmul(b_m[:, k, P:C], tr[b][:, s], w["src_r"][:, :], start=True, stop=False)
                            pe.matmul(b_m[:, k, P:C], tr[b][:, t], w["dst_r"][:, :], start=False, stop=True)
                            ins = pe.matmul(b_w[b][:, k, 0:224], attr[b][:, s], w["rbf"][:, :], start=True, stop=True)
                        ins.then_inc(msg_done[b], 1)
                    for b in range(2):
                        pe.wait_ge(m1_ready[b], n)
                        if b:
                            pe.wait_ge(m1_out[0], n)
                        else:
                            free(pe, h_ready[1], i)
                        for k in range(K):
                            pe.transpose(b_u[0:96, k, 0:P], m1[b][:, k, 0:96], ident[:, :])
                            for c in range(3):
                                ins = pe.transpose(b_u[:, k, P * (c + 1):P * (c + 2)],
                                                   m1[b][:, k, 96 + P * c:96 + P * (c + 1)], ident[:, :])
                        ins.then_inc(m1_turned[b], 1)
                    for b in range(2):
                        pe.wait_ge(m1_out[b], n)
                        for k in range(K):
                            pe.matmul(b_w[b][:, k, 0:C], m1t[b][0:96, k, 0:P], w["va"][:, :], start=True, stop=True)
                            for c in range(3):
                                ins = pe.matmul(b_w[b][:, k, C + 32 * c:C + 32 * c + 32],
                                                m1t[b][:, k, P * (c + 1):P * (c + 2)], w["wvval"][:, :],
                                                start=True, stop=True)
                        ins.then_inc(va_done[b], 1)
                    for b in range(2):
                        pe.wait_ge(c_ready[b], n)
                        if b:
                            pe.wait_ge(v_out[0], n)
                        for k in range(K):
                            s = slice(k * P, (k + 1) * P)
                            pe.transpose(b_t[:, s], val[b][:, k, 0:P], ident[:, :])
                            pe.transpose(b_r[0:64, s], val[b][:, k, P:192], ident[:, :])
                            ins = pe.transpose(b_r[0:4, (K + k) * P:(K + k + 1) * P], sc[b][:, k, :], ident[:, :])
                        ins.then_inc(v_turned[b], 1)
                    for b in range(2):
                        pe.wait_ge(v_out[b], n)
                        if b:
                            pe.wait_ge(h_ready[0], n)
                        for k in range(K):
                            s = slice(k * P, (k + 1) * P)
                            pe.matmul(b_u[:, k, 0:224], vt[b][:, s], w["h_m"][:, :], start=True, stop=True)
                            ins = pe.matmul(b_u[:, k, 224:352], vr[b][:, s], w["h_r"][:, :], start=True, stop=True)
                        ins.then_inc(h_done[b], 1)

                body(0)
                with pe.Fori(1, iters) as i:
                    body(i)


def soften0(nc, d):
    E_pad = d["E_pad"]
    CH = max(c for c in range(1, min(2048, E_pad // 4) + 1) if E_pad % (2 * c) == 0)
    iters = E_pad // (2 * CH)
    with phase(nc) as ctx:
        A = Alloc(nc, ctx, "soft")
        a, m, dr = A.sbs("a", [4, CH]), A.sbs("m", [4, CH]), A.sbs("dr", [4, CH + 1], I32)
        same, pen, top = A.sbs("same", [4, CH]), A.sbs("pen", [4, CH]), A.sbs("top", [4, CH])
        dif, ex, bs = A.sbs("dif", [4, CH]), A.sbs("ex", [4, CH]), A.sbs("bs", [4, CH])
        in_, same_done, pen_done, top_done, dif_done, ex_done, bs_done, stored = (
            A.sems(n) for n in ("in", "same", "pen", "top", "dif", "ex", "bs", "stored"))
        start = A.sem("start")

        def at(i, b):
            return i * (-2 * CH) + (E_pad - (b + 1) * CH)

        with nc.Block() as block:
            @block.sync
            def _(sp):
                def loads(i):
                    for b in range(2):
                        free(sp, bs_done[b], i)
                        sp.dma_start(a[b][:, :], edge_rows(nc, d["A0"], at(i, b), CH)).then_inc(in_[b], 16)
                        sp.dma_start(m[b][:, :], edge_rows(nc, d["R0"], at(i, b), CH)).then_inc(in_[b], 16)
                        sp.dma_start(dr[b][:, :], d["dst_row"][0:1, bass.ds(at(i, b) + 1, CH + 1)]
                                     .partition_broadcast(4)).then_inc(in_[b], 16)

                def stores(i):
                    for b in range(2):
                        ready(sp, bs_done, i, b)
                        sp.dma_start(edge_rows(nc, d["X0"], at(i, b), CH), ex[b][:, :]).then_inc(stored[b], 16)
                        sp.dma_start(edge_rows(nc, d["S0"], at(i, b), CH), bs[b][:, :]).then_inc(stored[b], 16)

                loads(0)
                if iters > 1:
                    with sp.Fori(1, iters) as i:
                        loads(i)
                        stores(i - 1)
                stores(iters - 1)
                for b in range(2):
                    sp.wait_ge(stored[b], 32 * iters)

            @block.vector
            def _(dve):
                dve.memset(top[1][:, :], NEG)
                dve.memset(bs[1][:, :], 0.0).then_inc(start, 1)
                dve.wait_ge(start, 1)
                def body(i):
                    n = i + 1
                    for b in range(2):
                        dve.wait_ge(in_[b], 48 * n)
                        dve.tensor_tensor(same[b][:, :], dr[b][:, 0:CH], dr[b][:, 1:CH + 1], ALU.is_equal).then_inc(same_done[b], 1)
                    for b in range(2):
                        dve.wait_ge(same_done[b], n)
                        dve.tensor_scalar(pen[b][:, :], same[b][:, :], -NEG, NEG, ALU.mult, ALU.add).then_inc(pen_done[b], 1)
                    for b in range(2):
                        dve.wait_ge(pen_done[b], n)
                        if b:
                            dve.wait_ge(top_done[0], n)
                        else:
                            free(dve, top_done[1], i)
                        dve.tensor_tensor_scan(top[b][:, ::-1], pen[b][:, ::-1], m[b][:, ::-1], top[1 - b][:, 0:1],
                                               ALU.add, ALU.max).then_inc(top_done[b], 1)
                    for b in range(2):
                        dve.wait_ge(top_done[b], n)
                        dve.tensor_tensor(dif[b][:, :], a[b][:, :], top[b][:, :], ALU.subtract).then_inc(dif_done[b], 1)
                    for b in range(2):
                        dve.wait_ge(ex_done[b], n)
                        free(dve, stored[b], 32 * i)
                        if b:
                            dve.wait_ge(bs_done[0], n)
                        else:
                            free(dve, bs_done[1], i)
                        dve.tensor_tensor_scan(bs[b][:, ::-1], same[b][:, ::-1], ex[b][:, ::-1], bs[1 - b][:, 0:1],
                                               ALU.mult, ALU.add).then_inc(bs_done[b], 1)

                body(0)
                with dve.Fori(1, iters) as i:
                    body(i)

            @block.scalar
            def _(act):
                def body(i):
                    for b in range(2):
                        ready(act, dif_done, i, b)
                        free(act, stored[b], 32 * i)
                        act.activation(ex[b][:, :], dif[b][:, :], ACT.Exp).then_inc(ex_done[b], 1)

                body(0)
                with act.Fori(1, iters) as i:
                    body(i)


class Runs:

    def __init__(self, A):
        self.row = A.sbs("row", [P, PAIR * P + 1], I32)
        self.eq, self.ind = A.sbs("eq", [P, PAIR, P]), A.sbs("ind", [P, PAIR, P])
        self.done = A.sems("runs")

    def load(self, sp, d, at, b, sem):
        sp.dma_start(self.row[b][:, :], d["dst_row"][0:1, bass.ds(at, PAIR * P + 1)]
                     .partition_broadcast(P)).then_inc(sem, 16)

    def matrices(self, eng, b, dst_col):
        rows = self.row[b][:, 1:PAIR * P + 1].rearrange("p (k e) -> p k e", k=PAIR)
        before_ = self.row[b][:, 0:PAIR * P].rearrange("p (k e) -> p k e", k=PAIR)[:, :, 0:1]
        eng.tensor_tensor(self.eq[b][:, :, :], rows, dst_col.to_broadcast([P, PAIR, P]), ALU.is_equal)
        eng.tensor_tensor(self.ind[b][:, :, :], rows, before_.to_broadcast([P, PAIR, P]),
                          ALU.is_equal).then_inc(self.done[b], 1)


class Norm:

    def __init__(self, A):
        K = PAIR
        self.st, self.mv = A.sbs("n_st", [P, K, 6]), A.sbs("n_mv", [P, K, 2])
        self.sd, self.rs, self.nb = A.sbs("n_sd", [P, K]), A.sbs("n_rs", [P, K]), A.sbs("n_nb", [P, K])
        self.stats, self.aggr, self.roots, self.scl, self.nbd = (
            A.sems("n_" + x) for x in ("stats", "aggr", "roots", "scl", "nbd"))
        self.passed = A.sem("n_passed")

    def vector(self, dve, n, pre, pre_ready):
        for b in range(2):
            dve.wait_ge(pre_ready[b], n)
            for k in range(PAIR):
                ins = dve.bn_stats(self.st[b][:, k, :], pre[b][:, k, :])
            ins.then_inc(self.stats[b], 1)
        for b in range(2):
            apart(dve, self.stats[b], n, self.passed)
            for k in range(PAIR):
                ins = dve.bn_aggr(self.mv[b][:, k, :], self.st[b][:, k, :])
            ins.then_inc(self.aggr[b], 1)
        for b in range(2):
            dve.wait_ge(self.roots[b], n)
            dve.reciprocal(self.rs[b][:, :], self.sd[b][:, :]).then_inc(self.scl[b], 1)
        for b in range(2):
            dve.wait_ge(self.scl[b], n)
            dve.scalar_tensor_tensor(self.nb[b][:, :], self.mv[b][:, :, 0], -1.0, self.rs[b][:, :],
                                     ALU.mult, ALU.mult).then_inc(self.nbd[b], 1)

    def scalar_roots(self, act, n, eps):
        for b in range(2):
            act.wait_ge(self.aggr[b], n)
            act.activation(self.sd[b][:, :], self.mv[b][:, :, 1], ACT.Sqrt, bias=eps).then_inc(self.roots[b], 1)

    def scalar_apply(self, act, b, k, out, pre):
        return act.activation(out, pre, ACT.Identity, bias=self.nb[b][:, k:k + 1], scale=self.rs[b][:, k:k + 1])


def update0(nc, w, d):
    NT = d["NT"]
    iters, K = NT // BODY, PAIR
    with phase(nc) as ctx:
        A = Alloc(nc, ctx, "upd")
        h, x0, eint = A.sbs("h", [P, K, C]), A.sbs("x0", [P, K, C + 1]), A.sbs("eint", [P, K, 4], I32)
        ex, bs, same = A.sbs("ex", [4, K * P]), A.sbs("bs", [4, K * P]), A.sbs("same", [4, K * P])
        den, de2, rden, alt = (A.sbs(n, [4, K * P]) for n in ("den", "de2", "rden", "alt"))
        ha, gm, gr = A.sbs("ha", [P, K, C]), A.sbs("gm", [P, K, P]), A.sbs("gr", [CV, K, P])
        pre, x1 = A.sbs("pre", [P, K, C]), A.sbs("x1", [P, K, ROW])
        runs, norm = Runs(A), Norm(A)
        b_al = [A.ps(f"b_al{b}", [P, 512]) for b in range(2)]
        b_s, b_y = [A.ps(f"b_s{b}", [P, K, 256]) for b in range(2)], [A.ps(f"b_y{b}", [P, K, 256]) for b in range(2)]
        in_, x_in, same_done, den_done, de2_done, rden_done, alt_done = (
            A.sems(n) for n in ("in", "x_in", "same", "den", "de2", "rden", "alt"))
        al_done, ha_done, seg_done, g_done, y_done, pre_done, x1_s, x1_v, stored = (
            A.sems(n) for n in ("al", "ha", "seg", "g", "y", "pre", "x1_s", "x1_v", "stored"))
        g_half, start, passed = A.sems("g_half"), A.sem("start"), A.sem("passed")

        def pos(i, b):
            return (2 * i + b) * K * P

        with nc.Block() as block:
            @block.sync
            def _(sp):
                def early(i):
                    for b in range(2):
                        free(sp, g_done[b], i)
                        at = pos(i, b)
                        sp.dma_start(h[b][:, :, :], tiles_of(d["H0"], at, K)).then_inc(in_[b], 16)
                        sp.dma_start(eint[b][:, :, :], tiles_of(d["eint"], at, K)).then_inc(in_[b], 16)
                        sp.dma_start(ex[b][:, :], d["X0"][:, bass.ds(at, K * P)]).then_inc(in_[b], 16)
                        sp.dma_start(bs[b][:, :], d["S0"][:, bass.ds(at, K * P)]).then_inc(in_[b], 16)
                        runs.load(sp, d, at, b, in_[b])

                def late(i):
                    for b in range(2):
                        free(sp, x1_v[b], i)
                        sp.dma_start(x0[b][:, :, :], tiles_of(d["D0"], pos(i, b), K)).then_inc(x_in[b], 16)

                def stores(i):
                    for b in range(2):
                        ready(sp, x1_s, i, b)
                        ready(sp, x1_v, i, b)
                        sp.dma_start(tiles_of(d["D1"], pos(i, b), K), x1[b][:, :, :]).then_inc(stored[b], 16)

                early(0)
                late(0)
                with sp.Fori(1, iters) as i:
                    early(i)
                    stores(i - 1)
                    late(i)
                stores(iters - 1)
                for b in range(2):
                    sp.wait_ge(stored[b], 16 * iters)

            @block.vector
            def _(dve):
                dve.memset(den[1][:, :], 0.0)
                dve.memset(gm[1][:, :, :], 0.0)
                dve.memset(gr[1][:, :, :], 0.0).then_inc(start, 1)
                dve.wait_ge(start, 1)
                def body(i):
                    n = i + 1
                    for b in range(2):
                        dve.wait_ge(in_[b], 80 * n)
                        row = runs.row[b]
                        dve.tensor_tensor(same[b][:, :], row[0:4, 1:K * P + 1], row[0:4, 0:K * P],
                                          ALU.is_equal).then_inc(same_done[b], 1)
                        runs.matrices(dve, b, eint[b][:, :, 1:2])
                    for b in range(2):
                        dve.wait_ge(same_done[b], n)
                        if b:
                            dve.wait_ge(den_done[0], n)
                        else:
                            free(dve, den_done[1], i)
                        dve.tensor_tensor_scan(den[b][:, :], same[b][:, :], bs[b][:, :], den[1 - b][:, K * P - 1:K * P],
                                               ALU.mult, ALU.max).then_inc(den_done[b], 1)
                    for b in range(2):
                        dve.wait_ge(den_done[b], n)
                        dve.tensor_scalar(de2[b][:, :], den[b][:, :], 1e-16, None, ALU.add).then_inc(de2_done[b], 1)
                    for b in range(2):
                        dve.wait_ge(de2_done[b], n)
                        dve.reciprocal(rden[b][:, :], de2[b][:, :]).then_inc(rden_done[b], 1)
                    for b in range(2):
                        dve.wait_ge(rden_done[b], n)
                        dve.tensor_tensor(alt[b][:, :], ex[b][:, :], rden[b][:, :], ALU.mult).then_inc(alt_done[b], 1)
                    for b in range(2):
                        dve.wait_ge(al_done[b], n)
                        al = b_al[b][:, 0:4 * K].rearrange("p (k h) -> p k h", k=K)
                        dve.tensor_tensor(ha[b][:, :, 0:CS].rearrange("p k (h u) -> p k h u", h=4),
                                          h[b][:, :, 0:CS].rearrange("p k (h u) -> p k h u", h=4),
                                          al.unsqueeze(3).to_broadcast([P, K, 4, 16]), ALU.mult)
                        for k in range(K):
                            ins = dve.tensor_tensor(ha[b][:, k, CS:C].rearrange("p (c h u) -> p c h u", c=3, h=4),
                                                    h[b][:, k, CS:C].rearrange("p (c h u) -> p c h u", c=3, h=4),
                                                    al[:, k, :].unsqueeze(1).unsqueeze(3).to_broadcast([P, 3, 4, 8]), ALU.mult)
                        ins.then_inc(ha_done[b], 1)
                    for b in range(2):
                        dve.wait_ge(seg_done[b], n)
                        for k in range(K):
                            if k:
                                dve.wait_ge(g_half[b], n)
                            elif b:
                                dve.wait_ge(g_done[0], n)
                            else:
                                free(dve, g_done[1], i)
                            pb, pk = (b, 0) if k else (1 - b, K - 1)
                            dve.scalar_tensor_tensor(gm[b][:, k, :], runs.ind[b][:, k, :], gm[pb][:, pk, P - 1:P],
                                                     b_s[b][:, k, 0:P], ALU.mult, ALU.add)
                            dve.scalar_tensor_tensor(gr[b][:, k, :], runs.ind[b][0:CV, k, :], gr[pb][:, pk, P - 1:P],
                                                     b_s[b][0:CV, k, P:2 * P], ALU.mult,
                                                     ALU.add).then_inc((g_done if k else g_half)[b], 1)
                    for b in range(2):
                        dve.wait_ge(y_done[b], n)
                        dve.wait_ge(x_in[b], 16 * n)
                        dve.scalar_tensor_tensor(pre[b][:, :, 0:CS], x0[b][:, :, 0:CS], 2.0, b_y[b][:, :, 0:CS],
                                                 ALU.mult, ALU.add)
                        for k in range(K):
                            ins = dve.scalar_tensor_tensor(pre[b][:, k, CS:C].rearrange("p (c u) -> p c u", c=3),
                                                           cm(x0[b][:, k, CS:C]), 2.0,
                                                           b_y[b][:, k, CS:C].rearrange("p (c u) -> p c u", c=3),
                                                           ALU.mult, ALU.add)
                        ins.then_inc(pre_done[b], 1)
                    norm.vector(dve, n, pre, pre_done)
                    for b in range(2):
                        free(dve, stored[b], 16 * i)
                        dve.tensor_copy(x1[b][:, :, C:C + 1], x0[b][:, :, C:C + 1])
                        dve.tensor_tensor(x1[b][:, :, C + 1:C + 2], x0[b][:, :, C:C + 1], x0[b][:, :, C:C + 1],
                                          ALU.mult).then_inc(x1_v[b], 1)

                body(0)
                with dve.Fori(1, iters) as i:
                    body(i)

            @block.scalar
            def _(act):
                def body(i):
                    norm.scalar_roots(act, i + 1, w["eps"][:, 0:1])
                    for b in range(2):
                        act.wait_ge(norm.nbd[b], i + 1)
                        free(act, stored[b], 16 * i)
                        for k in range(K):
                            ins = norm.scalar_apply(act, b, k, x1[b][:, k, 0:C], pre[b][:, k, :])
                        ins.then_inc(x1_s[b], 1)

                body(0)
                with act.Fori(1, iters) as i:
                    body(i)

            @block.tensor
            def _(pe):
                def body(i):
                    n = i + 1
                    for b in range(2):
                        apart(pe, alt_done[b], n, passed)
                        for k in range(K):
                            ins = pe.transpose(b_al[b][:, 4 * k:4 * k + 4], alt[b][:, k * P:(k + 1) * P], w["ident"][0:4, 0:4])
                        ins.then_inc(al_done[b], 1)
                    for b in range(2):
                        pe.wait_ge(ha_done[b], n)
                        pe.wait_ge(runs.done[b], n)
                        for k in range(K):
                            pe.matmul(b_s[b][:, k, 0:P], ha[b][:, k, 0:P], runs.eq[b][:, k, :], start=True, stop=True)
                            ins = pe.matmul(b_s[b][0:CV, k, P:2 * P], ha[b][:, k, P:C], runs.eq[b][:, k, :],
                                            start=True, stop=True)
                        ins.then_inc(seg_done[b], 1)
                    for b in range(2):
                        pe.wait_ge(g_done[b], n)
                        for k in range(K):
                            pe.matmul(b_y[b][:, k, 0:P], gm[b][:, k, :], w["out0_m"][:, :], start=True, stop=True)
                            ins = pe.matmul(b_y[b][:, k, P:C], gr[b][:, k, :], w["out0_r"][:, :], start=True, stop=True)
                        ins.then_inc(y_done[b], 1)

                body(0)
                with pe.Fori(1, iters) as i:
                    body(i)


def source_rows(pool, d, l, b, xs, meta, sem, top):
    for k in range(PAIR):
        pool.indirect_dma_start(xs[b][:, k, :], None, d[f"D{l}"],
                                bass.IndirectOffsetOnAxis(ap=meta[b][:, k, M_REP:M_REP + 1].bitcast(I32), axis=0),
                                bounds_check=top, oob_is_err=False).then_inc(sem[b], 16)


def conv(nc, w, d, l):
    NT, E_pad = d["NT"], d["E_pad"]
    iters, K = NT // BODY, PAIR
    FIN = 8 if l == 1 else 16
    S3, S64 = [P, K, 3, CV], [P, K, 3, CS]
    with phase(nc) as ctx:
        A = Alloc(nc, ctx, f"l{l}")
        xs, meta, attr = A.sbs("xs", [P, K, ROW]), A.sbs("meta", [P, K, MW]), A.sbs("attr", [FIN, K * P])
        xd = A.sbs("xd", [P, K, ROW])
        sm, sr = A.sbs("sm", [P, K * P]), A.sbs("sr", [CV, K * P])
        dm, dr = A.sbs("dm", [P, K * P]), A.sbs("dr", [CV, K * P])
        g1, g2, we = A.sbs("g1", [64, K * P]), A.sbs("g2", [64, K * P]), A.sbs("we", [P, K, 192])
        p1, p2, q, dt = A.sbs("p1", [P, K, 128]), A.sbs("p2", [P, K, 96]), A.sbs("q", [P, K, 96]), A.sbs("dt", [P, K, CV])
        M1 = W96 + 1
        mid = A.sbs("mid", [P, K, M1 + 3 * W96])
        g = A.sbs("g", [M1, K, 512])
        cn, rc, rc2, ta, qq = (A.sbs(n, [P, K]) for n in ("cn", "rc", "rc2", "ta", "qq"))
        s1, pre, xo = A.sbs("s1", [P, K, C]), A.sbs("pre", [P, K, C]), A.sbs("xo", [P, K, ROW])
        runs, norm = Runs(A), Norm(A)
        b_t, b_f, b_h, b_w = A.ps("b_t", [P, 512]), A.ps("b_f", [P, K, 256]), A.ps("b_h", [64, 512]), A.ps("b_w", [P, K, 256])
        b_s, b_c, b_y = A.ps("b_s", [P, K, 512]), A.ps("b_c", [P, K, 256]), A.ps("b_y", [P, K, 256])
        in_, row_in, xd_in, stored = A.sems("in"), A.sems("row_in"), A.sems("xd_in"), A.sems("stored")
        hid1, act1, hid2, act2, w_done, w_out = (A.sems(n) for n in ("hid1", "act1", "hid2", "act2", "w_done", "w_out"))
        s_turned, s_out, f_done, f_used, mid_a, mid_ready = (
            A.sems(n) for n in ("s_turned", "s_out", "f_done", "f_used", "mid_a", "mid_ready"))
        seg_done, g_half, g_done, c_done = (A.sems(n) for n in ("seg", "g_half", "g_done", "c_done"))
        d_turned, d_out, y_done, s1_done, pre_done, xo_s, xo_v = (
            A.sems(n) for n in ("d_turned", "d_out", "y_done", "s1", "pre", "xo_s", "xo_v"))
        q_sem, start, passed = A.sems("q_sem"), A.sem("start"), A.sem("passed")

        def pos(i, b):
            return (2 * i + b) * K * P

        with nc.Block() as block:
            @block.sync
            def _(sp):
                def early(i):
                    for b in range(2):
                        free(sp, seg_done[b], i)
                        at = pos(i, b)
                        sp.dma_start(meta[b][:, :, :], tiles_of(d["meta"], at, K)).then_inc(in_[b], 16)
                        sp.dma_start(xs[b][:, :, 0:C], tiles_of(d[f"B{l}"], at, K)).then_inc(in_[b], 16)
                        sp.dma_start(attr[b][:, :], d["attr8" if l == 1 else "attr16"][0:FIN, bass.ds(at, K * P)]).then_inc(in_[b], 16)
                        runs.load(sp, d, at, b, in_[b])

                def late(i):
                    for b in range(2):
                        free(sp, xo_v[b], i)
                        sp.dma_start(xd[b][:, :, :], tiles_of(d[f"D{l}"], pos(i, b), K)).then_inc(xd_in[b], 16)

                def stores(i):
                    for b in range(2):
                        ready(sp, xo_s, i, b)
                        ready(sp, xo_v, i, b)
                        sp.dma_start(tiles_of(d[f"D{l + 1}"], pos(i, b), K), xo[b][:, :, :]).then_inc(stored[b], 16)

                early(0)
                late(0)
                with sp.Fori(1, iters) as i:
                    early(i)
                    stores(i - 1)
                    late(i)
                stores(iters - 1)
                for b in range(2):
                    sp.wait_ge(stored[b], 16 * iters)

            @block.gpsimd
            def _(pool):
                top = pool.to_reg(E_pad - 1)
                def body(i):
                    for b in range(2):
                        apart(pool, in_[b], 64 * i + 64, passed)
                        source_rows(pool, d, l, b, xs, meta, row_in, top)

                body(0)
                with pool.Fori(1, iters) as i:
                    body(i)

            @block.vector
            def _(dve):
                for b in range(2):
                    dve.memset(mid[b][:, :, W96:M1], 1.0)
                dve.memset(g[1][:, :, :], 0.0).then_inc(start, 1)
                dve.wait_ge(start, 1)
                def body(i):
                    n = i + 1
                    for b in range(2):
                        dve.wait_ge(in_[b], 64 * n)
                        runs.matrices(dve, b, meta[b][:, :, M_DST:M_DST + 1].bitcast(I32))
                    for b in range(2):
                        y, F, W = meta[b], b_f, we[b]
                        y0, yx = y[:, :, M_YA:M_YA + 1], y[:, :, M_YA + 1:M_YA + 4]
                        gv = F[:, :, CS:C].rearrange("p k (c u) -> p k c u", c=3)
                        dve.wait_ge(f_done[b], n)
                        dve.wait_ge(w_out[b], n)
                        dve.tensor_tensor(p1[b][:, :, :].rearrange("p k (a u) -> p k a u", a=2),
                                          W[:, :, 0:128].rearrange("p k (a u) -> p k a u", a=2),
                                          F[:, :, 0:CS].unsqueeze(2).to_broadcast([P, K, 2, CS]), ALU.mult)
                        dve.tensor_tensor(vecs(p2[b][:, :, :]), gv, W[:, :, 128:160].unsqueeze(2).to_broadcast(S3), ALU.mult)
                        dve.tensor_tensor(vecs(q[b][:, :, :]), gv, yx.unsqueeze(3).to_broadcast(S3), ALU.mult).then_inc(f_used[b], 1)
                        dve.wait_ge(f_used[b], n)
                        mx = mid[b][:, :, M1:].rearrange("p k (c u) -> p k c u", c=3)
                        dve.tensor_reduce(dt[b][:, :, :], q[b][:, :, :].rearrange("p k (c u) -> p k u c", c=3),
                                          AX.X, ALU.add).then_inc(mid_a[b], 1)
                        dve.tensor_tensor(mid[b][:, :, 0:CS], p1[b][:, :, 0:CS], y0.to_broadcast([P, K, CS]), ALU.mult)
                        dve.tensor_tensor(mx[:, :, :, 0:CS], p1[b][:, :, 64:128].unsqueeze(2).to_broadcast(S64),
                                          yx.unsqueeze(3).to_broadcast(S64), ALU.mult)
                        dve.tensor_tensor(mx[:, :, :, CS:W96], vecs(p2[b][:, :, :]), y0.unsqueeze(3).to_broadcast(S3), ALU.mult)
                        dve.wait_ge(mid_a[b], n)
                        dve.tensor_tensor(mid[b][:, :, CS:W96], W[:, :, 160:192], dt[b][:, :, :], ALU.mult).then_inc(mid_ready[b], 1)
                    for b in range(2):
                        dve.wait_ge(seg_done[b], n)
                        for k in range(K):
                            if k:
                                dve.wait_ge(g_half[b], n)
                            elif b:
                                dve.wait_ge(g_done[0], n)
                            else:
                                free(dve, g_done[1], i)
                            pb, pk = (b, 0) if k else (1 - b, K - 1)
                            for c in range(4):
                                R = M1 if c == 0 else W96
                                ins = dve.scalar_tensor_tensor(
                                    g[b][0:R, k, P * c:P * (c + 1)], runs.ind[b][0:R, k, :],
                                    g[pb][0:R, pk, P * (c + 1) - 1:P * (c + 1)], b_s[0:R, k, P * c:P * (c + 1)],
                                    ALU.mult, ALU.add)
                            ins.then_inc((g_done if k else g_half)[b], 1)
                    for b in range(2):
                        x = xd[b]
                        dve.wait_ge(xd_in[b], 16 * n)
                        dve.wait_ge(c_done[b], n)
                        dve.tensor_tensor(ta[b][:, :], b_c[:, :, C], x[:, :, C + 1], ALU.mult)
                        dve.tensor_scalar(cn[b][:, :], b_c[:, :, C + 1], 1.0, None, ALU.max).then_inc(q_sem[b], 1)
                        if l == 2:
                            dve.wait_ge(q_sem[b], 4 * i + 1)
                            dve.reciprocal(rc[b][:, :], cn[b][:, :]).then_inc(q_sem[b], 1)
                            dve.wait_ge(q_sem[b], 4 * i + 2)
                            dve.tensor_tensor(rc2[b][:, :], rc[b][:, :], rc[b][:, :], ALU.mult).then_inc(q_sem[b], 1)
                            dve.wait_ge(q_sem[b], 4 * i + 3)
                            dve.tensor_tensor(qq[b][:, :], ta[b][:, :], rc2[b][:, :], ALU.mult).then_inc(q_sem[b], 1)
                        dve.wait_ge(y_done[b], n)
                        for k in range(K):
                            ins = dve.scalar_tensor_tensor(s1[b][:, k, :], b_y[:, k, 0:C], x[:, k, C:C + 1],
                                                           x[:, k, 0:C], ALU.mult, ALU.add)
                        ins.then_inc(s1_done[b], 1)
                        dve.wait_ge(s1_done[b], n)
                        f = qq if l == 2 else ta
                        for k in range(K):
                            ins = dve.scalar_tensor_tensor(pre[b][:, k, :], b_c[:, k, 0:C], f[b][:, k:k + 1],
                                                           s1[b][:, k, :], ALU.mult, ALU.add)
                        ins.then_inc(pre_done[b], 1)
                    norm.vector(dve, n, pre, pre_done)
                    for b in range(2):
                        free(dve, stored[b], 16 * i)
                        dve.tensor_copy(xo[b][:, :, C:ROW], xd[b][:, :, C:ROW]).then_inc(xo_v[b], 1)

                body(0)
                with dve.Fori(1, iters) as i:
                    body(i)

            @block.scalar
            def _(act):
                def body(i):
                    n = i + 1
                    for b in range(2):
                        act.wait_ge(hid1[b], n)
                        act.activation(g1[b][:, :], b_h[:, 0:K * P], ACT.Gelu_apprx_tanh if l == 1 else ACT.Silu,
                                       scale=float(FIN) ** -0.5).then_inc(act1[b], 1)
                        if l == 1:
                            act.wait_ge(hid2[b], n)
                            act.activation(g2[b][:, :], b_h[:, K * P:2 * K * P], ACT.Gelu_apprx_tanh,
                                           scale=0.125).then_inc(act2[b], 1)
                    for b in range(2):
                        act.wait_ge(s_turned[b], n)
                        act.activation(sm[b][:, :], b_t[:, 0:K * P], ACT.Copy)
                        act.activation(sr[b][:, :], b_t[0:CV, K * P:2 * K * P], ACT.Copy).then_inc(s_out[b], 1)
                        act.wait_ge(w_done[b], n)
                        act.activation(we[b][:, :, :], b_w[:, :, 0:192], ACT.Copy, scale=0.125).then_inc(w_out[b], 1)
                    for b in range(2):
                        act.wait_ge(d_turned[b], n)
                        act.activation(dm[b][:, :], b_t[:, 0:K * P], ACT.Copy)
                        act.activation(dr[b][:, :], b_t[0:CV, K * P:2 * K * P], ACT.Copy).then_inc(d_out[b], 1)
                    norm.scalar_roots(act, n, w["eps"][:, 0:1])
                    for b in range(2):
                        act.wait_ge(norm.nbd[b], n)
                        free(act, stored[b], 16 * i)
                        for k in range(K):
                            ins = norm.scalar_apply(act, b, k, xo[b][:, k, 0:C], pre[b][:, k, :])
                        ins.then_inc(xo_s[b], 1)

                body(0)
                with act.Fori(1, iters) as i:
                    body(i)

            @block.tensor
            def _(pe):
                ident = w["ident"]

                def turn(rows):
                    for k in range(K):
                        s = slice(k * P, (k + 1) * P)
                        pe.transpose(b_t[:, s], rows[:, k, 0:P], ident[:, :])
                        ins = pe.transpose(b_t[0:CV, K * P + k * P:K * P + (k + 1) * P], rows[:, k, P:C], ident[:, :])
                    return ins

                def body(i):
                    n = i + 1
                    for b in range(2):
                        pe.wait_ge(in_[b], 64 * n)
                        before(pe, act1, i, b)
                        if l == 1:
                            before(pe, act2, i, b)
                        pe.matmul(b_h[:, 0:K * P], w[f"fc{l}_1"][:, :], attr[b][:, :], start=True, stop=True).then_inc(hid1[b], 1)
                        if l == 1:
                            apart(pe, act1[b], n, passed)
                            pe.matmul(b_h[:, K * P:2 * K * P], w["fc1_2"][:, :], g1[b][:, :], start=True, stop=True).then_inc(hid2[b], 1)
                    for b in range(2):
                        pe.wait_ge(row_in[b], 32 * n)
                        if b:
                            pe.wait_ge(s_out[0], n)
                        else:
                            free(pe, d_out[1], i)
                        turn(xs[b]).then_inc(s_turned[b], 1)
                        hid = g2 if l == 1 else g1
                        pe.wait_ge((act2 if l == 1 else act1)[b], n)
                        before(pe, w_out, i, b)
                        for k in range(K):
                            ins = pe.matmul(b_w[:, k, 0:192], hid[b][:, k * P:(k + 1) * P], w[f"fc{l}_3"][:, :], start=True, stop=True)
                        ins.then_inc(w_done[b], 1)
                        pe.wait_ge(s_out[b], n)
                        before(pe, f_used, i, b)
                        for k in range(K):
                            s = slice(k * P, (k + 1) * P)
                            pe.matmul(b_f[:, k, 0:P], sm[b][:, s], w[f"f{l}_m"][:, :], start=True, stop=True)
                            ins = pe.matmul(b_f[:, k, P:C], sr[b][:, s], w[f"f{l}_r"][:, :], start=True, stop=True)
                        ins.then_inc(f_done[b], 1)
                    for b in range(2):
                        pe.wait_ge(xd_in[b], 16 * n)
                        pe.wait_ge(d_out[0] if b else s_out[1], n)
                        turn(xd[b]).then_inc(d_turned[b], 1)
                    for b in range(2):
                        pe.wait_ge(mid_ready[b], n)
                        pe.wait_ge(runs.done[b], n)
                        before(pe, g_done, i, b)
                        for k in range(K):
                            pe.matmul(b_s[0:M1, k, 0:P], mid[b][:, k, 0:M1], runs.eq[b][:, k, :], start=True, stop=True)
                            for c in range(3):
                                ins = pe.matmul(b_s[0:W96, k, P * (c + 1):P * (c + 2)],
                                                mid[b][:, k, M1 + W96 * c:M1 + W96 * (c + 1)], runs.eq[b][:, k, :],
                                                start=True, stop=True)
                        ins.then_inc(seg_done[b], 1)
                    for b in range(2):
                        pe.wait_ge(d_out[b], n)
                        before(pe, pre_done, i, b)
                        for k in range(K):
                            s = slice(k * P, (k + 1) * P)
                            pe.matmul(b_y[:, k, 0:P], dm[b][:, s], w[f"sc{l}_m"][:, :], start=True, stop=True)
                            ins = pe.matmul(b_y[:, k, P:C], dr[b][:, s], w[f"sc{l}_r"][:, :], start=True, stop=True)
                        ins.then_inc(y_done[b], 1)
                        pe.wait_ge(g_done[b], n)
                        for k in range(K):
                            pe.matmul(b_c[:, k, 0:CS], g[b][0:W96, k, 0:P], w[f"os{l}"][:, :], start=True, stop=True)
                            for c in range(3):
                                pe.matmul(b_c[:, k, CS + CV * c:CS + CV * (c + 1)], g[b][0:W96, k, P * (c + 1):P * (c + 2)],
                                          w[f"ov{l}"][:, :], start=True, stop=True)
                            ins = pe.matmul(b_c[:, k, C:C + 2], g[b][:, k, 0:P], w[f"oa{l}"][:, :], start=True, stop=True)
                        ins.then_inc(c_done[b], 1)

                body(0)
                with pe.Fori(1, iters) as i:
                    body(i)


def conv3(nc, w, d):
    NT, E_pad, N = d["NT"], d["E_pad"], d["xa"].shape[0]
    iters, K = NT // BODY, PAIR
    S3, S64 = [P, K, 3, CV], [P, K, 3, CS]
    with phase(nc) as ctx:
        A = Alloc(nc, ctx, "l3")
        xs, meta, attr = A.sbs("xs", [P, K, ROW]), A.sbs("meta", [P, K, MW]), A.sbs("attr", [17, K * P])
        xd, last = A.sbs("xd", [P, K, ROW]), A.sbs("last", [P, K, MW])
        sm, sr = A.sbs("sm", [P, K * P]), A.sbs("sr", [CV, K * P])
        dm, dr = A.sbs("dm", [P, K * P]), A.sbs("dr", [CV, K * P])
        gate = A.sbs("gate", [P, K, C])
        h1, hq, hs, qv = A.sbs("h1", [P, K, CS]), A.sbs("hq", [P, K, CS]), A.sbs("hs", [P, K, CS]), A.sbs("qv", [P, K, 192])
        c1, p1, c2 = A.sbs("c1", [P, K, 96]), A.sbs("p1", [P, K, 96]), A.sbs("c2", [P, K, 96])
        mid, gm, gr = A.sbs("mid", [P, K, C]), A.sbs("gm", [P, K, P]), A.sbs("gr", [CV, K, P])
        pre, xo = A.sbs("pre", [P, K, C]), A.sbs("xo", [P, K, C])
        runs, norm = Runs(A), Norm(A)
        b_t, b_f, b_g = A.ps("b_t", [P, 512]), A.ps("b_f", [P, K, 512]), A.ps("b_g", [P, K, 256])
        b_s, b_y = [A.ps(f"b_s{b}", [P, K, 256]) for b in range(2)], [A.ps(f"b_y{b}", [P, K, 256]) for b in range(2)]
        in_, row_in, xd_in, stored = A.sems("in"), A.sems("row_in"), A.sems("xd_in"), A.sems("stored")
        s_turned, s_out, f_done, f_used, gt_done, gt_out = (
            A.sems(n) for n in ("s_turned", "s_out", "f_done", "f_used", "gt_done", "gt_out"))
        mid_a, mid_b, mid_ready = A.sems("mid_a"), A.sems("mid_b"), A.sems("mid_ready")
        seg_done, g_half, g_done = A.sems("seg"), A.sems("g_half"), A.sems("g_done")
        d_turned, d_out, y_done, pre_done, xo_done = (A.sems(n) for n in ("d_turned", "d_out", "y", "pre", "xo"))
        start, passed = A.sem("start"), A.sem("passed")

        def pos(i, b):
            return (2 * i + b) * K * P

        with nc.Block() as block:
            @block.sync
            def _(sp):
                def early(i):
                    for b in range(2):
                        free(sp, seg_done[b], i)
                        at = pos(i, b)
                        sp.dma_start(meta[b][:, :, :], tiles_of(d["meta"], at, K)).then_inc(in_[b], 16)
                        sp.dma_start(xs[b][:, :, 0:C], tiles_of(d["B3"], at, K)).then_inc(in_[b], 16)
                        sp.dma_start(attr[b][:, :], d["attr16"][:, bass.ds(at, K * P)]).then_inc(in_[b], 16)
                        runs.load(sp, d, at, b, in_[b])

                def late(i):
                    for b in range(2):
                        free(sp, stored[b], 32 * i)
                        free(sp, pre_done[b], i)
                        at = pos(i, b)
                        sp.dma_start(xd[b][:, :, :], tiles_of(d["D3"], at, K)).then_inc(xd_in[b], 16)
                        sp.dma_start(last[b][:, :, :], tiles_of(d["meta"], at, K)).then_inc(xd_in[b], 16)

                early(0)
                late(0)
                with sp.Fori(1, iters) as i:
                    early(i)
                    late(i)

            @block.gpsimd
            def _(pool):
                top, top_node = pool.to_reg(E_pad - 1), pool.to_reg(N - 1)

                def gathers(i):
                    for b in range(2):
                        apart(pool, in_[b], 64 * i + 64, passed)
                        source_rows(pool, d, 3, b, xs, meta, row_in, top)

                def scatters(i):
                    for b in range(2):
                        pool.wait_ge(xd_in[b], 32 * i + 32)
                        apart(pool, xo_done[b], i + 1, passed)
                        for k in range(K):
                            pool.indirect_dma_start(
                                d["out"], bass.IndirectOffsetOnAxis(
                                    ap=last[b][:, k, M_LAST:M_LAST + 1].bitcast(I32), axis=0),
                                xo[b][:, k, :], None, bounds_check=top_node, oob_is_err=False).then_inc(stored[b], 16)

                gathers(0)
                with pool.Fori(1, iters) as i:
                    gathers(i)
                    scatters(i - 1)
                scatters(iters - 1)
                for b in range(2):
                    pool.wait_ge(stored[b], 32 * iters)

            @block.vector
            def _(dve):
                dve.memset(gm[1][:, :, :], 0.0)
                dve.memset(gr[1][:, :, :], 0.0).then_inc(start, 1)
                dve.wait_ge(start, 1)
                def body(i):
                    n = i + 1
                    for b in range(2):
                        dve.wait_ge(in_[b], 64 * n)
                        runs.matrices(dve, b, meta[b][:, :, M_DST:M_DST + 1].bitcast(I32))
                    for b in range(2):
                        y = meta[b]
                        y0, yx = y[:, :, M_Y:M_Y + 1], y[:, :, M_Y + 1:M_Y + 4].unsqueeze(3)
                        fx = b_f[:, :, 96:384].rearrange("p k (c u) -> p k c u", c=3)
                        dve.wait_ge(f_done[b], n)
                        dve.tensor_tensor(h1[b][:, :, :], b_f[:, :, 0:CS], y0.to_broadcast([P, K, CS]), ALU.mult)
                        dve.tensor_tensor(vecs(qv[b][:, :, :]), fx[:, :, :, 0:CS], yx.to_broadcast(S64), ALU.mult)
                        dve.tensor_tensor(vecs(c1[b][:, :, :]), b_f[:, :, CS:W96].unsqueeze(2).to_broadcast(S3),
                                          yx.to_broadcast(S3), ALU.mult)
                        dve.tensor_tensor(vecs(p1[b][:, :, :]), fx[:, :, :, CS:W96],
                                          y0.unsqueeze(3).to_broadcast(S3), ALU.mult).then_inc(f_used[b], 1)
                        dve.wait_ge(f_used[b], n)
                        dve.tensor_reduce(hq[b][:, :, :], qv[b][:, :, :].rearrange("p k (c u) -> p k u c", c=3), AX.X, ALU.add)
                        dve.tensor_tensor(c2[b][:, :, :], c1[b][:, :, :], p1[b][:, :, :], ALU.add).then_inc(mid_a[b], 1)
                        dve.wait_ge(mid_a[b], n)
                        dve.wait_ge(gt_out[b], n)
                        dve.tensor_tensor(hs[b][:, :, :], h1[b][:, :, :], hq[b][:, :, :], ALU.add).then_inc(mid_b[b], 1)
                        dve.tensor_tensor(mid[b][:, :, CS:C], c2[b][:, :, :], gate[b][:, :, CS:C], ALU.mult)
                        dve.wait_ge(mid_b[b], n)
                        dve.tensor_tensor(mid[b][:, :, 0:CS], hs[b][:, :, :], gate[b][:, :, 0:CS], ALU.mult).then_inc(mid_ready[b], 1)
                    for b in range(2):
                        dve.wait_ge(seg_done[b], n)
                        for k in range(K):
                            if k:
                                dve.wait_ge(g_half[b], n)
                            elif b:
                                dve.wait_ge(g_done[0], n)
                            else:
                                free(dve, g_done[1], i)
                            pb, pk = (b, 0) if k else (1 - b, K - 1)
                            dve.scalar_tensor_tensor(gm[b][:, k, :], runs.ind[b][:, k, :], gm[pb][:, pk, P - 1:P],
                                                     b_s[b][:, k, 0:P], ALU.mult, ALU.add)
                            dve.scalar_tensor_tensor(gr[b][:, k, :], runs.ind[b][0:CV, k, :], gr[pb][:, pk, P - 1:P],
                                                     b_s[b][0:CV, k, P:2 * P], ALU.mult,
                                                     ALU.add).then_inc((g_done if k else g_half)[b], 1)
                    for b in range(2):
                        dve.wait_ge(y_done[b], n)
                        dve.wait_ge(xd_in[b], 32 * n)
                        dve.tensor_tensor(pre[b][:, :, :], b_y[b][:, :, 0:C], xd[b][:, :, 0:C], ALU.add).then_inc(pre_done[b], 1)
                    norm.vector(dve, n, pre, pre_done)

                body(0)
                with dve.Fori(1, iters) as i:
                    body(i)

            @block.scalar
            def _(act):
                def body(i):
                    n = i + 1
                    for b in range(2):
                        act.wait_ge(s_turned[b], n)
                        act.activation(sm[b][:, :], b_t[:, 0:K * P], ACT.Copy)
                        act.activation(sr[b][:, :], b_t[0:CV, K * P:2 * K * P], ACT.Copy).then_inc(s_out[b], 1)
                        act.wait_ge(gt_done[b], n)
                        act.activation(gate[b][:, :, :], b_g[:, :, 0:C], ACT.Sigmoid).then_inc(gt_out[b], 1)
                    for b in range(2):
                        act.wait_ge(d_turned[b], n)
                        act.activation(dm[b][:, :], b_t[:, 0:K * P], ACT.Copy)
                        act.activation(dr[b][:, :], b_t[0:CV, K * P:2 * K * P], ACT.Copy).then_inc(d_out[b], 1)
                    norm.scalar_roots(act, n, w["eps"][:, 0:1])
                    for b in range(2):
                        act.wait_ge(norm.nbd[b], n)
                        free(act, stored[b], 32 * i)
                        for k in range(K):
                            norm.scalar_apply(act, b, k, xo[b][:, k, 0:CS], pre[b][:, k, 0:CS])
                            ins = norm.scalar_apply(act, b, k, cm(xo[b][:, k, CS:C]),
                                                    pre[b][:, k, CS:C].rearrange("p (c u) -> p c u", c=3))
                        ins.then_inc(xo_done[b], 1)

                body(0)
                with act.Fori(1, iters) as i:
                    body(i)

            @block.tensor
            def _(pe):
                ident = w["ident"]

                def turn(rows):
                    for k in range(K):
                        s = slice(k * P, (k + 1) * P)
                        pe.transpose(b_t[:, s], rows[:, k, 0:P], ident[:, :])
                        ins = pe.transpose(b_t[0:CV, K * P + k * P:K * P + (k + 1) * P], rows[:, k, P:C], ident[:, :])
                    return ins

                def body(i):
                    n = i + 1
                    for b in range(2):
                        pe.wait_ge(in_[b], 64 * n)
                        pe.wait_ge(row_in[b], 32 * n)
                        if b:
                            pe.wait_ge(s_out[0], n)
                        else:
                            free(pe, d_out[1], i)
                        turn(xs[b]).then_inc(s_turned[b], 1)
                        before(pe, gt_out, i, b)
                        for k in range(K):
                            ins = pe.matmul(b_g[:, k, 0:C], attr[b][:, k * P:(k + 1) * P], w["rad"][:, :], start=True, stop=True)
                        ins.then_inc(gt_done[b], 1)
                        pe.wait_ge(s_out[b], n)
                        before(pe, f_used, i, b)
                        for k in range(K):
                            s = slice(k * P, (k + 1) * P)
                            pe.matmul(b_f[:, k, 0:288], sm[b][:, s], w["g_m"][:, :], start=True, stop=True)
                            ins = pe.matmul(b_f[:, k, 288:384], sr[b][:, s], w["g_r"][:, :], start=True, stop=True)
                        ins.then_inc(f_done[b], 1)
                    for b in range(2):
                        pe.wait_ge(xd_in[b], 32 * n)
                        pe.wait_ge(d_out[0] if b else s_out[1], n)
                        turn(xd[b]).then_inc(d_turned[b], 1)
                    for b in range(2):
                        pe.wait_ge(mid_ready[b], n)
                        pe.wait_ge(runs.done[b], n)
                        for k in range(K):
                            pe.matmul(b_s[b][:, k, 0:P], mid[b][:, k, 0:P], runs.eq[b][:, k, :], start=True, stop=True)
                            ins = pe.matmul(b_s[b][0:CV, k, P:2 * P], mid[b][:, k, P:C], runs.eq[b][:, k, :],
                                            start=True, stop=True)
                        ins.then_inc(seg_done[b], 1)
                    for b in range(2):
                        pe.wait_ge(d_out[b], n)
                        pe.wait_ge(g_done[b], n)
                        for k in range(K):
                            s = slice(k * P, (k + 1) * P)
                            pe.matmul(b_y[b][:, k, 0:P], dm[b][:, s], w["sc3_m"][:, :], start=True, stop=False)
                            pe.matmul(b_y[b][:, k, 0:P], gm[b][:, k, :], w["sc3_m"][:, :], start=False, stop=True)
                            pe.matmul(b_y[b][:, k, P:C], dr[b][:, s], w["sc3_r"][:, :], start=True, stop=False)
                            ins = pe.matmul(b_y[b][:, k, P:C], gr[b][:, k, :], w["sc3_r"][:, :], start=False, stop=True)
                        ins.then_inc(y_done[b], 1)

                body(0)
                with pe.Fori(1, iters) as i:
                    body(i)



def build(nc, ins, out):
    d = dict(ins)
    d["out"] = out
    NT = d["ends"].shape[1]
    E_pad = NT * P
    N = d["xa"].shape[0]
    d["NT"], d["E_pad"] = NT, E_pad

    def table(name, shape, dt=F32):
        d[name] = nc.dram_tensor(name, shape, dt, kind="Internal").ap()

    table("slot", (N, 1), I32)
    table("meta", (E_pad, MW))
    table("B0", (E_pad, C + 1))
    for l in (1, 2, 3):
        table(f"B{l}", (E_pad, C))
    table("D0", (E_pad, C + 1))
    table("H0", (E_pad, C))
    for l in (1, 2, 3):
        table(f"D{l}", (E_pad, ROW))
    for n in ("A0", "R0", "X0", "S0"):
        table(n, (4, E_pad))
    with ExitStack() as ctx:
        w = load_weights(nc, ctx, d)
        iters = -(-N // (8 * P))
        assert NT == 2 * iters and NT % BODY == 0
        chain(nc, w, d, "nodes", 4, iters, sources=False)
        chain(nc, w, d, "sources", PAIR, NT // BODY, sources=True)
        attend0(nc, w, d)
        soften0(nc, d)
        update0(nc, w, d)
        conv(nc, w, d, 1)
        conv(nc, w, d, 2)
        conv3(nc, w, d)


def layout(inputs):
    x = np.asarray(inputs["x"])
    N = x.shape[0]
    dst, src = np.asarray(inputs["dst"], np.int32), np.asarray(inputs["src"], np.int32)
    E = dst.shape[0]
    NT = -(-E // (BODY * P)) * BODY
    E_pad = NT * P

    def padded(a, fill):
        return np.concatenate([a, np.full((E_pad - E,) + a.shape[1:], fill, a.dtype)])

    def by_lane(a):
        return np.ascontiguousarray(a.reshape(NT, P, -1).transpose(1, 0, 2))

    d0, dp, sp = padded(dst, 0), padded(dst, N), padded(src, 0)
    nxt = np.concatenate([dp[1:], np.full(1, N + 1, np.int32)])
    a16, a8, a4 = (padded(np.asarray(inputs[k]), 0) for k in ("edge_attr_16", "edge_attr_8", "edge_attr_4"))
    order = np.concatenate([np.arange(CS), CS + np.arange(3 * CV).reshape(CV, 3).T.ravel()])
    out = {
        "xa": np.concatenate([x, np.asarray(inputs["node_vec1"])], 1),
        "ends": by_lane(np.stack([dp, nxt], 1)),
        "edge_ids": by_lane(np.repeat(np.arange(E_pad, dtype=np.int32)[:, None], 2, 1)),
        "eint": np.stack([sp, dp, nxt, d0], 1),
        "dst_row": np.concatenate([np.full(1, N + 1, np.int32), dp, np.full(1, N + 1, np.int32)])[None],
        "y": a4,
        "attr16": np.concatenate([a16.T, np.ones((1, E_pad), np.float32)]),
        "attr8": np.ascontiguousarray(a8.T),
        "ws_valT": np.ascontiguousarray(np.asarray(inputs["L0_gnn_Ws_val"]).T),
        "w_rad_ext": np.concatenate([np.asarray(inputs["L3_gnn_W_rad"]).T,
                                     np.asarray(inputs["L3_gnn_b_rad"])[None]])[:, order],
    }
    for k, v in inputs.items():
        if k.startswith("L") and k not in ("L3_gnn_W_rad", "L3_gnn_b_rad"):
            v = np.asarray(v)
            out[k] = v.reshape(-1) if k == "L0_gnn_alpha_dot" else v.reshape(v.shape[0], -1)
    return {k: np.ascontiguousarray(v) for k, v in out.items()}


def kernel(**inputs):
    import concourse.bacc as bacc
    from concourse.bass_utils import run_bass_kernel_spmd as run

    nc = bacc.Bacc("TRN2", target_bir_lowering=False, num_devices=1)
    arrays = {f"in_{k}": v for k, v in layout(inputs).items()}
    ins = {k[3:]: nc.dram_tensor(k, v.shape, mybir.dt.from_np(v.dtype), kind="ExternalInput").ap()
           for k, v in arrays.items()}
    N = arrays["in_xa"].shape[0]
    out = nc.dram_tensor("out_x", (N, C), F32, kind="ExternalOutput").ap()
    build(nc, ins, out)
    r = run(nc, [arrays], core_ids=[0])
    return r.results[0]["out_x"]
```

```python
from contextlib import ExitStack, contextmanager

import numpy as np

import concourse.bass as bass
from concourse import mybir

F32 = mybir.dt.float32
I32 = mybir.dt.int32
ALU = mybir.AluOpType
ACT = mybir.ActivationFunctionType
AX = mybir.AxisListType

P = 128
CS, CV = 64, 32
C = CS + 3 * CV
EPS = 1e-5
PAIR = 2
PLACES, NODE_PLACES = 4, 6
BODY = PLACES * PAIR
NEG = -1.0e30
ROW = C + 2
MW = 13
M_YA, M_Y, M_DST, M_REP, M_LAST = 0, 4, 10, 11, 12
W96 = CS + CV


def cm(ap):
    return ap.rearrange("p (u c) -> p c u", c=3)


@contextmanager
def phase(nc):
    with nc.cleanup_on_exit():
        with ExitStack() as ctx:
            yield ctx


class Alloc:

    def __init__(self, nc, ctx, name, places=2):
        self.nc, self.ctx, self.name, self.places = nc, ctx, name, places

    def sb(self, name, shape, dt=F32):
        return self.ctx.enter_context(self.nc.sbuf_tensor(f"{self.name}_{name}", shape, dt))

    def ps(self, name, shape):
        return self.ctx.enter_context(self.nc.psum_tensor(f"{self.name}_{name}", shape, F32))

    def sem(self, name):
        return self.nc.alloc_semaphore(name=f"{self.name}_{name}")

    def sems(self, name, n=None):
        return [self.sem(f"{name}{b}") for b in range(n or self.places)]

    def sbs(self, name, shape, dt=F32):
        return [self.sb(f"{name}{b}", shape, dt) for b in range(self.places)]


def free(eng, sem, value):
    if not (isinstance(value, int) and value == 0):
        eng.wait_ge(sem, value)


def staged(eng, iters, front, tail, mid, last_tail=None):
    front(0)
    mid(0)
    front(1)
    tail(0)
    mid(1)
    with eng.Fori(2, iters) as i:
        front(i)
        tail(i - 1)
        mid(i)
    (last_tail or tail)(iters - 1)


def interleaved(eng, iters, prepare, first, second):
    prepare(0)
    first(0)
    prepare(1)
    second(0)
    with eng.Fori(1, iters - 1) as i:
        first(i)
        prepare(i + 1)
        second(i)
    first(iters - 1)
    second(iters - 1)


def ready(eng, sems, i, b):
    eng.wait_ge(sems[b], i + 1)


def apart(eng, sem, value, passed):
    eng.wait_ge(sem, value).then_inc(passed, 1)


def vec(ap):
    return ap.rearrange("p (c u) -> p c u", c=3)


def before(eng, sems, i, b):
    free(eng, sems[b - 1], i + (1 if b else 0))



def load_weights(nc, ctx, d):
    A = Alloc(nc, ctx, "w")
    w = {}
    loads, scales, colscales = [], [], []

    def tile(name, shape):
        w[name] = A.sb(name, shape)
        return w[name]

    def block(name, ws, wv, fs, fv):
        m = tile(name + "_m", [P, P])
        r = tile(name + "_r", [CV, CV])
        loads.append((m[0:CS, 0:CS], d[ws]))
        loads.append((m[64:96, 64:96], d[wv]))
        loads.append((m[96:128, 96:128], d[wv]))
        loads.append((r[:, :], d[wv]))
        scales.append((r[:, :], fv))
        scales.append((m[0:CS, 0:CS], fs))
        scales.append((m[64:128, 64:128], fv))

    i8, i32 = 1 / 8.0, 1 / np.sqrt(32.0)
    block("sc1", "L1_gnn_Wsc0", "L1_gnn_Wsc1", i8, i32)
    block("sc2", "L2_gnn_Wsc0", "L2_gnn_Wsc1", i8, i32)
    block("sc3", "L3_gnn_L_s", "L3_gnn_L_v", i8, i32)
    block("f1", "L1_gnn_Wl1_0", "L1_gnn_Wl1_1", i8, i32)
    block("f2", "L2_gnn_Wl1_0", "L2_gnn_Wl1_1", i8, i32)
    src_m = tile("src_m", [P, P])
    loads.append((src_m[0:CS, 0:CS], d["L0_gnn_Ws_src"]))
    loads.append((src_m[64:96, 64:96], d["L0_gnn_Wv_src"]))
    loads.append((src_m[96:128, 96:128], d["L0_gnn_Wv_src"]))
    dst_m = tile("dst_m", [P, P])
    loads.append((dst_m[0:32, 96:128], d["L0_gnn_Wv_dst"]))
    loads.append((dst_m[32:64, 64:96], d["L0_gnn_Wv_dst"]))
    loads.append((dst_m[64:128, 0:CS], d["L0_gnn_Ws_dst"]))
    ends_r = tile("ends_r", [2 * CV + 1, C])
    loads.append((ends_r[0:CV, P:C], d["L0_gnn_Wv_src"]))
    loads.append((ends_r[CV:2 * CV, P:C], d["L0_gnn_Wv_dst"]))
    block("out0", "L0_gnn_Wps", "L0_gnn_Wpv", 1.0, 1.0)

    def plain(name, src, rows, cols, f=1.0):
        t = tile(name, [rows, cols])
        loads.append((t[:, :], d[src]))
        if f != 1.0:
            scales.append((t[:, :], f))
        return t

    plain("fc1_1", "L1_gnn_Wfc1", 8, 64)
    plain("fc1_2", "L1_gnn_Wfc2", 64, 64)
    t = plain("fc1_3", "L1_gnn_Wfc3", 64, 192)
    scales.append((t[:, 160:192], 1 / np.sqrt(3.0)))
    plain("fc2_1", "L2_gnn_Wfc1", 16, 64)
    t = plain("fc2_3", "L2_gnn_Wfc2", 64, 192)
    scales.append((t[:, 160:192], 1 / np.sqrt(3.0)))
    for l, f in ((1, 1 / np.sqrt(32.0) / np.sqrt(96.0)), (2, 1 / np.sqrt(96.0))):
        plain(f"ov{l}", f"L{l}_gnn_Wl2_v", W96, CV, f)
        t = tile(f"oa{l}", [W96 + 1, 2 + CS])
        loads.append((t[0:W96, 0:1], d[f"L{l}_gnn_Wa"]))
        loads.append((t[0:W96, 2:2 + CS], d[f"L{l}_gnn_Wl2_s"]))
        scales.append((t[0:W96, 0:1], f))
        scales.append((t[0:W96, 2:2 + CS], f))
    plain("rbf", "L0_gnn_W_rbf", 16, 224)
    scales.append((w["rbf"][:, 160:192], 1 / np.sqrt(3.0)))
    scales.append((w["rbf"][:, 192:224], 1 / np.sqrt(2.0)))
    va = tile("va", [W96, 160])
    loads.append((va[:, 0:64], d["L0_gnn_Ws_val"]))
    loads.append((va[:, 64:128], d["L0_gnn_W_alpha"]))
    plain("valT", "ws_valT", 64, W96)
    plain("wg", "L0_gnn_Wg", 64, CV)
    plain("wvval", "L0_gnn_Wv_val", P, CV)
    adot = tile("adot", [P, 64])
    loads.append((adot[:, :], d["L0_gnn_alpha_dot"].partition_broadcast(P)))
    hm = tile("h_m", [P, 224])
    hr = tile("h_r", [64, 128])
    loads.append((hm[0:64, 0:64], d["L0_gnn_Ws_vlin"][0:64, :]))
    loads.append((hm[0:64, 64:96], d["L0_gnn_Wv_vlin"][0:64, :]))
    for g in range(2):
        loads.append((hm[64 + 32 * g:96 + 32 * g, 96 + 64 * g:128 + 64 * g], d["L0_gnn_Wv_vlin"][64:96, :]))
        loads.append((hm[64 + 32 * g:96 + 32 * g, 128 + 64 * g:160 + 64 * g], d["L0_gnn_Wv_vlin"][96:128, :]))
    loads.append((hr[0:32, 0:32], d["L0_gnn_Wv_vlin"][64:96, :]))
    loads.append((hr[0:32, 32:64], d["L0_gnn_Wv_vlin"][96:128, :]))
    loads.append((hr[32:64, 64:128], d["L0_gnn_Ws_vlin"][64:96, :]))
    cols = tile("cols", [P, 12])

    def col(c, at, src, n):
        loads.append((cols[at:at + n, c:c + 1], d[src]))

    col(0, 0, "L0_gnn_w2_ss", 64)
    col(1, 0, "L0_gnn_w2_sv", 64)
    for at in (64, 96):
        col(2, at, "L0_gnn_w2_vs", 32)
        col(3, at, "L0_gnn_w2_vv1", 32)
    col(4, 0, "L0_gnn_w2_vs", 32)
    col(5, 0, "L0_gnn_w2_vv1", 32)
    col(6, 32, "L0_gnn_w2_vv0", 32)
    col(7, 0, "L0_gnn_gamma_s", 64)
    col(7, 64, "L0_gnn_gamma_v", 32)
    col(7, 96, "L0_gnn_gamma_v", 32)
    col(8, 0, "L0_gnn_gamma_v", 32)
    col(8, 32, "L0_gnn_gamma_v", 32)
    col(8, 64, "L0_gnn_gamma_s", 64)
    col(9, 0, "L0_gnn_beta_s", 64)
    colscales += [(hm[0:64, 0:64], cols[0:64, 0:1], 1.0), (hm[0:64, 64:96], cols[0:64, 1:2], 1.0)]
    for g in range(2):
        a, b = 64 + 32 * g, 96 + 32 * g
        colscales.append((hm[a:b, 96 + 64 * g:128 + 64 * g], cols[a:b, 2:3], 1.0))
        colscales.append((hm[a:b, 128 + 64 * g:160 + 64 * g], cols[a:b, 3:4], 1 / np.sqrt(2.0)))
    colscales.append((hr[0:32, 0:32], cols[0:32, 4:5], 1.0))
    colscales.append((hr[0:32, 32:64], cols[0:32, 5:6], 1 / np.sqrt(2.0)))
    colscales.append((hr[32:64, 64:128], cols[32:64, 6:7], 1 / np.sqrt(3.0)))
    raw_src, raw_dst = plain("ws_src", "L0_gnn_Ws_src", 64, 64), plain("ws_dst", "L0_gnn_Ws_dst", 64, 64)
    colscales.append((w["src_m"][:, :], cols[:, 7:8], 1.0))
    colscales.append((dst_m[:, :], cols[:, 8:9], 1.0))
    colscales.append((ends_r[0:2 * CV, P:C], cols[0:2 * CV, 8:9], 1.0))
    g_m, g_r = tile("g_m", [P, 288]), tile("g_r", [CV, W96])
    i2, i3 = 1 / np.sqrt(2.0), 1 / np.sqrt(3.0)
    loads.append((g_m[0:64, 0:64], d["L3_gnn_W_ss"]))
    loads.append((g_m[0:64, 64:96], d["L3_gnn_W_sv"]))
    scales += [(g_m[0:64, 0:64], i2 * i8), (g_m[0:64, 64:96], i2 * i3 * i8)]
    for g in range(2):
        a, c = 64 + 32 * g, 96 * (g + 1)
        loads.append((g_m[a:a + 32, c:c + 64], d["L3_gnn_W_vv"]))
        loads.append((g_m[a:a + 32, c + 64:c + 96], d["L3_gnn_W_vs"]))
        scales.append((g_m[a:a + 32, c:c + 96], i2 * i3 * i32))
    loads.append((g_r[:, 0:64], d["L3_gnn_W_vv"]))
    loads.append((g_r[:, 64:96], d["L3_gnn_W_vs"]))
    scales.append((g_r[:, :], i2 * i3 * i32))
    plain("rad", "w_rad_ext", 17, C)
    ident = tile("ident", [P, P])
    eps = tile("eps", [P, 5])
    big = [w[n] for n in w if n.endswith("_m") or n.endswith("_r")]
    with phase(nc) as pctx:
        A = Alloc(nc, pctx, "setup")
        N = d["xa"].shape[0]
        slots = A.sb("slots", [P, (N + P - 1) // P], I32)
        pw = A.ps("pw", [W96, 512])

        zeroed, ident_done, weights_in = A.sem("zeroed"), A.sem("ident_done"), A.sem("weights_in")
        scaled, products, slots_set = A.sem("scaled"), A.sem("products"), A.sem("slots_set")
        slots_out = A.sem("slots_out")
        with nc.Block() as block:
            @block.gpsimd
            def _(pool):
                for t in big:
                    last = pool.memset(t[:, :], 0.0)
                last.then_inc(zeroed, 1)
                pool.memset(ident[:, :], 0.0).then_inc(ident_done, 1)
                pool.wait_ge(ident_done, 1)
                pool.affine_select(out=ident[:, :], in_=ident[:, :], compare_op=ALU.not_equal, fill=1.0,
                                   base=0, pattern=[[-1, P]], channel_multiplier=1).then_inc(ident_done, 1)
                pool.wait_ge(ident_done, 2)

            @block.sync
            def _(sp):
                sp.wait_ge(zeroed, 1)
                for dst, src in loads:
                    sp.dma_start(dst, src).then_inc(weights_in, 16)
                sp.wait_ge(slots_set, 1)
                full = slots.shape[1]
                rows = N // full
                sp.dma_start(d["slot"][0:rows * full, :].rearrange("(p k) c -> p (k c)", k=full),
                             slots[0:rows, :]).then_inc(slots_out, 16)
                if N % full:
                    sp.dma_start(d["slot"][rows * full:N, :].rearrange("(p k) c -> p (k c)", p=1),
                                 slots[0:1, 0:N % full]).then_inc(slots_out, 16)
                    sp.wait_ge(slots_out, 32)
                else:
                    sp.wait_ge(slots_out, 16)

            @block.vector
            def _(dve):
                dve.memset(slots[:, :], d["E_pad"] + 1).then_inc(slots_set, 1)
                dve.memset(eps[:, 0:1], EPS)
                for k in range(1, 5):
                    dve.memset(eps[:, k:k + 1], EPS ** k / 4)
                for l in (1, 2):
                    dve.memset(w[f"oa{l}"][0:W96, 1:2], 0.0)
                    dve.memset(w[f"oa{l}"][W96:W96 + 1, 0:1], 0.0)
                    dve.memset(w[f"oa{l}"][W96:W96 + 1, 1:2], 1.0)
                    dve.memset(w[f"oa{l}"][W96:W96 + 1, 2:2 + CS], 0.0)
                dve.wait_ge(weights_in, 16 * len(loads))
                for k, (ap, f) in enumerate(scales):
                    dve.tensor_scalar(ap, ap, float(f), None, ALU.mult).then_inc(scaled, 1)
                dve.wait_ge(scaled, len(scales))
                for ap, c, f in colscales:
                    dve.tensor_scalar(ap, ap, c, float(f), ALU.mult, ALU.mult).then_inc(scaled, 1)
                dve.wait_ge(scaled, len(scales) + len(colscales))
                dve.wait_ge(products, 1)
                dve.tensor_copy(w["va"][:, 128:160], pw[:, 0:CV]).then_inc(scaled, 1)
                dve.tensor_copy(ends_r[2 * CV:2 * CV + 1, 0:CS], pw[0:1, 128:128 + CS]).then_inc(scaled, 1)
                dve.wait_ge(scaled, len(scales) + len(colscales) + 2)

            @block.tensor
            def _(pe):
                pe.wait_ge(weights_in, 16 * len(loads))
                pe.matmul(pw[:, 0:CV], w["valT"][:, :], w["wg"][:, :], start=True, stop=True)
                pe.matmul(pw[0:1, 128:192], cols[0:64, 9:10], raw_src[:, :], start=True, stop=False)
                pe.matmul(pw[0:1, 128:192], cols[0:64, 9:10], raw_dst[:, :], start=False, stop=True).then_inc(products, 1)
    return w



def tiles_of(ap, at, g):
    return ap[bass.ds(at, g * P), :].rearrange("(g p) c -> p g c", p=P)


def last_edges(dve, out, ends, flag, big, done, value):
    dve.tensor_tensor(flag, ends[:, :, 0], ends[:, :, 1], ALU.not_equal).then_inc(done, 1)
    dve.wait_ge(done, value + 1)
    dve.scalar_tensor_tensor(flag, ends[:, :, 0], float(-big), flag, ALU.add, ALU.mult).then_inc(done, 1)
    dve.wait_ge(done, value + 2)
    return dve.tensor_scalar(out, flag, float(big), None, ALU.add)


def chain(nc, w, d, name, NB, iters, sources):
    N, NT = d["xa"].shape[0], d["NT"]
    G = PAIR
    step_rows = NB * G * P
    slots = min(NB, 3) if NB % 3 == 0 else NB
    groups = [(b, b + 1) for b in range(0, NB, 2)]
    layers = 2 if sources else 3
    L = layers + 1
    big = 2 * N
    with phase(nc) as ctx:
        A = Alloc(nc, ctx, name, NB)
        xin, ac = A.sbs("xin", [P, G, C + 1]), A.sbs("ac", [P, G])
        st, mv = A.sbs("st", [P, G, 6]), A.sb("mv", [P, L, NB, G, 2])
        z = [A.sbs(f"z{l + 1}", [P, G, C]) for l in range(layers)]
        pre = A.sbs("pre", [P, G, C])
        tm, tr = A.sbs("tm", [P, G * P]), A.sbs("tr", [CV, G * P])
        terms = (1, 2, 3) if sources else (4,)
        n_s = len(terms)
        wt = A.sb("wt", [P, n_s, L, NB, G])
        va, vs, sd, rs, nb = (A.sb(n, [P, n_s] + s) for n, s in (
            ("va", [L, NB, G]), ("vs", [NB, G]), ("sd", [NB, G]), ("rs", [NB, G]), ("nb", [NB, G])))
        b_t = [A.ps(f"b_t{s}", [P, 512]) for s in range(slots)]
        b_y = [A.ps(f"b_y{s}", [P, G, 256]) for s in range(slots)]

        x_in, taken = A.sems("x_in"), A.sems("taken")
        stats, aggr, z_ready = A.sems("stats"), A.sems("aggr"), [A.sems(f"z{l + 1}_ready") for l in range(layers)]
        turned, turned_out, y_done, pre_done = (A.sems(n) for n in ("turned", "turned_out", "y_done", "pre_done"))
        weighted, summed, roots, inverse, shift = (
            [A.sem(f"{n}{q}") for q in range(len(groups))] for n in ("weighted", "summed", "roots", "inverse", "shift"))
        passed, start = A.sem("passed"), A.sem("start")
        out_ready, entered, stored = A.sems("out_ready"), A.sems("entered"), A.sems("stored")
        if sources:
            meta, eint, yin = A.sbs("meta", [P, G, MW]), A.sbs("eint", [P, G, 4], I32), A.sbs("yin", [P, G, 4])
            xl = [A.sbs(f"x{l}", [P, G, C]) for l in (1, 2, 3)]
            nrs, lst, rep = A.sb("nrs", [P, 2, NB, G]), A.sbs("lst", [P, G]), A.sbs("rep", [P, G], I32)
            e_in, rep_in, meta_set, lst_done = (A.sems(n) for n in ("e_in", "rep_in", "meta_set", "lst_done"))
        else:
            ob = A.sbs("ob", [P, G, C])
            ids, ends = A.sb("ids", [P, NT, 2], I32), A.sb("ends", [P, NT, 2], I32)
            endf = A.sb("endf", [P, NT])
            ring = [A.sb(f"ring{r}", [P, 1, 2], I32) for r in range(2)]
            ends_in, ids_done = A.sem("ends_in"), A.sem("ids_done")
            ring_in, ring_used = A.sems("ring_in", 2), A.sems("ring_used", 2)

        def slot_free(eng, sems, r, b):
            if b >= slots:
                eng.wait_ge(sems[b - slots], r + 1)
            else:
                free(eng, sems[b + NB - slots], r)

        def centre(eng, b):
            for k in range(G):
                eng.tensor_scalar(z[0][b][:, k, 0:CS], xin[b][:, k, 0:CS], mv[:, 0, b, k, 0:1], None, ALU.subtract)
                ins = eng.tensor_scalar(vec(z[0][b][:, k, CS:C]), cm(xin[b][:, k, CS:C]), mv[:, 0, b, k, 0:1],
                                        None, ALU.subtract)
            ins.then_inc(z_ready[0][b], 1)

        with nc.Block() as block:
            @block.sync
            def _(sp):
                if sources:
                    def loads(i):
                        for b in range(NB):
                            at = (NB * i + b) * G * P
                            free(sp, meta_set[b], i)
                            sp.dma_start(eint[b][:, :, :], tiles_of(d["eint"], at, G)).then_inc(e_in[b], 16)
                            sp.dma_start(yin[b][:, :, :], tiles_of(d["y"], at, G)).then_inc(e_in[b], 16)

                    def entries(i):
                        for b in range(NB):
                            at = (NB * i + b) * G * P
                            ready(sp, meta_set, i, b)
                            ready(sp, z_ready[0], i, b)
                            sp.dma_start(tiles_of(d["meta"], at, G), meta[b][:, :, :]).then_inc(entered[b], 16)
                            sp.dma_start(tiles_of(d["B0"], at, G), xin[b][:, :, :]).then_inc(entered[b], 16)

                    def stores(i):
                        for b in range(NB):
                            at = (NB * i + b) * G * P
                            ready(sp, out_ready, i, b)
                            for l in range(3):
                                sp.dma_start(tiles_of(d[f"B{l + 1}"], at, G), xl[l][b][:, :, :]).then_inc(stored[b], 16)

                    loads(0)
                    entries(0)
                    loads(1)
                    with sp.Fori(1, iters - 1) as i:
                        entries(i)
                        loads(i + 1)
                        stores(i - 1)
                    entries(iters - 1)
                    stores(iters - 2)
                    stores(iters - 1)
                    for b in range(NB):
                        sp.wait_ge(entered[b], 32 * iters)
                        sp.wait_ge(stored[b], 48 * iters)
                    return

                sp.dma_start(ends[:, :, :], d["ends"]).then_inc(ends_in, 16)
                sp.dma_start(ids[:, :, :], d["edge_ids"]).then_inc(ends_in, 16)

                def nodes(i, row):
                    for b in range(NB):
                        free(sp, z_ready[0][b], i)
                        free(sp, taken[b], i)
                        sp.dma_start(xin[b][:, :, :], d["xa"][bass.ds(row + b * G * P, G * P), :]
                                     .rearrange("(p g) c -> p g c", g=G)).then_inc(x_in[b], 16)

                def outs(i, row):
                    for b in range(NB):
                        ready(sp, out_ready, i, b)
                        sp.dma_start(d["out"][bass.ds(row + b * G * P, G * P), :]
                                     .rearrange("(p g) c -> p g c", g=G), ob[b][:, :, :]).then_inc(stored[b], 16)

                nodes(0, 0)
                with sp.Fori(1, iters - 1) as i:
                    nodes(i, i * step_rows)
                    outs(i - 1, (i - 1) * step_rows)
                nodes(iters - 1, N - step_rows)
                outs(iters - 2, (iters - 2) * step_rows)
                for b in range(NB):
                    sp.wait_ge(stored[b], 16 * (iters - 1))
                outs(iters - 1, N - step_rows)
                for b in range(NB):
                    sp.wait_ge(stored[b], 16 * iters)

            @block.gpsimd
            def _(pool):
                top = pool.to_reg(N - 1)

                def gathers(i):
                    for b in range(NB):
                        free(pool, entered[b], 32 * i)
                        apart(pool, e_in[b], 32 * i + 32, passed)
                        for k in range(G):
                            pool.indirect_dma_start(
                                xin[b][:, k, :], None, d["xa"],
                                bass.IndirectOffsetOnAxis(ap=eint[b][:, k, 0:1], axis=0),
                                bounds_check=top, oob_is_err=False).then_inc(x_in[b], 16)
                            pool.indirect_dma_start(
                                rep[b][:, k:k + 1], None, d["slot"],
                                bass.IndirectOffsetOnAxis(ap=eint[b][:, k, 0:1], axis=0),
                                bounds_check=top, oob_is_err=False).then_inc(rep_in[b], 16)

                def scatters(i):
                    for r in range(2):
                        free(pool, ring_used[r], 16 * i)
                        pool.dma_start(ring[r][:, :, :], ids[:, bass.ds(2 * i + r, 1), :]).then_inc(ring_in[r], 16)
                    for r in range(2):
                        apart(pool, ring_in[r], 16 * i + 16, passed)
                        pool.indirect_dma_start(
                            d["slot"], bass.IndirectOffsetOnAxis(ap=ring[r][:, 0, 0:1], axis=0),
                            ring[r][:, 0, 1:2], None, bounds_check=top,
                            oob_is_err=False).then_inc(ring_used[r], 16)

                def centres(i):
                    for b in range(NB):
                        free(pool, pre_done[b], i * layers)
                        apart(pool, aggr[b], i * L + 1, passed)
                        centre(pool, b)

                if sources:
                    gathers(0)
                    with pool.Fori(1, iters) as i:
                        gathers(i)
                else:
                    centres(0)
                    pool.wait_ge(ids_done, 3)
                    scatters(0)
                    with pool.Fori(1, iters) as i:
                        centres(i)
                        scatters(i)
                    with pool.Fori(iters, NT // 2) as i:
                        scatters(i)
                    for r in range(2):
                        pool.wait_ge(ring_used[r], 16 * (NT // 2))

            @block.vector
            def _(dve):
                for k in range(n_s):
                    for l in range(L):
                        ins = dve.memset(wt[:, k, l, :, :], float(EPS) ** (terms[k] - 1 - l) if l < terms[k] else 0.0)
                ins.then_inc(start, 1)
                dve.wait_ge(start, 1)
                if not sources:
                    dve.wait_ge(ends_in, 32)
                    last_edges(dve, ids[:, :, 0], ends, endf[:, :], big, ids_done, 0).then_inc(ids_done, 1)

                def statistics(r, l, src, group):
                    for b in group:
                        for k in range(G):
                            ins = dve.bn_stats(st[b][:, k, :], src[b][:, k, 0:C])
                        ins.then_inc(stats[b], 1)
                    for b in group:
                        apart(dve, stats[b], r + 1, passed)
                        for k in range(G):
                            ins = dve.bn_aggr(mv[:, l, b, k, :], st[b][:, k, :])
                        ins.then_inc(aggr[b], 1)

                def describe(i, b):
                    dve.wait_ge(e_in[b], 32 * i + 32)
                    dve.wait_ge(rep_in[b], 16 * G * (i + 1))
                    dve.tensor_tensor(meta[b][:, :, M_YA:M_YA + 4], yin[b][:, :, :],
                                      xin[b][:, :, C:C + 1].to_broadcast([P, G, 4]), ALU.mult)
                    dve.tensor_copy(meta[b][:, :, M_Y:M_Y + 4], yin[b][:, :, :])
                    dve.tensor_copy(meta[b][:, :, M_Y + 4:M_Y + 6], yin[b][:, :, 1:3])
                    mint = meta[b][:, :, :].bitcast(I32)
                    dve.tensor_copy(mint[:, :, M_DST:M_DST + 1], eint[b][:, :, 1:2])
                    dve.tensor_copy(mint[:, :, M_REP], rep[b][:, :])
                    last_edges(dve, mint[:, :, M_LAST], eint[b][:, :, 1:3], lst[b][:, :], big,
                               lst_done[b], 2 * i).then_inc(meta_set[b], 1)

                def enter(i, group):
                    for b in group:
                        dve.wait_ge(x_in[b], 16 * (G if sources else 1) * (i + 1))
                    statistics(i * L, 0, xin, group)
                    for b in group:
                        dve.tensor_copy(ac[b][:, :], xin[b][:, :, C]).then_inc(taken[b], 1)
                        if sources:
                            describe(i, b)
                    if sources:
                        for b in group:
                            dve.wait_ge(aggr[b], i * L + 1)
                            free(dve, out_ready[b], i)
                            centre(dve, b)

                def advance(i, l, group):
                    for b in group:
                        s = b % slots
                        dve.wait_ge(y_done[b], i * layers + l + 1)
                        for k in range(G):
                            if l < 2:
                                ins = dve.scalar_tensor_tensor(pre[b][:, k, :], b_y[s][:, k, 0:C],
                                                               ac[b][:, k:k + 1], z[l][b][:, k, :],
                                                               ALU.mult, ALU.add)
                            else:
                                ins = dve.tensor_tensor(pre[b][:, k, :], b_y[s][:, k, 0:C],
                                                        z[l][b][:, k, :], ALU.add)
                        ins.then_inc(pre_done[b], 1)
                    for b in group:
                        dve.wait_ge(pre_done[b], i * layers + l + 1)
                    statistics(i * L + l + 1, l + 1, pre, group)

                def deviations(i, q):
                    bs = slice(groups[q][0], groups[q][-1] + 1)
                    for b in groups[q]:
                        dve.wait_ge(aggr[b], i * L + L)
                    for k, n in enumerate(terms):
                        ins = dve.tensor_tensor(va[:, k, 0:n, bs, :].rearrange("p l b g -> p l (b g)"),
                                                mv[:, 0:n, bs, :, 1].rearrange("p l b g -> p l (b g)"),
                                                wt[:, k, 0:n, bs, :].rearrange("p l b g -> p l (b g)"), ALU.mult)
                    ins.then_inc(weighted[q], 1)
                    dve.wait_ge(weighted[q], i + 1)
                    for k, n in enumerate(terms):
                        ins = dve.tensor_reduce(vs[:, k, bs, :].rearrange("p b g -> p (b g)"),
                                                va[:, k, 0:n, bs, :].rearrange("p l b g -> p (b g) l"), AX.X, ALU.add)
                    ins.then_inc(summed[q], 1)

                def inverses(i, q):
                    bs = slice(groups[q][0], groups[q][-1] + 1)
                    dve.wait_ge(roots[q], i + 1)
                    dve.reciprocal(rs[:, :, bs, :], sd[:, :, bs, :]).then_inc(inverse[q], 1)
                    dve.wait_ge(inverse[q], i + 1)
                    if sources:
                        dve.tensor_scalar(nrs[:, :, bs, :], rs[:, 1:3, bs, :], -1.0, None, ALU.mult)
                    dve.scalar_tensor_tensor(nb[:, 0, bs, :], mv[:, layers, bs, :, 0], 1.0 if sources else -1.0,
                                             rs[:, n_s - 1, bs, :], ALU.mult, ALU.mult).then_inc(shift[q], 1)

                def body(i, more=True):
                    for l in range(layers - 1):
                        for group in groups:
                            advance(i, l, group)
                    for q, group in enumerate(groups):
                        advance(i, layers - 1, group)
                        deviations(i, q)
                        if q:
                            inverses(i, q - 1)
                            if more:
                                enter(i + 1, groups[q - 1])
                    inverses(i, len(groups) - 1)
                    if more:
                        enter(i + 1, groups[-1])

                for group in groups:
                    enter(0, group)
                body(0)
                with dve.Fori(1, iters - 1) as i:
                    body(i)
                body(iters - 1, more=False)

            @block.scalar
            def _(act):
                def turn_out(i, l, group):
                    if l:
                        for b in group:
                            act.wait_ge(aggr[b], i * L + l + 1)
                            for k in range(G):
                                ins = act.activation(z[l][b][:, k, :], pre[b][:, k, :], ACT.Identity,
                                                     bias=mv[:, l, b, k, 0:1], scale=-1.0)
                            ins.then_inc(z_ready[l][b], 1)
                    for b in group:
                        s = b % slots
                        act.wait_ge(turned[b], i * layers + l + 1)
                        act.activation(tm[b][:, :], b_t[s][:, 0:G * P], ACT.Copy)
                        act.activation(tr[b][:, :], b_t[s][0:CV, G * P:2 * G * P], ACT.Copy).then_inc(turned_out[b], 1)

                def deviations(i, q):
                    bs = slice(groups[q][0], groups[q][-1] + 1)
                    act.wait_ge(summed[q], i + 1)
                    for k, n in enumerate(terms):
                        ins = act.activation(sd[:, k, bs, :], vs[:, k, bs, :], ACT.Sqrt, bias=w["eps"][:, n:n + 1])
                    ins.then_inc(roots[q], 1)

                def results(i, q):
                    act.wait_ge(shift[q], i + 1)
                    for b in groups[q]:
                        free(act, stored[b], (48 if sources else 16) * i)
                        for k in range(G):
                            if sources:
                                act.activation(xl[0][b][:, k, :], z[0][b][:, k, :], ACT.Copy, scale=rs[:, 0, b, k:k + 1])
                                act.activation(xl[1][b][:, k, :], z[1][b][:, k, :], ACT.Copy, scale=nrs[:, 0, b, k:k + 1])
                                ins = act.activation(xl[2][b][:, k, :], pre[b][:, k, :], ACT.Identity,
                                                     bias=nb[:, 0, b, k:k + 1], scale=nrs[:, 1, b, k:k + 1])
                            else:
                                sc, bi = rs[:, 0, b, k:k + 1], nb[:, 0, b, k:k + 1]
                                act.activation(ob[b][:, k, 0:CS], pre[b][:, k, 0:CS], ACT.Identity, bias=bi, scale=sc)
                                ins = act.activation(cm(ob[b][:, k, CS:C]), vec(pre[b][:, k, CS:C]), ACT.Identity,
                                                     bias=bi, scale=sc)
                        ins.then_inc(out_ready[b], 1)

                def body(i, more=True):
                    for l in range(1, layers - 1):
                        for group in groups:
                            turn_out(i, l, group)
                    Q = len(groups)
                    for q in range(Q):
                        turn_out(i, layers - 1, groups[q])
                        if q:
                            deviations(i, q - 1)
                            if q > 1:
                                results(i, q - 2)
                    deviations(i, Q - 1)
                    for q in range(Q):
                        if q >= Q - 2:
                            results(i, q)
                        if more:
                            turn_out(i + 1, 0, groups[q])

                for group in groups:
                    turn_out(0, 0, group)
                body(0)
                with act.Fori(1, iters - 1) as i:
                    body(i)
                body(iters - 1, more=False)

            @block.tensor
            def _(pe):
                def body(i):
                    for l in range(layers):
                        wm, wr = w[f"sc{l + 1}_m"], w[f"sc{l + 1}_r"]
                        r = i * layers + l
                        for group in groups:
                            for b in group:
                                s = b % slots
                                ready(pe, z_ready[l], i, b)
                                slot_free(pe, turned_out, r, b)
                                for k in range(G):
                                    pe.transpose(b_t[s][:, k * P:(k + 1) * P], z[l][b][:, k, 0:P], w["ident"][:, :])
                                    ins = pe.transpose(b_t[s][0:CV, (G + k) * P:(G + k + 1) * P], z[l][b][:, k, P:C],
                                                       w["ident"][:, :])
                                ins.then_inc(turned[b], 1)
                            for b in group:
                                s = b % slots
                                pe.wait_ge(turned_out[b], r + 1)
                                slot_free(pe, pre_done, r, b)
                                for k in range(G):
                                    pe.matmul(b_y[s][:, k, 0:P], tm[b][:, k * P:(k + 1) * P], wm[:, :], start=True, stop=True)
                                    ins = pe.matmul(b_y[s][:, k, P:C], tr[b][:, k * P:(k + 1) * P], wr[:, :],
                                                    start=True, stop=True)
                                ins.then_inc(y_done[b], 1)

                body(0)
                with pe.Fori(1, iters) as i:
                    body(i)



def vecs(ap):
    return ap.rearrange("p k (c u) -> p k c u", c=3)


def spread(ap, shape):
    return ap.to_broadcast(shape)


def edge_rows(nc, ap, at, n):
    return ap[:, bass.ds(at, n)]


def attend0(nc, w, d):
    NT, N = d["NT"], d["xa"].shape[0]
    iters = NT // BODY
    K = PAIR
    with phase(nc) as ctx:
        A = Alloc(nc, ctx, "att", PLACES)
        xr = A.sbs("xr", [P, 2 * K, C + 1])
        meta, eint = A.sbs("meta", [P, K, MW]), A.sbs("eint", [P, K, 4], I32)
        attr, drow = A.sbs("attr", [16, K * P]), A.sbs("drow", [4, K * P + 2], I32)
        st, mv, sq = A.sbs("st", [P, 2 * K, 6]), A.sbs("mv", [P, 2 * K, 2]), A.sbs("sq", [P, 2 * K, 96])
        ss, sd, rs = (A.sbs(n, [P, 2 * K] + r) for n, r in (("ss", []), ("sd", [2]), ("rs", [2])))
        xn = A.sbs("xn", [P, K, 2 * C])
        tm, tr = A.sbs("tm", [P, 2 * K * P]), A.sbs("tr", [2 * CV + 1, K * P])
        msg = A.sbs("msg", [P, K, CS + 5 * CV])
        ws, t1, t2, q = A.sbs("ws", [P, K, 128]), A.sbs("t1", [P, K, 96]), A.sbs("t2", [P, K, 96]), A.sbs("q", [P, K, 96])
        wv, cr, dt = A.sbs("wv", [P, K, CV]), A.sbs("cr", [P, K, 96]), A.sbs("dt", [P, K, CV])
        m1 = A.sbs("m1", [P, K, 480])
        m1t = A.sbs("m1t", [P, K, 512])
        val, gate, al = A.sbs("val", [P, K, 192]), A.sbs("gate", [P, K, CV]), A.sbs("al", [P, K, 64])
        la, lb, q2, sc = A.sbs("la", [P, K, 64]), A.sbs("lb", [P, K, 64]), A.sbs("q2", [P, K, 96]), A.sbs("sc", [P, K, 4])
        vt, vr, at4 = A.sbs("vt", [P, K * P]), A.sbs("vr", [64, K * P]), A.sbs("at4", [4, K * P])
        e5 = A.sbs("e5", [P, K, 160])
        h1, c1, p1, e1, e2, c2, e3 = (A.sbs(n, [P, K, 64 if n == "h1" else 96])
                                      for n in ("h1", "c1", "p1", "e1", "e2", "c2", "e3"))
        h = A.sbs("h", [P, K, C])
        pen, pen2, mrun = A.sbs("pen", [4, K * P]), A.sbs("pen2", [4, K * P]), A.sbs("mrun", [4, K * P])

        banks = A.ps("banks", [P, 8, 512])
        halves = [banks[:, k, :].rearrange("p (k e) -> p k e", k=K) for k in range(8)]
        b_t, b_r = (banks[:, 0, :], banks[:, 2, :]), (banks[:, 1, :], banks[:, 3, :])
        b_m, b_w = (halves[4], halves[5]), (halves[6], halves[7])
        b_u = (banks[:, 0:2, :], banks[:, 2:4, :])
        b_vt, b_vr = (banks[:, 4, :], banks[:, 0, :]), (banks[:, 5, :], banks[:, 1, :])
        b_h = (banks[:, 2:4, :], banks[:, 4:6, :])

        in_, meta_in, d_in, d0_out = (A.sems(n) for n in ("in", "meta_in", "d_in", "d0_out"))
        stats, squares, aggr, roots, scl = (A.sems(n) for n in ("stats", "squares", "aggr", "roots", "scl"))
        xn_s, xn_v, turned, turned_out = (A.sems(n) for n in ("xn_s", "xn_v", "turned", "turned_out"))
        msg_done, msg_out, p_a, p_b, m1_ready = (A.sems(n) for n in ("msg_done", "msg_out", "p_a", "p_b", "m1_ready"))
        m1_turned, m1_out, va_done, acts = (A.sems(n) for n in ("m1_turned", "m1_out", "va_done", "acts"))
        c_a, c_b, c_ready, v_turned, v_out = (A.sems(n) for n in ("c_a", "c_b", "c_ready", "v_turned", "v_out"))
        h_done, e_out, d_a, d_b, h_ready, stored = (A.sems(n) for n in ("h_done", "e_out", "d_a", "d_b", "h_ready", "stored"))
        start, passed = A.sem("start"), A.sem("passed")

        def pos(i, b):
            return (PLACES * i + b) * K * P

        with nc.Block() as block:
            @block.sync
            def _(sp):
                def row_loads(i):
                    for b in range(PLACES):
                        free(sp, xn_s[b], i)
                        free(sp, xn_v[b], i)
                        free(sp, msg_done[b], i)
                        at = pos(i, b)
                        sp.dma_start(xr[b][:, 0:K, :], tiles_of(d["B0"], at, K)).then_inc(in_[b], 16)
                        sp.dma_start(eint[b][:, :, :], tiles_of(d["eint"], at, K)).then_inc(in_[b], 16)
                        sp.dma_start(attr[b][:, :], d["attr16"][0:16, bass.ds(at, K * P)]).then_inc(in_[b], 16)

                def edge_loads(i):
                    for b in range(PLACES):
                        free(sp, h_ready[b], i)
                        sp.dma_start(meta[b][:, :, :], tiles_of(d["meta"], pos(i, b), K)).then_inc(meta_in[b], 16)
                        sp.dma_start(drow[b][:, :], d["dst_row"][0:1, bass.ds(pos(i, b), K * P + 2)]
                                     .partition_broadcast(4)).then_inc(meta_in[b], 16)

                def stores(i):
                    for b in range(PLACES):
                        ready(sp, h_ready, i, b)
                        at = pos(i, b)
                        sp.dma_start(tiles_of(d["H0"], at, K), h[b][:, :, :]).then_inc(stored[b], 16)
                        sp.dma_start(d["A0"][:, bass.ds(at, K * P)], at4[b][:, :]).then_inc(stored[b], 16)
                        sp.dma_start(d["R0"][:, bass.ds(at, K * P)], mrun[b][:, :]).then_inc(stored[b], 16)

                row_loads(0)
                edge_loads(0)
                row_loads(1)
                with sp.Fori(1, iters - 1) as i:
                    edge_loads(i)
                    stores(i - 1)
                    row_loads(i + 1)
                edge_loads(iters - 1)
                stores(iters - 2)
                stores(iters - 1)
                for b in range(PLACES):
                    sp.wait_ge(stored[b], 48 * iters)

            @block.gpsimd
            def _(pool):
                top = pool.to_reg(N - 1)
                def body(i):
                    for b in range(PLACES):
                        free(pool, d0_out[b], 16 * i)
                        apart(pool, in_[b], 48 * i + 48, passed)
                        for k in range(K):
                            pool.indirect_dma_start(
                                xr[b][:, K + k, :], None, d["xa"],
                                bass.IndirectOffsetOnAxis(ap=eint[b][:, k, 3:4], axis=0),
                                bounds_check=top, oob_is_err=False).then_inc(d_in[b], 16)

                body(0)
                with pool.Fori(1, iters) as i:
                    body(i)

            @block.vector
            def _(dve):
                for b in range(PLACES):
                    dve.memset(tr[b][2 * CV:2 * CV + 1, :], 1.0)
                dve.memset(mrun[-1][:, :], NEG).then_inc(start, 1)
                dve.wait_ge(start, 1)
                def normalise(i):
                    n = i + 1
                    for b in range(PLACES):
                        dve.wait_ge(in_[b], 48 * n)
                        dve.wait_ge(d_in[b], 32 * n)
                        for k in range(2 * K):
                            ins = dve.bn_stats(st[b][:, k, :], xr[b][:, k, 0:CS])
                        ins.then_inc(stats[b], 1)
                    for b in range(PLACES):
                        apart(dve, stats[b], n, passed)
                        for k in range(2 * K):
                            ins = dve.bn_aggr(mv[b][:, k, :], st[b][:, k, :])
                        ins.then_inc(aggr[b], 1)
                    for b in range(PLACES):
                        dve.wait_ge(roots[b], n)
                        dve.reciprocal(rs[b][:, :, :], sd[b][:, :, :]).then_inc(scl[b], 1)
                    for b in range(PLACES):
                        dve.wait_ge(scl[b], n)
                        for k in range(2 * K):
                            to = xn[b][:, k, 0:CS] if k < K else xn[b][:, k - K, 2 * C - CS:2 * C]
                            ins = dve.tensor_scalar(to, xr[b][:, k, 0:CS], mv[b][:, k, 0:1],
                                                    rs[b][:, k, 0:1], ALU.subtract, ALU.mult)
                        ins.then_inc(xn_s[b], 1)

                def products(i):
                    n = i + 1
                    for b in range(PLACES):
                        dve.wait_ge(meta_in[b], 32 * n)
                        dve.wait_ge(msg_done[b], n)
                        dve.wait_ge(msg_out[b], n)
                        y, W, m = meta[b], b_w[b % 2], msg[b]
                        S3, S64 = [P, K, 3, CV], [P, K, 3, CS]
                        y0, yx = y[:, :, M_Y:M_Y + 1], y[:, :, M_Y + 1:M_Y + 4]
                        yx1, yx2 = y[:, :, M_Y + 2:M_Y + 5], y[:, :, M_Y + 3:M_Y + 6]

                        def over(ap, shape):
                            return ap.unsqueeze(3).to_broadcast(shape)

                        dve.tensor_tensor(ws[b][:, :, :].rearrange("p k (a u) -> p k a u", a=2),
                                          W[:, :, 0:128].rearrange("p k (a u) -> p k a u", a=2),
                                          m[:, :, 0:CS].unsqueeze(2).to_broadcast([P, K, 2, CS]), ALU.mult)
                        dve.tensor_tensor(vecs(t1[b][:, :, :]), vecs(m[:, :, 96:192]), over(yx2, S3), ALU.mult)
                        dve.tensor_tensor(vecs(t2[b][:, :, :]), vecs(m[:, :, 128:224]), over(yx1, S3), ALU.mult)
                        dve.tensor_tensor(vecs(q[b][:, :, :]), vecs(m[:, :, 64:160]), over(yx, S3), ALU.mult)
                        dve.tensor_tensor(wv[b][:, :, :], W[:, :, 128:160], y0.to_broadcast([P, K, CV]),
                                          ALU.mult).then_inc(p_a[b], 1)
                        dve.wait_ge(p_a[b], n)
                        dve.tensor_tensor(m1[b][:, :, 0:CS], ws[b][:, :, 0:CS], y0.to_broadcast([P, K, CS]), ALU.mult)
                        mx = m1[b][:, :, 96:480].rearrange("p k (c u) -> p k c u", c=3)
                        dve.tensor_tensor(mx[:, :, :, 0:CS], ws[b][:, :, 64:128].unsqueeze(2).to_broadcast(S64),
                                          over(yx, S64), ALU.mult)
                        dve.tensor_tensor(cr[b][:, :, :], t1[b][:, :, :], t2[b][:, :, :], ALU.subtract)
                        dve.tensor_tensor(mx[:, :, :, 64:96], vecs(m[:, :, 64:160]),
                                          wv[b][:, :, :].unsqueeze(2).to_broadcast(S3), ALU.mult)
                        dve.tensor_reduce(dt[b][:, :, :], q[b][:, :, :].rearrange("p k (c u) -> p k u c", c=3),
                                          AX.X, ALU.add).then_inc(p_b[b], 1)
                        dve.wait_ge(p_b[b], n)
                        dve.tensor_tensor(m1[b][:, :, CS:96], W[:, :, 160:192], dt[b][:, :, :], ALU.mult)
                        dve.tensor_tensor(mx[:, :, :, 96:128], W[:, :, 192:224].unsqueeze(2).to_broadcast(S3),
                                          vecs(cr[b][:, :, :]), ALU.mult).then_inc(m1_ready[b], 1)

                def values(i):
                    n = i + 1
                    for b in range(PLACES):
                        y, W = meta[b], b_w[b % 2]
                        S3 = [P, K, 3, CV]
                        yx = y[:, :, M_Y + 1:M_Y + 4]
                        dve.wait_ge(va_done[b], n)
                        dve.wait_ge(acts[b], n)
                        dve.tensor_tensor(vecs(val[b][:, :, 64:160]), vecs(W[:, :, 160:256]),
                                          gate[b][:, :, :].unsqueeze(2).to_broadcast(S3), ALU.mult)
                        dve.scalar_tensor_tensor(la[b][:, :, :], al[b][:, :, :], 0.2, al[b][:, :, :],
                                                 ALU.mult, ALU.max).then_inc(c_a[b], 1)
                        dve.wait_ge(c_a[b], n)
                        dve.tensor_tensor(vecs(q2[b][:, :, :]), vecs(val[b][:, :, 64:160]),
                                          yx.unsqueeze(3).to_broadcast(S3), ALU.mult)
                        dve.tensor_tensor(lb[b][:, :, :], la[b][:, :, :],
                                          w["adot"][:, :].unsqueeze(1).to_broadcast([P, K, 64]), ALU.mult).then_inc(c_b[b], 1)
                        dve.wait_ge(c_b[b], n)
                        dve.tensor_reduce(val[b][:, :, 160:192], q2[b][:, :, :].rearrange("p k (c u) -> p k u c", c=3),
                                          AX.X, ALU.add)
                        dve.tensor_reduce(sc[b][:, :, :], lb[b][:, :, :].rearrange("p k (h u) -> p k h u", h=4),
                                          AX.X, ALU.add).then_inc(c_ready[b], 1)
                    for b in range(PLACES):
                        y = meta[b]
                        S3 = [P, K, 3, CV]
                        y0, yx = y[:, :, M_Y:M_Y + 1], y[:, :, M_Y + 1:M_Y + 4].unsqueeze(3).to_broadcast(S3)
                        yx1 = y[:, :, M_Y + 2:M_Y + 5].unsqueeze(3).to_broadcast(S3)
                        yx2 = y[:, :, M_Y + 3:M_Y + 6].unsqueeze(3).to_broadcast(S3)
                        dve.wait_ge(h_done[b], n)
                        dve.wait_ge(e_out[b], n)
                        free(dve, stored[b], 48 * i)
                        dve.tensor_tensor(h1[b][:, :, :], b_h[b % 2][:, :, 0:CS], y0.to_broadcast([P, K, CS]), ALU.mult)
                        dve.tensor_tensor(vecs(c1[b][:, :, :]), b_h[b % 2][:, :, 64:96].unsqueeze(2).to_broadcast(S3), yx, ALU.mult)
                        de = b_h[b % 2][:, :, 96:288].rearrange("p k (c u) -> p k c u", c=3)
                        dve.tensor_tensor(vecs(p1[b][:, :, :]), de[:, :, :, 0:CV],
                                          y0.unsqueeze(3).to_broadcast(S3), ALU.mult)
                        dve.tensor_tensor(vecs(e1[b][:, :, :]), vecs(e5[b][:, :, 32:128]), yx2, ALU.mult)
                        dve.tensor_tensor(vecs(e2[b][:, :, :]), vecs(e5[b][:, :, 64:160]), yx1, ALU.mult)
                        dve.tensor_tensor(pen[b][:, :], drow[b][:, 1:K * P + 1], drow[b][:, 0:K * P],
                                          ALU.not_equal).then_inc(d_a[b], 1)
                        dve.wait_ge(d_a[b], n)
                        dve.tensor_tensor(h[b][:, :, 0:CS], b_h[b % 2][:, :, 288:352], h1[b][:, :, :], ALU.add)
                        dve.tensor_tensor(c2[b][:, :, :], c1[b][:, :, :], p1[b][:, :, :], ALU.add)
                        dve.tensor_tensor(e3[b][:, :, :], e1[b][:, :, :], e2[b][:, :, :], ALU.subtract)
                        dve.tensor_scalar(pen2[b][:, :], pen[b][:, :], NEG, None, ALU.mult).then_inc(d_b[b], 1)
                        dve.wait_ge(d_b[b], n)
                        if b:
                            dve.wait_ge(h_ready[b - 1], n)
                        dve.tensor_tensor(h[b][:, :, CS:C], c2[b][:, :, :], e3[b][:, :, :], ALU.add)
                        dve.tensor_tensor_scan(mrun[b][:, :], pen2[b][:, :], at4[b][:, :],
                                               mrun[b - 1][:, K * P - 1:K * P], ALU.add, ALU.max).then_inc(h_ready[b], 1)
                    dve.wait_ge(h_ready[-1], n)

                interleaved(dve, iters, normalise, products, values)

            @block.scalar
            def _(act):
                def normalise(i):
                    n = i + 1
                    for b in range(PLACES):
                        act.wait_ge(in_[b], 48 * n)
                        act.wait_ge(d_in[b], 32 * n)
                        act.dma_start(tiles_of(d["D0"], pos(i, b), K), xr[b][:, K:2 * K, :]).then_inc(d0_out[b], 16)
                        for k in range(2 * K):
                            ins = act.activation(sq[b][:, k, :], xr[b][:, k, CS:C], ACT.Square, accum_out=ss[b][:, k:k + 1])
                        ins.then_inc(squares[b], 1)
                    for b in range(PLACES):
                        act.wait_ge(squares[b], n)
                        act.activation(sd[b][:, :, 1], ss[b][:, :], ACT.Sqrt, bias=w["eps"][:, 0:1], scale=1.0 / CV)
                        act.wait_ge(aggr[b], n)
                        act.activation(sd[b][:, :, 0], mv[b][:, :, 1], ACT.Sqrt, bias=w["eps"][:, 0:1]).then_inc(roots[b], 1)
                    for b in range(PLACES):
                        act.wait_ge(scl[b], n)
                        for k in range(2 * K):
                            to = vec(xn[b][:, k, CS:C]) if k < K else vec(xn[b][:, k - K, C:2 * C - CS])[:, ::-1, :]
                            ins = act.activation(to, cm(xr[b][:, k, CS:C]), ACT.Copy, scale=rs[b][:, k, 1:2])
                        ins.then_inc(xn_v[b], 1)

                def products(i):
                    n = i + 1
                    for b in range(PLACES):
                        act.wait_ge(turned[b], n)
                        act.activation(tm[b][:, :], b_t[b % 2], ACT.Copy)
                        act.activation(tr[b][0:2 * CV, :], b_r[b % 2][0:2 * CV, 0:K * P], ACT.Copy).then_inc(turned_out[b], 1)
                    for b in range(PLACES):
                        act.wait_ge(msg_done[b], n)
                        act.activation(msg[b][:, :, 0:C], b_m[b % 2][:, :, 0:C], ACT.Copy)
                        act.activation(msg[b][:, :, C:C + 64], b_m[b % 2][:, :, CS:CS + 64], ACT.Copy).then_inc(msg_out[b], 1)
                    for b in range(PLACES):
                        act.wait_ge(m1_turned[b], n)
                        for k in range(K):
                            act.activation(m1t[b][0:96, k, 0:128], b_u[b % 2][0:96, k, 0:128], ACT.Copy)
                            ins = act.activation(m1t[b][:, k, 128:512], b_u[b % 2][:, k, 128:512], ACT.Copy)
                        ins.then_inc(m1_out[b], 1)

                def values(i):
                    n = i + 1
                    for b in range(PLACES):
                        act.wait_ge(va_done[b], n)
                        act.activation(val[b][:, :, 0:CS], b_w[b % 2][:, :, 0:CS], ACT.Sigmoid)
                        act.activation(gate[b][:, :, :], b_w[b % 2][:, :, 128:160], ACT.Sigmoid)
                        act.activation(al[b][:, :, :], b_w[b % 2][:, :, 64:128], ACT.Copy).then_inc(acts[b], 1)
                    for b in range(PLACES):
                        act.wait_ge(v_turned[b], n)
                        free(act, stored[b], 48 * i)
                        act.activation(vt[b][:, :], b_vt[b % 2][:, 0:K * P], ACT.Copy)
                        act.activation(vr[b][:, :], b_vr[b % 2][0:64, 0:K * P], ACT.Copy)
                        act.activation(at4[b][:, :], b_vr[b % 2][0:4, K * P:2 * K * P], ACT.Copy).then_inc(v_out[b], 1)
                    for b in range(PLACES):
                        act.wait_ge(h_done[b], n)
                        de = b_h[b % 2][:, :, 96:288].rearrange("p k (c u) -> p k c u", c=3)
                        act.activation(vecs(e5[b][:, :, 0:96]), de[:, :, :, CV:2 * CV], ACT.Copy)
                        act.activation(e5[b][:, :, 96:160].rearrange("p k (c u) -> p k c u", c=2), de[:, :, 0:2, CV:2 * CV],
                                       ACT.Copy).then_inc(e_out[b], 1)

                interleaved(act, iters, normalise, products, values)
                for b in range(PLACES):
                    act.wait_ge(d0_out[b], 16 * iters)

            @block.tensor
            def _(pe):
                ident = w["ident"]
                def products(i):
                    n = i + 1
                    for b in range(PLACES):
                        pe.wait_ge(xn_s[b], n)
                        pe.wait_ge(xn_v[b], n)
                        if b >= 2:
                            pe.wait_ge(turned_out[b - 2], n)
                        elif b:
                            free(pe, h_ready[2], i)
                        for k in range(K):
                            pe.transpose(b_t[b % 2][:, k * P:(k + 1) * P], xn[b][:, k, 0:P], ident[:, :])
                            pe.transpose(b_t[b % 2][:, (K + k) * P:(K + k + 1) * P], xn[b][:, k, 2 * C - P:2 * C], ident[:, :])
                            ins = pe.transpose(b_r[b % 2][0:2 * CV, k * P:(k + 1) * P], xn[b][:, k, P:2 * C - P], ident[:, :])
                        ins.then_inc(turned[b], 1)
                    for b in range(PLACES):
                        pe.wait_ge(turned_out[b], n)
                        pe.wait_ge(in_[b], 48 * n)
                        if b >= 2:
                            pe.wait_ge(msg_out[b - 2], n)
                            pe.wait_ge(m1_ready[b - 2], n)
                        elif b == 0:
                            free(pe, h_ready[3], i)
                        for k in range(K):
                            s, t = slice(k * P, (k + 1) * P), slice((K + k) * P, (K + k + 1) * P)
                            pe.matmul(b_m[b % 2][:, k, 0:C], tr[b][:, s], w["ends_r"][:, :], start=True, stop=False)
                            pe.matmul(b_m[b % 2][:, k, 0:P], tm[b][:, s], w["src_m"][:, :], start=False, stop=False)
                            pe.matmul(b_m[b % 2][:, k, 0:P], tm[b][:, t], w["dst_m"][:, :], start=False, stop=True)
                            ins = pe.matmul(b_w[b % 2][:, k, 0:224], attr[b][:, s], w["rbf"][:, :], start=True, stop=True)
                        ins.then_inc(msg_done[b], 1)
                    for b in range(PLACES):
                        pe.wait_ge(m1_ready[b], n)
                        if b >= 2:
                            pe.wait_ge(m1_out[b - 2], n)
                        for k in range(K):
                            pe.transpose(b_u[b % 2][0:96, k, 0:P], m1[b][:, k, 0:96], ident[:, :])
                            for c in range(3):
                                ins = pe.transpose(b_u[b % 2][:, k, P * (c + 1):P * (c + 2)],
                                                   m1[b][:, k, 96 + P * c:96 + P * (c + 1)], ident[:, :])
                        ins.then_inc(m1_turned[b], 1)

                def values(i):
                    n = i + 1
                    for b in range(PLACES):
                        pe.wait_ge(m1_out[b], n)
                        if b >= 2:
                            pe.wait_ge(acts[b - 2], n)
                            pe.wait_ge(c_a[b - 2], n)
                        for k in range(K):
                            pe.matmul(b_w[b % 2][:, k, 0:C], m1t[b][0:96, k, 0:P], w["va"][:, :], start=True, stop=True)
                            for c in range(3):
                                ins = pe.matmul(b_w[b % 2][:, k, C + 32 * c:C + 32 * c + 32],
                                                m1t[b][:, k, P * (c + 1):P * (c + 2)], w["wvval"][:, :],
                                                start=True, stop=True)
                        ins.then_inc(va_done[b], 1)
                    for b in range(PLACES):
                        pe.wait_ge(c_ready[b], n)
                        if b >= 2:
                            pe.wait_ge(v_out[b - 2], n)
                        for k in range(K):
                            s = slice(k * P, (k + 1) * P)
                            pe.transpose(b_vt[b % 2][:, s], val[b][:, k, 0:P], ident[:, :])
                            pe.transpose(b_vr[b % 2][0:64, s], val[b][:, k, P:192], ident[:, :])
                            ins = pe.transpose(b_vr[b % 2][0:4, (K + k) * P:(K + k + 1) * P], sc[b][:, k, :], ident[:, :])
                        ins.then_inc(v_turned[b], 1)
                    for b in range(PLACES):
                        pe.wait_ge(v_out[b], n)
                        if b >= 2:
                            pe.wait_ge(h_ready[b - 2], n)
                        elif b:
                            pe.wait_ge(v_out[2], n)
                        for k in range(K):
                            s = slice(k * P, (k + 1) * P)
                            pe.matmul(b_h[b % 2][:, k, 0:224], vt[b][:, s], w["h_m"][:, :], start=True, stop=True)
                            ins = pe.matmul(b_h[b % 2][:, k, 224:352], vr[b][:, s], w["h_r"][:, :], start=True, stop=True)
                        ins.then_inc(h_done[b], 1)

                def body(i):
                    products(i)
                    values(i)

                body(0)
                with pe.Fori(1, iters) as i:
                    body(i)


def soften0(nc, d):
    E_pad = d["E_pad"]
    CH = max(c for c in range(1, min(2048, E_pad // 4) + 1) if E_pad % (2 * c) == 0)
    iters = E_pad // (2 * CH)
    with phase(nc) as ctx:
        A = Alloc(nc, ctx, "soft")
        a, m, dr = A.sbs("a", [4, CH]), A.sbs("m", [4, CH]), A.sbs("dr", [4, CH + 1], I32)
        same, pen, top = A.sbs("same", [4, CH]), A.sbs("pen", [4, CH]), A.sbs("top", [4, CH])
        dif, ex, bs = A.sbs("dif", [4, CH]), A.sbs("ex", [4, CH]), A.sbs("bs", [4, CH])
        in_, same_done, pen_done, top_done, dif_done, ex_done, bs_done, stored = (
            A.sems(n) for n in ("in", "same", "pen", "top", "dif", "ex", "bs", "stored"))
        start = A.sem("start")

        def at(i, b):
            return i * (-2 * CH) + (E_pad - (b + 1) * CH)

        with nc.Block() as block:
            @block.sync
            def _(sp):
                def loads(i):
                    for b in range(2):
                        free(sp, bs_done[b], i)
                        sp.dma_start(a[b][:, :], edge_rows(nc, d["A0"], at(i, b), CH)).then_inc(in_[b], 16)
                        sp.dma_start(m[b][:, :], edge_rows(nc, d["R0"], at(i, b), CH)).then_inc(in_[b], 16)
                        sp.dma_start(dr[b][:, :], d["dst_row"][0:1, bass.ds(at(i, b) + 1, CH + 1)]
                                     .partition_broadcast(4)).then_inc(in_[b], 16)

                def stores(i):
                    for b in range(2):
                        ready(sp, bs_done, i, b)
                        sp.dma_start(edge_rows(nc, d["X0"], at(i, b), CH), ex[b][:, :]).then_inc(stored[b], 16)
                        sp.dma_start(edge_rows(nc, d["S0"], at(i, b), CH), bs[b][:, :]).then_inc(stored[b], 16)

                loads(0)
                if iters > 1:
                    with sp.Fori(1, iters) as i:
                        loads(i)
                        stores(i - 1)
                stores(iters - 1)
                for b in range(2):
                    sp.wait_ge(stored[b], 32 * iters)

            @block.vector
            def _(dve):
                dve.memset(top[1][:, :], NEG)
                dve.memset(bs[1][:, :], 0.0).then_inc(start, 1)
                dve.wait_ge(start, 1)
                def body(i):
                    n = i + 1
                    for b in range(2):
                        dve.wait_ge(in_[b], 48 * n)
                        dve.tensor_tensor(same[b][:, :], dr[b][:, 0:CH], dr[b][:, 1:CH + 1], ALU.is_equal).then_inc(same_done[b], 1)
                    for b in range(2):
                        dve.wait_ge(same_done[b], n)
                        dve.tensor_scalar(pen[b][:, :], same[b][:, :], -NEG, NEG, ALU.mult, ALU.add).then_inc(pen_done[b], 1)
                    for b in range(2):
                        dve.wait_ge(pen_done[b], n)
                        if b:
                            dve.wait_ge(top_done[0], n)
                        else:
                            free(dve, top_done[1], i)
                        dve.tensor_tensor_scan(top[b][:, ::-1], pen[b][:, ::-1], m[b][:, ::-1], top[1 - b][:, 0:1],
                                               ALU.add, ALU.max).then_inc(top_done[b], 1)
                    for b in range(2):
                        dve.wait_ge(top_done[b], n)
                        dve.tensor_tensor(dif[b][:, :], a[b][:, :], top[b][:, :], ALU.subtract).then_inc(dif_done[b], 1)
                    for b in range(2):
                        dve.wait_ge(ex_done[b], n)
                        free(dve, stored[b], 32 * i)
                        if b:
                            dve.wait_ge(bs_done[0], n)
                        else:
                            free(dve, bs_done[1], i)
                        dve.tensor_tensor_scan(bs[b][:, ::-1], same[b][:, ::-1], ex[b][:, ::-1], bs[1 - b][:, 0:1],
                                               ALU.mult, ALU.add).then_inc(bs_done[b], 1)

                body(0)
                with dve.Fori(1, iters) as i:
                    body(i)

            @block.scalar
            def _(act):
                def body(i):
                    for b in range(2):
                        ready(act, dif_done, i, b)
                        free(act, stored[b], 32 * i)
                        act.activation(ex[b][:, :], dif[b][:, :], ACT.Exp).then_inc(ex_done[b], 1)

                body(0)
                with act.Fori(1, iters) as i:
                    body(i)


class Runs:

    def __init__(self, A):
        self.row = A.sbs("row", [P, PAIR * P + 1], I32)
        self.eq, self.ind = A.sbs("eq", [P, PAIR, P]), A.sbs("ind", [P, PAIR, P])
        self.done = A.sems("runs")

    def load(self, sp, d, at, b, sem):
        sp.dma_start(self.row[b][:, :], d["dst_row"][0:1, bass.ds(at, PAIR * P + 1)]
                     .partition_broadcast(P)).then_inc(sem, 16)

    def matrices(self, eng, b, dst_col):
        rows = self.row[b][:, 1:PAIR * P + 1].rearrange("p (k e) -> p k e", k=PAIR)
        before_ = self.row[b][:, 0:PAIR * P].rearrange("p (k e) -> p k e", k=PAIR)[:, :, 0:1]
        eng.tensor_tensor(self.eq[b][:, :, :], rows, dst_col.to_broadcast([P, PAIR, P]), ALU.is_equal)
        eng.tensor_tensor(self.ind[b][:, :, :], rows, before_.to_broadcast([P, PAIR, P]),
                          ALU.is_equal).then_inc(self.done[b], 1)


class Norm:

    def __init__(self, A):
        K = PAIR
        self.st, self.mv = A.sbs("n_st", [P, K, 6]), A.sbs("n_mv", [P, K, 2])
        self.sd, self.rs, self.nb = A.sbs("n_sd", [P, K]), A.sbs("n_rs", [P, K]), A.sbs("n_nb", [P, K])
        self.stats, self.aggr, self.roots, self.scl, self.nbd = (
            A.sems("n_" + x) for x in ("stats", "aggr", "roots", "scl", "nbd"))
        self.passed = A.sem("n_passed")

    def vector(self, dve, n, pre, pre_ready):
        for b in range(PLACES):
            dve.wait_ge(pre_ready[b], n)
            for k in range(PAIR):
                ins = dve.bn_stats(self.st[b][:, k, :], pre[b][:, k, :])
            ins.then_inc(self.stats[b], 1)
        for b in range(PLACES):
            apart(dve, self.stats[b], n, self.passed)
            for k in range(PAIR):
                ins = dve.bn_aggr(self.mv[b][:, k, :], self.st[b][:, k, :])
            ins.then_inc(self.aggr[b], 1)
        for b in range(PLACES):
            dve.wait_ge(self.roots[b], n)
            dve.reciprocal(self.rs[b][:, :], self.sd[b][:, :]).then_inc(self.scl[b], 1)
        for b in range(PLACES):
            dve.wait_ge(self.scl[b], n)
            dve.scalar_tensor_tensor(self.nb[b][:, :], self.mv[b][:, :, 0], -1.0, self.rs[b][:, :],
                                     ALU.mult, ALU.mult).then_inc(self.nbd[b], 1)

    def scalar_roots(self, act, n, eps):
        for b in range(PLACES):
            act.wait_ge(self.aggr[b], n)
            act.activation(self.sd[b][:, :], self.mv[b][:, :, 1], ACT.Sqrt, bias=eps).then_inc(self.roots[b], 1)

    def scalar_apply(self, act, b, k, out, pre):
        return act.activation(out, pre, ACT.Identity, bias=self.nb[b][:, k:k + 1], scale=self.rs[b][:, k:k + 1])


def update0(nc, w, d):
    NT = d["NT"]
    iters, K = NT // BODY, PAIR
    with phase(nc) as ctx:
        A = Alloc(nc, ctx, "upd", PLACES)
        h, x0, eint = A.sbs("h", [P, K, C]), A.sbs("x0", [P, K, C + 1]), A.sbs("eint", [P, K, 4], I32)
        ex, bs, same = A.sbs("ex", [4, K * P]), A.sbs("bs", [4, K * P]), A.sbs("same", [4, K * P])
        den = A.sbs("den", [4, K * P])
        de2, rden, alpha = (A.sbs(n, [P, K, 4]) for n in ("de2", "rden", "alpha"))
        ha, gm, gr = A.sbs("ha", [P, K, C]), A.sbs("gm", [P, K, P]), A.sbs("gr", [CV, K, P])
        pre, x1 = A.sbs("pre", [P, K, C]), A.sbs("x1", [P, K, ROW])
        runs, norm = Runs(A), Norm(A)
        b_al = [A.ps(f"b_al{b}", [P, 512]) for b in range(2)]
        b_s, b_y = [A.ps(f"b_s{b}", [P, K, 256]) for b in range(2)], [A.ps(f"b_y{b}", [P, K, 256]) for b in range(2)]
        in_, x_in, same_done, den_done, de2_done, rden_done, alpha_done = (
            A.sems(n) for n in ("in", "x_in", "same", "den", "de2", "rden", "alpha"))
        al_done, ha_done, seg_done, g_done, y_done, pre_done, x1_s, x1_v, stored = (
            A.sems(n) for n in ("al", "ha", "seg", "g", "y", "pre", "x1_s", "x1_v", "stored"))
        h_in = A.sems("h_in")
        g_half, start, passed = A.sems("g_half"), A.sem("start"), A.sem("passed")

        def pos(i, b):
            return (PLACES * i + b) * K * P

        with nc.Block() as block:
            @block.sync
            def _(sp):
                def early(i):
                    for b in range(PLACES):
                        free(sp, al_done[b], i)
                        free(sp, runs.done[b], i)
                        at = pos(i, b)
                        sp.dma_start(eint[b][:, :, :], tiles_of(d["eint"], at, K)).then_inc(in_[b], 16)
                        sp.dma_start(ex[b][:, :], d["X0"][:, bass.ds(at, K * P)]).then_inc(in_[b], 16)
                        sp.dma_start(bs[b][:, :], d["S0"][:, bass.ds(at, K * P)]).then_inc(in_[b], 16)
                        runs.load(sp, d, at, b, in_[b])

                def messages(i):
                    for b in range(PLACES):
                        free(sp, ha_done[b], i)
                        sp.dma_start(h[b][:, :, :], tiles_of(d["H0"], pos(i, b), K)).then_inc(h_in[b], 16)

                def late(i):
                    for b in range(PLACES):
                        free(sp, x1_v[b], i)
                        sp.dma_start(x0[b][:, :, :], tiles_of(d["D0"], pos(i, b), K)).then_inc(x_in[b], 16)

                def stores(i):
                    for b in range(PLACES):
                        ready(sp, x1_s, i, b)
                        ready(sp, x1_v, i, b)
                        sp.dma_start(tiles_of(d["D1"], pos(i, b), K), x1[b][:, :, :]).then_inc(stored[b], 16)

                early(0)
                messages(0)
                late(0)
                early(1)
                with sp.Fori(1, iters - 1) as i:
                    messages(i)
                    early(i + 1)
                    stores(i - 1)
                    late(i)
                messages(iters - 1)
                stores(iters - 2)
                late(iters - 1)
                stores(iters - 1)
                for b in range(PLACES):
                    sp.wait_ge(stored[b], 16 * iters)

            @block.vector
            def _(dve):
                dve.memset(den[-1][:, :], 0.0)
                dve.memset(gm[-1][:, :, :], 0.0)
                dve.memset(gr[-1][:, :, :], 0.0).then_inc(start, 1)
                dve.wait_ge(start, 1)
                def sums(i):
                    n = i + 1
                    for b in range(PLACES):
                        free(dve, g_done[b], i)
                        dve.wait_ge(in_[b], 64 * n)
                        row = runs.row[b]
                        dve.tensor_tensor(same[b][:, :], row[0:4, 1:K * P + 1], row[0:4, 0:K * P],
                                          ALU.is_equal).then_inc(same_done[b], 1)
                        runs.matrices(dve, b, eint[b][:, :, 1:2])
                    for b in range(PLACES):
                        dve.wait_ge(same_done[b], n)
                        if b:
                            dve.wait_ge(den_done[b - 1], n)
                        else:
                            free(dve, den_done[-1], i)
                        dve.tensor_tensor_scan(den[b][:, :], same[b][:, :], bs[b][:, :], den[b - 1][:, K * P - 1:K * P],
                                               ALU.mult, ALU.max).then_inc(den_done[b], 1)

                def messages(i):
                    n = i + 1
                    for b in range(PLACES):
                        dve.wait_ge(al_done[b], n)
                        dve.tensor_scalar(de2[b][:, :, :], b_al[b % 2][:, 8:16].rearrange("p (k h) -> p k h", k=K),
                                          1e-16, None, ALU.add).then_inc(de2_done[b], 1)
                        dve.wait_ge(de2_done[b], n)
                        dve.reciprocal(rden[b][:, :, :], de2[b][:, :, :]).then_inc(rden_done[b], 1)
                        dve.wait_ge(rden_done[b], n)
                        dve.tensor_tensor(alpha[b][:, :, :], b_al[b % 2][:, 0:8].rearrange("p (k h) -> p k h", k=K),
                                          rden[b][:, :, :], ALU.mult).then_inc(alpha_done[b], 1)
                    for b in range(PLACES):
                        dve.wait_ge(alpha_done[b], n)
                        dve.wait_ge(h_in[b], 16 * n)
                        al = alpha[b][:, :, :]
                        dve.tensor_tensor(ha[b][:, :, 0:CS].rearrange("p k (h u) -> p k h u", h=4),
                                          h[b][:, :, 0:CS].rearrange("p k (h u) -> p k h u", h=4),
                                          al.unsqueeze(3).to_broadcast([P, K, 4, 16]), ALU.mult)
                        for k in range(K):
                            ins = dve.tensor_tensor(ha[b][:, k, CS:C].rearrange("p (c h u) -> p c h u", c=3, h=4),
                                                    h[b][:, k, CS:C].rearrange("p (c h u) -> p c h u", c=3, h=4),
                                                    al[:, k, :].unsqueeze(1).unsqueeze(3).to_broadcast([P, 3, 4, 8]), ALU.mult)
                        ins.then_inc(ha_done[b], 1)
                    for b in range(PLACES):
                        dve.wait_ge(seg_done[b], n)
                        for k in range(K):
                            if k:
                                dve.wait_ge(g_half[b], n)
                            elif b:
                                dve.wait_ge(g_done[b - 1], n)
                            else:
                                free(dve, g_done[-1], i)
                            pb, pk = (b, 0) if k else (b - 1, K - 1)
                            dve.scalar_tensor_tensor(gm[b][:, k, :], runs.ind[b][:, k, :], gm[pb][:, pk, P - 1:P],
                                                     b_s[b % 2][:, k, 0:P], ALU.mult, ALU.add)
                            dve.scalar_tensor_tensor(gr[b][:, k, :], runs.ind[b][0:CV, k, :], gr[pb][:, pk, P - 1:P],
                                                     b_s[b % 2][0:CV, k, P:2 * P], ALU.mult,
                                                     ALU.add).then_inc((g_done if k else g_half)[b], 1)

                def update(i):
                    n = i + 1
                    for b in range(PLACES):
                        dve.wait_ge(y_done[b], n)
                        dve.wait_ge(x_in[b], 16 * n)
                        dve.scalar_tensor_tensor(pre[b][:, :, 0:CS], x0[b][:, :, 0:CS], 2.0, b_y[b % 2][:, :, 0:CS],
                                                 ALU.mult, ALU.add)
                        for k in range(K):
                            ins = dve.scalar_tensor_tensor(pre[b][:, k, CS:C].rearrange("p (c u) -> p c u", c=3),
                                                           cm(x0[b][:, k, CS:C]), 2.0,
                                                           b_y[b % 2][:, k, CS:C].rearrange("p (c u) -> p c u", c=3),
                                                           ALU.mult, ALU.add)
                        ins.then_inc(pre_done[b], 1)
                    norm.vector(dve, n, pre, pre_done)
                    for b in range(PLACES):
                        free(dve, stored[b], 16 * i)
                        dve.tensor_copy(x1[b][:, :, C:C + 1], x0[b][:, :, C:C + 1])
                        dve.tensor_tensor(x1[b][:, :, C + 1:C + 2], x0[b][:, :, C:C + 1], x0[b][:, :, C:C + 1],
                                          ALU.mult).then_inc(x1_v[b], 1)

                staged(dve, iters, sums, update, messages)

            @block.scalar
            def _(act):
                def body(i):
                    norm.scalar_roots(act, i + 1, w["eps"][:, 0:1])
                    for b in range(PLACES):
                        act.wait_ge(norm.nbd[b], i + 1)
                        free(act, stored[b], 16 * i)
                        for k in range(K):
                            ins = norm.scalar_apply(act, b, k, x1[b][:, k, 0:C], pre[b][:, k, :])
                        ins.then_inc(x1_s[b], 1)

                body(0)
                with act.Fori(1, iters) as i:
                    body(i)

            @block.tensor
            def _(pe):
                def body(i):
                    n = i + 1
                    for b in range(PLACES):
                        if b >= 2:
                            pe.wait_ge(alpha_done[b - 2], n)
                        apart(pe, den_done[b], n, passed)
                        for k in range(K):
                            s = slice(k * P, (k + 1) * P)
                            pe.transpose(b_al[b % 2][:, 4 * k:4 * k + 4], ex[b][:, s], w["ident"][0:4, 0:4])
                            ins = pe.transpose(b_al[b % 2][:, 8 + 4 * k:8 + 4 * k + 4], den[b][:, s], w["ident"][0:4, 0:4])
                        ins.then_inc(al_done[b], 1)
                    for b in range(PLACES):
                        pe.wait_ge(ha_done[b], n)
                        pe.wait_ge(runs.done[b], n)
                        if b >= 2:
                            pe.wait_ge(g_done[b - 2], n)
                        for k in range(K):
                            pe.matmul(b_s[b % 2][:, k, 0:P], ha[b][:, k, 0:P], runs.eq[b][:, k, :], start=True, stop=True)
                            ins = pe.matmul(b_s[b % 2][0:CV, k, P:2 * P], ha[b][:, k, P:C], runs.eq[b][:, k, :],
                                            start=True, stop=True)
                        ins.then_inc(seg_done[b], 1)
                    for b in range(PLACES):
                        pe.wait_ge(g_done[b], n)
                        if b >= 2:
                            pe.wait_ge(pre_done[b - 2], n)
                        else:
                            free(pe, pre_done[b - 2], i)
                        for k in range(K):
                            pe.matmul(b_y[b % 2][:, k, 0:P], gm[b][:, k, :], w["out0_m"][:, :], start=True, stop=True)
                            ins = pe.matmul(b_y[b % 2][:, k, P:C], gr[b][:, k, :], w["out0_r"][:, :], start=True, stop=True)
                        ins.then_inc(y_done[b], 1)

                body(0)
                with pe.Fori(1, iters) as i:
                    body(i)


def source_rows(pool, d, l, b, xs, meta, sem, top):
    for k in range(PAIR):
        pool.indirect_dma_start(xs[b][:, k, :], None, d[f"D{l}"],
                                bass.IndirectOffsetOnAxis(ap=meta[b][:, k, M_REP:M_REP + 1].bitcast(I32), axis=0),
                                bounds_check=top, oob_is_err=False).then_inc(sem[b], 16)


def conv(nc, w, d, l):
    NT, E_pad = d["NT"], d["E_pad"]
    iters, K = NT // BODY, PAIR
    FIN = 8 if l == 1 else 16
    S3, S64 = [P, K, 3, CV], [P, K, 3, CS]
    with phase(nc) as ctx:
        A = Alloc(nc, ctx, f"l{l}", PLACES)
        xs, meta, attr = A.sbs("xs", [P, K, ROW]), A.sbs("meta", [P, K, MW]), A.sbs("attr", [FIN, K * P])
        slot = A.sbs("slot", [P, K, MW])
        xd = A.sbs("xd", [P, K, ROW])
        sm, sr = A.sbs("sm", [P, K * P]), A.sbs("sr", [CV, K * P])
        dm, dr = A.sbs("dm", [P, K * P]), A.sbs("dr", [CV, K * P])
        g1, g2, we = A.sbs("g1", [64, K * P]), A.sbs("g2", [64, K * P]), A.sbs("we", [P, K, 192])
        p1, p2, q, dt = A.sbs("p1", [P, K, 128]), A.sbs("p2", [P, K, 96]), A.sbs("q", [P, K, 96]), A.sbs("dt", [P, K, CV])
        M1 = W96 + 1
        mid = A.sbs("mid", [P, K, M1 + 3 * W96])
        g = A.sbs("g", [M1, K, 512])
        cn, rc, rc2, ta, qq = (A.sbs(n, [P, K]) for n in ("cn", "rc", "rc2", "ta", "qq"))
        s1, pre, xo = A.sbs("s1", [P, K, C]), A.sbs("pre", [P, K, C]), A.sbs("xo", [P, K, ROW])
        runs, norm = Runs(A), Norm(A)
        bank = [A.ps(f"bank{k}", [P, 512]) for k in range(8)]
        halves = [t[:, :].rearrange("p (k e) -> p k e", k=K) for t in bank]
        b_t, b_d, b_h = (bank[0], bank[6]), (bank[0], bank[4]), (bank[1], bank[7])
        b_f, b_w = (halves[2], halves[6]), (halves[3], halves[7])
        b_s, b_y, b_c = ((bank[4], bank[5]), (bank[2], bank[3])), (halves[6], halves[2]), (halves[7], halves[3])
        in_, src_in, row_in, xd_in, stored = A.sems("in"), A.sems("src_in"), A.sems("row_in"), A.sems("xd_in"), A.sems("stored")
        hid1, act1, hid2, act2, w_done, w_out = (A.sems(n) for n in ("hid1", "act1", "hid2", "act2", "w_done", "w_out"))
        s_turned, s_out, f_done, f_used, mid_a, mid_ready = (
            A.sems(n) for n in ("s_turned", "s_out", "f_done", "f_used", "mid_a", "mid_ready"))
        seg_done, g_half, g_done, c_done = (A.sems(n) for n in ("seg", "g_half", "g_done", "c_done"))
        d_turned, d_out, y_done, s1_done, pre_done, xo_s, xo_v = (
            A.sems(n) for n in ("d_turned", "d_out", "y_done", "s1", "pre", "xo_s", "xo_v"))
        q_sem, start, passed = A.sems("q_sem"), A.sem("start"), A.sem("passed")

        def pos(i, b):
            return (PLACES * i + b) * K * P

        with nc.Block() as block:
            @block.sync
            def _(sp):
                def source_loads(i):
                    for b in range(PLACES):
                        free(sp, s_turned[b], i)
                        free(sp, hid1[b], i)
                        at = pos(i, b)
                        sp.dma_start(slot[b][:, :, :], tiles_of(d["meta"], at, K)).then_inc(src_in[b], 16)
                        sp.dma_start(xs[b][:, :, 0:C], tiles_of(d[f"B{l}"], at, K)).then_inc(src_in[b], 16)
                        sp.dma_start(attr[b][:, :], d["attr8" if l == 1 else "attr16"][0:FIN, bass.ds(at, K * P)]).then_inc(src_in[b], 16)

                def edge_loads(i):
                    for b in range(PLACES):
                        free(sp, seg_done[b], i)
                        free(sp, g_done[b], i)
                        at = pos(i, b)
                        sp.dma_start(meta[b][:, :, :], tiles_of(d["meta"], at, K)).then_inc(in_[b], 16)
                        runs.load(sp, d, at, b, in_[b])

                def late(i):
                    for b in range(PLACES):
                        free(sp, xo_v[b], i)
                        sp.dma_start(xd[b][:, :, :], tiles_of(d[f"D{l}"], pos(i, b), K)).then_inc(xd_in[b], 16)

                def stores(i):
                    for b in range(PLACES):
                        ready(sp, xo_s, i, b)
                        ready(sp, xo_v, i, b)
                        sp.dma_start(tiles_of(d[f"D{l + 1}"], pos(i, b), K), xo[b][:, :, :]).then_inc(stored[b], 16)

                source_loads(0)
                edge_loads(0)
                late(0)
                source_loads(1)
                with sp.Fori(1, iters - 1) as i:
                    edge_loads(i)
                    source_loads(i + 1)
                    stores(i - 1)
                    late(i)
                edge_loads(iters - 1)
                stores(iters - 2)
                late(iters - 1)
                stores(iters - 1)
                for b in range(PLACES):
                    sp.wait_ge(stored[b], 16 * iters)

            @block.gpsimd
            def _(pool):
                top = pool.to_reg(E_pad - 1)
                def body(i):
                    for b in range(PLACES):
                        apart(pool, src_in[b], 48 * i + 48, passed)
                        source_rows(pool, d, l, b, xs, slot, row_in, top)

                body(0)
                with pool.Fori(1, iters) as i:
                    body(i)

            @block.vector
            def _(dve):
                for b in range(PLACES):
                    dve.memset(mid[b][:, :, W96:M1], 1.0)
                dve.memset(g[-1][:, :, :], 0.0).then_inc(start, 1)
                dve.wait_ge(start, 1)
                def matrices(i):
                    n = i + 1
                    for b in range(PLACES):
                        dve.wait_ge(in_[b], 32 * n)
                        runs.matrices(dve, b, meta[b][:, :, M_DST:M_DST + 1].bitcast(I32))

                def messages(i):
                    n = i + 1
                    for b in range(PLACES):
                        y, F, W = meta[b], b_f[b % 2], we[b]
                        y0, yx = y[:, :, M_YA:M_YA + 1], y[:, :, M_YA + 1:M_YA + 4]
                        gv = F[:, :, CS:C].rearrange("p k (c u) -> p k c u", c=3)
                        dve.wait_ge(f_done[b], n)
                        dve.wait_ge(w_out[b], n)
                        dve.tensor_tensor(p1[b][:, :, :].rearrange("p k (a u) -> p k a u", a=2),
                                          W[:, :, 0:128].rearrange("p k (a u) -> p k a u", a=2),
                                          F[:, :, 0:CS].unsqueeze(2).to_broadcast([P, K, 2, CS]), ALU.mult)
                        dve.tensor_tensor(vecs(p2[b][:, :, :]), gv, W[:, :, 128:160].unsqueeze(2).to_broadcast(S3), ALU.mult)
                        dve.tensor_tensor(vecs(q[b][:, :, :]), gv, yx.unsqueeze(3).to_broadcast(S3), ALU.mult).then_inc(f_used[b], 1)
                        dve.wait_ge(f_used[b], n)
                        mx = mid[b][:, :, M1:].rearrange("p k (c u) -> p k c u", c=3)
                        dve.tensor_reduce(dt[b][:, :, :], q[b][:, :, :].rearrange("p k (c u) -> p k u c", c=3),
                                          AX.X, ALU.add).then_inc(mid_a[b], 1)
                        dve.tensor_tensor(mid[b][:, :, 0:CS], p1[b][:, :, 0:CS], y0.to_broadcast([P, K, CS]), ALU.mult)
                        dve.tensor_tensor(mx[:, :, :, 0:CS], p1[b][:, :, 64:128].unsqueeze(2).to_broadcast(S64),
                                          yx.unsqueeze(3).to_broadcast(S64), ALU.mult)
                        dve.tensor_tensor(mx[:, :, :, CS:W96], vecs(p2[b][:, :, :]), y0.unsqueeze(3).to_broadcast(S3), ALU.mult)
                        dve.wait_ge(mid_a[b], n)
                        dve.tensor_tensor(mid[b][:, :, CS:W96], W[:, :, 160:192], dt[b][:, :, :], ALU.mult).then_inc(mid_ready[b], 1)
                    for b in range(PLACES):
                        dve.wait_ge(seg_done[b], n)
                        for k in range(K):
                            if k:
                                dve.wait_ge(g_half[b], n)
                            elif b:
                                dve.wait_ge(g_done[b - 1], n)
                            else:
                                free(dve, g_done[-1], i)
                            pb, pk = (b, 0) if k else (b - 1, K - 1)
                            for c in range(4):
                                R = M1 if c == 0 else W96
                                ins = dve.scalar_tensor_tensor(
                                    g[b][0:R, k, P * c:P * (c + 1)], runs.ind[b][0:R, k, :],
                                    g[pb][0:R, pk, P * (c + 1) - 1:P * (c + 1)], b_s[b % 2][k][0:R, P * c:P * (c + 1)],
                                    ALU.mult, ALU.add)
                            ins.then_inc((g_done if k else g_half)[b], 1)

                def update(i):
                    n = i + 1
                    for b in range(PLACES):
                        x = xd[b]
                        dve.wait_ge(xd_in[b], 16 * n)
                        dve.wait_ge(c_done[b], n)
                        dve.tensor_tensor(ta[b][:, :], b_c[b % 2][:, :, 0], x[:, :, C + 1], ALU.mult)
                        dve.tensor_scalar(cn[b][:, :], b_c[b % 2][:, :, 1], 1.0, None, ALU.max).then_inc(q_sem[b], 1)
                        if l == 2:
                            dve.wait_ge(q_sem[b], 4 * i + 1)
                            dve.reciprocal(rc[b][:, :], cn[b][:, :]).then_inc(q_sem[b], 1)
                            dve.wait_ge(q_sem[b], 4 * i + 2)
                            dve.tensor_tensor(rc2[b][:, :], rc[b][:, :], rc[b][:, :], ALU.mult).then_inc(q_sem[b], 1)
                            dve.wait_ge(q_sem[b], 4 * i + 3)
                            dve.tensor_tensor(qq[b][:, :], ta[b][:, :], rc2[b][:, :], ALU.mult).then_inc(q_sem[b], 1)
                        dve.wait_ge(y_done[b], n)
                        for k in range(K):
                            ins = dve.scalar_tensor_tensor(s1[b][:, k, :], b_y[b % 2][:, k, 0:C], x[:, k, C:C + 1],
                                                           x[:, k, 0:C], ALU.mult, ALU.add)
                        ins.then_inc(s1_done[b], 1)
                        dve.wait_ge(s1_done[b], n)
                        f = qq if l == 2 else ta
                        for k in range(K):
                            ins = dve.scalar_tensor_tensor(pre[b][:, k, :], b_c[b % 2][:, k, 2:2 + C], f[b][:, k:k + 1],
                                                           s1[b][:, k, :], ALU.mult, ALU.add)
                        ins.then_inc(pre_done[b], 1)
                    norm.vector(dve, n, pre, pre_done)
                    for b in range(PLACES):
                        free(dve, stored[b], 16 * i)
                        dve.tensor_copy(xo[b][:, :, C:ROW], xd[b][:, :, C:ROW]).then_inc(xo_v[b], 1)

                staged(dve, iters, matrices, update, messages)

            @block.scalar
            def _(act):
                def hidden(i):
                    n = i + 1
                    for group in ((0, 1), (2, 3)):
                        for b in group:
                            act.wait_ge(hid1[b], n)
                            act.activation(g1[b][:, :], b_h[b % 2][0:64, 0:K * P], ACT.Gelu_apprx_tanh if l == 1 else ACT.Silu,
                                           scale=float(FIN) ** -0.5).then_inc(act1[b], 1)
                        for b in group:
                            act.wait_ge(s_turned[b], n)
                            act.activation(sm[b][:, :], b_t[b % 2][:, 0:K * P], ACT.Copy)
                            act.activation(sr[b][:, :], b_t[b % 2][0:CV, K * P:2 * K * P], ACT.Copy).then_inc(s_out[b], 1)
                            if l == 1:
                                act.wait_ge(hid2[b], n)
                                act.activation(g2[b][:, :], b_h[b % 2][0:64, 0:K * P], ACT.Gelu_apprx_tanh,
                                               scale=0.125).then_inc(act2[b], 1)

                def weights(i):
                    n = i + 1
                    for b in range(PLACES):
                        act.wait_ge(w_done[b], n)
                        act.activation(we[b][:, :, :], b_w[b % 2][:, :, 0:192], ACT.Copy, scale=0.125).then_inc(w_out[b], 1)
                    for b in range(PLACES):
                        act.wait_ge(d_turned[b], n)
                        act.activation(dm[b][:, :], b_d[b % 2][:, 0:K * P], ACT.Copy)
                        act.activation(dr[b][:, :], b_d[b % 2][0:CV, K * P:2 * K * P], ACT.Copy).then_inc(d_out[b], 1)

                def results(i):
                    n = i + 1
                    norm.scalar_roots(act, n, w["eps"][:, 0:1])
                    for b in range(PLACES):
                        act.wait_ge(norm.nbd[b], n)
                        free(act, stored[b], 16 * i)
                        for k in range(K):
                            ins = norm.scalar_apply(act, b, k, xo[b][:, k, 0:C], pre[b][:, k, :])
                        ins.then_inc(xo_s[b], 1)

                staged(act, iters, hidden, results, weights)

            @block.tensor
            def _(pe):
                ident = w["ident"]
                act_last = act2 if l == 1 else act1

                def turn(rows, bank_):
                    for k in range(K):
                        s = slice(k * P, (k + 1) * P)
                        pe.transpose(bank_[:, s], rows[:, k, 0:P], ident[:, :])
                        ins = pe.transpose(bank_[0:CV, K * P + k * P:K * P + (k + 1) * P], rows[:, k, P:C], ident[:, :])
                    return ins

                def hidden(i):
                    n = i + 1
                    for group in ((0, 1), (2, 3)):
                        for b in group:
                            pe.wait_ge(src_in[b], 48 * n)
                            if b >= 2:
                                pe.wait_ge(act_last[b - 2], n)
                            pe.matmul(b_h[b % 2][0:64, 0:K * P], w[f"fc{l}_1"][:, :], attr[b][:, :], start=True, stop=True).then_inc(hid1[b], 1)
                        for b in group:
                            pe.wait_ge(row_in[b], 32 * n)
                            if b >= 2:
                                pe.wait_ge(s_out[b - 2], n)
                            turn(xs[b], b_t[b % 2]).then_inc(s_turned[b], 1)
                            if l == 1:
                                apart(pe, act1[b], n, passed)
                                pe.matmul(b_h[b % 2][0:64, 0:K * P], w["fc1_2"][:, :], g1[b][:, :], start=True, stop=True).then_inc(hid2[b], 1)

                def messages(i):
                    n = i + 1
                    for b in range(PLACES):
                        hid = g2 if l == 1 else g1
                        pe.wait_ge(act_last[b], n)
                        if b >= 2:
                            pe.wait_ge(w_out[b - 2], n)
                        elif b:
                            pe.wait_ge(act_last[-1], n)
                            pe.wait_ge(s_out[-1], n)
                        else:
                            free(pe, pre_done[-1], i)
                        for k in range(K):
                            ins = pe.matmul(b_w[b % 2][:, k, 0:192], hid[b][:, k * P:(k + 1) * P], w[f"fc{l}_3"][:, :], start=True, stop=True)
                        ins.then_inc(w_done[b], 1)
                        pe.wait_ge(s_out[b], n)
                        if b >= 2:
                            pe.wait_ge(f_used[b - 2], n)
                        for k in range(K):
                            s = slice(k * P, (k + 1) * P)
                            pe.matmul(b_f[b % 2][:, k, 0:P], sm[b][:, s], w[f"f{l}_m"][:, :], start=True, stop=True)
                            ins = pe.matmul(b_f[b % 2][:, k, P:C], sr[b][:, s], w[f"f{l}_r"][:, :], start=True, stop=True)
                        ins.then_inc(f_done[b], 1)
                    for b in range(PLACES):
                        pe.wait_ge(xd_in[b], 16 * n)
                        if b >= 2:
                            pe.wait_ge(d_out[b - 2], n)
                        turn(xd[b], b_d[b % 2]).then_inc(d_turned[b], 1)
                    for b in range(PLACES):
                        pe.wait_ge(mid_ready[b], n)
                        pe.wait_ge(runs.done[b], n)
                        if b >= 2:
                            pe.wait_ge(g_done[b - 2], n)
                        elif b:
                            pe.wait_ge(f_used[-1], n)
                            pe.wait_ge(w_out[-1], n)
                        else:
                            pe.wait_ge(d_out[-1], n)
                        for k in range(K):
                            pe.matmul(b_s[b % 2][k][0:M1, 0:P], mid[b][:, k, 0:M1], runs.eq[b][:, k, :], start=True, stop=True)
                            for c in range(3):
                                ins = pe.matmul(b_s[b % 2][k][0:W96, P * (c + 1):P * (c + 2)],
                                                mid[b][:, k, M1 + W96 * c:M1 + W96 * (c + 1)], runs.eq[b][:, k, :],
                                                start=True, stop=True)
                        ins.then_inc(seg_done[b], 1)

                def update(i, fronts=None):
                    n = i + 1
                    fronts = i + 2 if fronts is None else fronts
                    for b in range(PLACES):
                        pe.wait_ge(d_out[b], n)
                        if b >= 2:
                            pe.wait_ge(pre_done[b - 2], n)
                        elif b:
                            pe.wait_ge(g_done[-1], n)
                        else:
                            pe.wait_ge(s_out[-1], fronts)
                            pe.wait_ge(act_last[-1], fronts)
                        for k in range(K):
                            s = slice(k * P, (k + 1) * P)
                            pe.matmul(b_y[b % 2][:, k, 0:P], dm[b][:, s], w[f"sc{l}_m"][:, :], start=True, stop=True)
                            ins = pe.matmul(b_y[b % 2][:, k, P:C], dr[b][:, s], w[f"sc{l}_r"][:, :], start=True, stop=True)
                        ins.then_inc(y_done[b], 1)
                        pe.wait_ge(g_done[b], n)
                        for k in range(K):
                            pe.matmul(b_c[b % 2][:, k, 0:2 + CS], g[b][:, k, 0:P], w[f"oa{l}"][:, :], start=True, stop=True)
                            for c in range(3):
                                ins = pe.matmul(b_c[b % 2][:, k, 2 + CS + CV * c:2 + CS + CV * (c + 1)],
                                                g[b][0:W96, k, P * (c + 1):P * (c + 2)], w[f"ov{l}"][:, :],
                                                start=True, stop=True)
                        ins.then_inc(c_done[b], 1)

                staged(pe, iters, hidden, update, messages, last_tail=lambda i: update(i, iters))


def conv3(nc, w, d):
    NT, E_pad, N = d["NT"], d["E_pad"], d["xa"].shape[0]
    iters, K = NT // BODY, PAIR
    S3, S64 = [P, K, 3, CV], [P, K, 3, CS]
    with phase(nc) as ctx:
        A = Alloc(nc, ctx, "l3", PLACES)
        xs, meta, attr = A.sbs("xs", [P, K, ROW]), A.sbs("meta", [P, K, MW]), A.sbs("attr", [17, K * P])
        slot = A.sbs("slot", [P, K, MW])
        xd, last = A.sbs("xd", [P, K, ROW]), A.sbs("last", [P, K, MW])
        sm, sr = A.sbs("sm", [P, K * P]), A.sbs("sr", [CV, K * P])
        dm, dr = A.sbs("dm", [P, K * P]), A.sbs("dr", [CV, K * P])
        gate = A.sbs("gate", [P, K, C])
        h1, hq, hs, qv = A.sbs("h1", [P, K, CS]), A.sbs("hq", [P, K, CS]), A.sbs("hs", [P, K, CS]), A.sbs("qv", [P, K, 192])
        c1, p1, c2 = A.sbs("c1", [P, K, 96]), A.sbs("p1", [P, K, 96]), A.sbs("c2", [P, K, 96])
        mid, gm, gr = A.sbs("mid", [P, K, C]), A.sbs("gm", [P, K, P]), A.sbs("gr", [CV, K, P])
        pre, xo = A.sbs("pre", [P, K, C]), A.sbs("xo", [P, K, C])
        runs, norm = Runs(A), Norm(A)
        banks = A.ps("banks", [P, 8, 512])
        half = [banks[:, k, :].rearrange("p (k e) -> p k e", k=K) for k in range(8)]
        b_t, b_g, b_f = (banks[:, 0, :], banks[:, 2, :]), (half[1], half[3]), (banks[:, 2:4, :], banks[:, 6:8, :])
        b_d = banks[:, 0, :], banks[:, 1, :]
        b_s, b_y = (half[4], half[5]), (half[6], half[7])
        in_, src_in, row_in, xd_in, stored = A.sems("in"), A.sems("src_in"), A.sems("row_in"), A.sems("xd_in"), A.sems("stored")
        s_turned, s_out, f_done, f_used, gt_done, gt_out = (
            A.sems(n) for n in ("s_turned", "s_out", "f_done", "f_used", "gt_done", "gt_out"))
        mid_a, mid_b, mid_ready = A.sems("mid_a"), A.sems("mid_b"), A.sems("mid_ready")
        seg_done, g_half, g_done = A.sems("seg"), A.sems("g_half"), A.sems("g_done")
        d_turned, d_out, y_done, pre_done, xo_done = (A.sems(n) for n in ("d_turned", "d_out", "y", "pre", "xo"))
        start, passed = A.sem("start"), A.sem("passed")

        def pos(i, b):
            return (PLACES * i + b) * K * P

        with nc.Block() as block:
            @block.sync
            def _(sp):
                def source_loads(i):
                    for b in range(PLACES):
                        free(sp, s_turned[b], i)
                        free(sp, gt_done[b], i)
                        at = pos(i, b)
                        sp.dma_start(slot[b][:, :, :], tiles_of(d["meta"], at, K)).then_inc(src_in[b], 16)
                        sp.dma_start(xs[b][:, :, 0:C], tiles_of(d["B3"], at, K)).then_inc(src_in[b], 16)
                        sp.dma_start(attr[b][:, :], d["attr16"][:, bass.ds(at, K * P)]).then_inc(src_in[b], 16)

                def edge_loads(i):
                    for b in range(PLACES):
                        free(sp, mid_ready[b], i)
                        free(sp, runs.done[b], i)
                        at = pos(i, b)
                        sp.dma_start(meta[b][:, :, :], tiles_of(d["meta"], at, K)).then_inc(in_[b], 16)
                        runs.load(sp, d, at, b, in_[b])

                def late(i):
                    for b in range(PLACES):
                        free(sp, stored[b], 32 * i)
                        free(sp, pre_done[b], i)
                        at = pos(i, b)
                        sp.dma_start(xd[b][:, :, :], tiles_of(d["D3"], at, K)).then_inc(xd_in[b], 16)
                        sp.dma_start(last[b][:, :, :], tiles_of(d["meta"], at, K)).then_inc(xd_in[b], 16)

                source_loads(0)
                edge_loads(0)
                late(0)
                source_loads(1)
                with sp.Fori(1, iters - 1) as i:
                    edge_loads(i)
                    source_loads(i + 1)
                    late(i)
                edge_loads(iters - 1)
                late(iters - 1)

            @block.gpsimd
            def _(pool):
                top, top_node = pool.to_reg(E_pad - 1), pool.to_reg(N - 1)

                def gathers(i):
                    for b in range(PLACES):
                        apart(pool, src_in[b], 48 * i + 48, passed)
                        source_rows(pool, d, 3, b, xs, slot, row_in, top)

                def scatters(i):
                    for b in range(PLACES):
                        pool.wait_ge(xd_in[b], 32 * i + 32)
                        apart(pool, xo_done[b], i + 1, passed)
                        for k in range(K):
                            pool.indirect_dma_start(
                                d["out"], bass.IndirectOffsetOnAxis(
                                    ap=last[b][:, k, M_LAST:M_LAST + 1].bitcast(I32), axis=0),
                                xo[b][:, k, :], None, bounds_check=top_node, oob_is_err=False).then_inc(stored[b], 16)

                gathers(0)
                with pool.Fori(1, iters) as i:
                    gathers(i)
                    scatters(i - 1)
                scatters(iters - 1)
                for b in range(PLACES):
                    pool.wait_ge(stored[b], 32 * iters)

            @block.vector
            def _(dve):
                dve.memset(gm[-1][:, :, :], 0.0)
                dve.memset(gr[-1][:, :, :], 0.0).then_inc(start, 1)
                dve.wait_ge(start, 1)
                def matrices(i):
                    n = i + 1
                    for b in range(PLACES):
                        free(dve, g_done[b], i)
                        dve.wait_ge(in_[b], 32 * n)
                        runs.matrices(dve, b, meta[b][:, :, M_DST:M_DST + 1].bitcast(I32))

                def messages(i):
                    n = i + 1
                    for b in range(PLACES):
                        y = meta[b]
                        y0, yx = y[:, :, M_Y:M_Y + 1], y[:, :, M_Y + 1:M_Y + 4].unsqueeze(3)
                        fx = b_f[b % 2][:, :, 96:384].rearrange("p k (c u) -> p k c u", c=3)
                        dve.wait_ge(f_done[b], n)
                        dve.tensor_tensor(h1[b][:, :, :], b_f[b % 2][:, :, 0:CS], y0.to_broadcast([P, K, CS]), ALU.mult)
                        dve.tensor_tensor(vecs(qv[b][:, :, :]), fx[:, :, :, 0:CS], yx.to_broadcast(S64), ALU.mult)
                        dve.tensor_tensor(vecs(c1[b][:, :, :]), b_f[b % 2][:, :, CS:W96].unsqueeze(2).to_broadcast(S3),
                                          yx.to_broadcast(S3), ALU.mult)
                        dve.tensor_tensor(vecs(p1[b][:, :, :]), fx[:, :, :, CS:W96],
                                          y0.unsqueeze(3).to_broadcast(S3), ALU.mult).then_inc(f_used[b], 1)
                        dve.wait_ge(f_used[b], n)
                        dve.tensor_reduce(hq[b][:, :, :], qv[b][:, :, :].rearrange("p k (c u) -> p k u c", c=3), AX.X, ALU.add)
                        dve.tensor_tensor(c2[b][:, :, :], c1[b][:, :, :], p1[b][:, :, :], ALU.add).then_inc(mid_a[b], 1)
                        dve.wait_ge(mid_a[b], n)
                        dve.wait_ge(gt_out[b], n)
                        dve.tensor_tensor(hs[b][:, :, :], h1[b][:, :, :], hq[b][:, :, :], ALU.add).then_inc(mid_b[b], 1)
                        dve.tensor_tensor(mid[b][:, :, CS:C], c2[b][:, :, :], gate[b][:, :, CS:C], ALU.mult)
                        dve.wait_ge(mid_b[b], n)
                        dve.tensor_tensor(mid[b][:, :, 0:CS], hs[b][:, :, :], gate[b][:, :, 0:CS], ALU.mult).then_inc(mid_ready[b], 1)
                    for b in range(PLACES):
                        dve.wait_ge(seg_done[b], n)
                        for k in range(K):
                            if k:
                                dve.wait_ge(g_half[b], n)
                            elif b:
                                dve.wait_ge(g_done[b - 1], n)
                            else:
                                free(dve, g_done[-1], i)
                            pb, pk = (b, 0) if k else (b - 1, K - 1)
                            dve.scalar_tensor_tensor(gm[b][:, k, :], runs.ind[b][:, k, :], gm[pb][:, pk, P - 1:P],
                                                     b_s[b % 2][:, k, 0:P], ALU.mult, ALU.add)
                            dve.scalar_tensor_tensor(gr[b][:, k, :], runs.ind[b][0:CV, k, :], gr[pb][:, pk, P - 1:P],
                                                     b_s[b % 2][0:CV, k, P:2 * P], ALU.mult,
                                                     ALU.add).then_inc((g_done if k else g_half)[b], 1)

                def update(i):
                    n = i + 1
                    for b in range(PLACES):
                        dve.wait_ge(y_done[b], n)
                        dve.wait_ge(xd_in[b], 32 * n)
                        dve.tensor_tensor(pre[b][:, :, :], b_y[b % 2][:, :, 0:C], xd[b][:, :, 0:C], ALU.add).then_inc(pre_done[b], 1)
                    norm.vector(dve, n, pre, pre_done)

                staged(dve, iters, matrices, update, messages)

            @block.scalar
            def _(act):
                def sources(i):
                    n = i + 1
                    for b in range(PLACES):
                        act.wait_ge(s_turned[b], n)
                        act.activation(sm[b][:, :], b_t[b % 2][:, 0:K * P], ACT.Copy)
                        act.activation(sr[b][:, :], b_t[b % 2][0:CV, K * P:2 * K * P], ACT.Copy).then_inc(s_out[b], 1)
                        act.wait_ge(gt_done[b], n)
                        act.activation(gate[b][:, :, :], b_g[b % 2][:, :, 0:C], ACT.Sigmoid).then_inc(gt_out[b], 1)

                def destinations(i):
                    n = i + 1
                    for b in range(PLACES):
                        act.wait_ge(d_turned[b], n)
                        act.activation(dm[b][:, :], b_d[b % 2][:, 0:K * P], ACT.Copy)
                        act.activation(dr[b][:, :], b_d[b % 2][0:CV, K * P:2 * K * P], ACT.Copy).then_inc(d_out[b], 1)

                def results(i):
                    n = i + 1
                    norm.scalar_roots(act, n, w["eps"][:, 0:1])
                    for b in range(PLACES):
                        act.wait_ge(norm.nbd[b], n)
                        free(act, stored[b], 32 * i)
                        for k in range(K):
                            norm.scalar_apply(act, b, k, xo[b][:, k, 0:CS], pre[b][:, k, 0:CS])
                            ins = norm.scalar_apply(act, b, k, cm(xo[b][:, k, CS:C]), vec(pre[b][:, k, CS:C]))
                        ins.then_inc(xo_done[b], 1)

                staged(act, iters, sources, results, destinations)

            @block.tensor
            def _(pe):
                ident = w["ident"]

                def turn(rows, b_t):
                    for k in range(K):
                        s = slice(k * P, (k + 1) * P)
                        pe.transpose(b_t[:, s], rows[:, k, 0:P], ident[:, :])
                        ins = pe.transpose(b_t[0:CV, K * P + k * P:K * P + (k + 1) * P], rows[:, k, P:C], ident[:, :])
                    return ins

                def body(i):
                    n = i + 1
                    for b in range(PLACES):
                        pe.wait_ge(src_in[b], 48 * n)
                        pe.wait_ge(row_in[b], 32 * n)
                        if b >= 2:
                            pe.wait_ge(s_out[b - 2], n)
                        turn(xs[b], b_t[b % 2]).then_inc(s_turned[b], 1)
                        if b >= 2:
                            pe.wait_ge(gt_out[b - 2], n)
                        for k in range(K):
                            ins = pe.matmul(b_g[b % 2][:, k, 0:C], attr[b][:, k * P:(k + 1) * P], w["rad"][:, :], start=True, stop=True)
                        ins.then_inc(gt_done[b], 1)
                    pe.wait_ge(gt_out[-1], n)
                    for b in range(PLACES):
                        pe.wait_ge(s_out[b], n)
                        if b >= 2:
                            pe.wait_ge(f_used[b - 2], n)
                        elif b:
                            free(pe, pre_done[-1], i)
                        for k in range(K):
                            s = slice(k * P, (k + 1) * P)
                            pe.matmul(b_f[b % 2][:, k, 0:288], sm[b][:, s], w["g_m"][:, :], start=True, stop=True)
                            ins = pe.matmul(b_f[b % 2][:, k, 288:384], sr[b][:, s], w["g_r"][:, :], start=True, stop=True)
                        ins.then_inc(f_done[b], 1)
                    for b in range(PLACES):
                        pe.wait_ge(xd_in[b], 32 * n)
                        if b >= 2:
                            pe.wait_ge(d_out[b - 2], n)
                        turn(xd[b], b_d[b % 2]).then_inc(d_turned[b], 1)
                    for b in range(PLACES):
                        pe.wait_ge(mid_ready[b], n)
                        pe.wait_ge(runs.done[b], n)
                        if b >= 2:
                            pe.wait_ge(g_done[b - 2], n)
                        for k in range(K):
                            pe.matmul(b_s[b % 2][:, k, 0:P], mid[b][:, k, 0:P], runs.eq[b][:, k, :], start=True, stop=True)
                            ins = pe.matmul(b_s[b % 2][0:CV, k, P:2 * P], mid[b][:, k, P:C], runs.eq[b][:, k, :],
                                            start=True, stop=True)
                        ins.then_inc(seg_done[b], 1)
                    for b in range(PLACES):
                        pe.wait_ge(d_out[b], n)
                        pe.wait_ge(g_done[b], n)
                        pe.wait_ge(*((pre_done[b - 2], n) if b >= 2 else (f_used[-1], n)))
                        for k in range(K):
                            s = slice(k * P, (k + 1) * P)
                            pe.matmul(b_y[b % 2][:, k, 0:P], dm[b][:, s], w["sc3_m"][:, :], start=True, stop=False)
                            pe.matmul(b_y[b % 2][:, k, 0:P], gm[b][:, k, :], w["sc3_m"][:, :], start=False, stop=True)
                            pe.matmul(b_y[b % 2][:, k, P:C], dr[b][:, s], w["sc3_r"][:, :], start=True, stop=False)
                            ins = pe.matmul(b_y[b % 2][:, k, P:C], gr[b][:, k, :], w["sc3_r"][:, :], start=False, stop=True)
                        ins.then_inc(y_done[b], 1)

                body(0)
                with pe.Fori(1, iters) as i:
                    body(i)



def build(nc, ins, out):
    d = dict(ins)
    d["out"] = out
    NT = d["ends"].shape[1]
    E_pad = NT * P
    N = d["xa"].shape[0]
    d["NT"], d["E_pad"] = NT, E_pad

    def table(name, shape, dt=F32):
        d[name] = nc.dram_tensor(name, shape, dt, kind="Internal").ap()

    table("slot", (N, 1), I32)
    table("meta", (E_pad, MW))
    table("B0", (E_pad, C + 1))
    for l in (1, 2, 3):
        table(f"B{l}", (E_pad, C))
    table("D0", (E_pad, C + 1))
    table("H0", (E_pad, C))
    for l in (1, 2, 3):
        table(f"D{l}", (E_pad, ROW))
    for n in ("A0", "R0", "X0", "S0"):
        table(n, (4, E_pad))
    with ExitStack() as ctx:
        w = load_weights(nc, ctx, d)
        chain(nc, w, d, "nodes", NODE_PLACES, -(-N // (NODE_PLACES * PAIR * P)), sources=False)
        chain(nc, w, d, "sources", PLACES, NT // BODY, sources=True)
        attend0(nc, w, d)
        soften0(nc, d)
        update0(nc, w, d)
        conv(nc, w, d, 1)
        conv(nc, w, d, 2)
        conv3(nc, w, d)


def layout(inputs):
    x = np.asarray(inputs["x"])
    N = x.shape[0]
    dst, src = np.asarray(inputs["dst"], np.int32), np.asarray(inputs["src"], np.int32)
    E = dst.shape[0]
    NT = -(-E // (BODY * P)) * BODY
    E_pad = NT * P

    def padded(a, fill):
        return np.concatenate([a, np.full((E_pad - E,) + a.shape[1:], fill, a.dtype)])

    def by_lane(a):
        return np.ascontiguousarray(a.reshape(NT, P, -1).transpose(1, 0, 2))

    d0, dp, sp = padded(dst, 0), padded(dst, N), padded(src, 0)
    nxt = np.concatenate([dp[1:], np.full(1, N + 1, np.int32)])
    a16, a8, a4 = (padded(np.asarray(inputs[k]), 0) for k in ("edge_attr_16", "edge_attr_8", "edge_attr_4"))
    order = np.concatenate([np.arange(CS), CS + np.arange(3 * CV).reshape(CV, 3).T.ravel()])
    out = {
        "xa": np.concatenate([x, np.asarray(inputs["node_vec1"])], 1),
        "ends": by_lane(np.stack([dp, nxt], 1)),
        "edge_ids": by_lane(np.repeat(np.arange(E_pad, dtype=np.int32)[:, None], 2, 1)),
        "eint": np.stack([sp, dp, nxt, d0], 1),
        "dst_row": np.concatenate([np.full(1, N + 1, np.int32), dp, np.full(1, N + 1, np.int32)])[None],
        "y": a4,
        "attr16": np.concatenate([a16.T, np.ones((1, E_pad), np.float32)]),
        "attr8": np.ascontiguousarray(a8.T),
        "ws_valT": np.ascontiguousarray(np.asarray(inputs["L0_gnn_Ws_val"]).T),
        "w_rad_ext": np.concatenate([np.asarray(inputs["L3_gnn_W_rad"]).T,
                                     np.asarray(inputs["L3_gnn_b_rad"])[None]])[:, order],
    }
    for k, v in inputs.items():
        if k.startswith("L") and k not in ("L3_gnn_W_rad", "L3_gnn_b_rad"):
            v = np.asarray(v)
            out[k] = v.reshape(-1) if k == "L0_gnn_alpha_dot" else v.reshape(v.shape[0], -1)
    return {k: np.ascontiguousarray(v) for k, v in out.items()}


def kernel(**inputs):
    import concourse.bacc as bacc
    from concourse.bass_utils import run_bass_kernel_spmd as run

    nc = bacc.Bacc("TRN2", target_bir_lowering=False, num_devices=1)
    arrays = {f"in_{k}": v for k, v in layout(inputs).items()}
    ins = {k[3:]: nc.dram_tensor(k, v.shape, mybir.dt.from_np(v.dtype), kind="ExternalInput").ap()
           for k, v in arrays.items()}
    N = arrays["in_xa"].shape[0]
    out = nc.dram_tensor("out_x", (N, C), F32, kind="ExternalOutput").ap()
    build(nc, ins, out)
    r = run(nc, [arrays], core_ids=[0])
    return r.results[0]["out_x"]
```

```python
from contextlib import ExitStack, contextmanager

import numpy as np

import concourse.bass as bass
from concourse import mybir

F32 = mybir.dt.float32
I32 = mybir.dt.int32
ALU = mybir.AluOpType
ACT = mybir.ActivationFunctionType
AX = mybir.AxisListType

P = 128
CS, CV = 64, 32
C = CS + 3 * CV
EPS = 1e-5
PAIR = 2
PLACES, NODE_PLACES = 4, 8
BODY = PLACES * PAIR
NEG = -1.0e30
ROW = C + 2
MW = 13
M_YA, M_Y, M_DST, M_REP, M_LAST = 0, 4, 10, 11, 12
W96 = CS + CV


def cm(ap):
    return ap.rearrange("p (u c) -> p c u", c=3)


@contextmanager
def phase(nc):
    with nc.cleanup_on_exit():
        with ExitStack() as ctx:
            yield ctx


class Alloc:

    def __init__(self, nc, ctx, name, places=2):
        self.nc, self.ctx, self.name, self.places = nc, ctx, name, places

    def sb(self, name, shape, dt=F32):
        return self.ctx.enter_context(self.nc.sbuf_tensor(f"{self.name}_{name}", shape, dt))

    def ps(self, name, shape):
        return self.ctx.enter_context(self.nc.psum_tensor(f"{self.name}_{name}", shape, F32))

    def sem(self, name):
        return self.nc.alloc_semaphore(name=f"{self.name}_{name}")

    def sems(self, name, n=None):
        return [self.sem(f"{name}{b}") for b in range(n or self.places)]

    def sbs(self, name, shape, dt=F32):
        return [self.sb(f"{name}{b}", shape, dt) for b in range(self.places)]


def free(eng, sem, value):
    if not (isinstance(value, int) and value == 0):
        eng.wait_ge(sem, value)


def staged(eng, iters, front, tail, mid, last_tail=None):
    front(0)
    mid(0)
    front(1)
    tail(0)
    mid(1)
    with eng.Fori(2, iters) as i:
        front(i)
        tail(i - 1)
        mid(i)
    (last_tail or tail)(iters - 1)


def ready(eng, sems, i, b):
    eng.wait_ge(sems[b], i + 1)


def apart(eng, sem, value, passed):
    eng.wait_ge(sem, value).then_inc(passed, 1)


def vec(ap):
    return ap.rearrange("p (c u) -> p c u", c=3)



class Tally:

    def __init__(self, sem, per):
        self.sem, self.per, self.n, self.i = sem, per, 0, 0

    def step(self, i):
        self.n, self.i = 0, i

    def done(self):
        assert self.n == self.per

    def add(self, ins, by):
        ins.then_inc(self.sem, by)
        self.n += by

    def wait(self, eng, passed):
        apart(eng, self.sem, self.i * self.per + self.n, passed)


def order_edges(nc, d):
    NT, E_pad, N = d["NT"], d["E_pad"], d["xa"].shape[0]
    given = {n: d["given_" + n] for n in ("eint", "ends", "dst_row", "y", "attr16", "attr8")}
    CHUNKS = PLACES * PAIR
    CH = E_pad // CHUNKS
    LOADS, OPS = 5, 4 + 2 * CHUNKS + 2
    MOVES, BACK = 16 * (LOADS + 5), 16 * 13
    with phase(nc) as ctx:
        A = Alloc(nc, ctx, "order")
        ends, gt, worst = A.sb("ends", [P, NT, 2], I32), A.sb("gt", [P, NT]), A.sb("worst", [P, 1])
        row, worst1, flag = A.sb("row", [1, P]), A.sb("worst1", [1, 1]), A.sb("flag", [1, 1], I32)
        keys, lower = A.sb("keys", [P, E_pad], I32), A.sb("lower", [P, CH])
        own, key, ahead, mixed = (A.sb(n, [P, P], I32) for n in ("own", "key", "ahead", "mixed"))
        tri, all_ones = A.sb("tri", [P, P]), A.sb("all_ones", [P, P])
        dst, dst2, rank = (A.sb(n, [P, 1], I32) for n in ("dst", "dst2", "rank"))
        part, rankf = A.sb("part", [P, CHUNKS]), A.sb("rankf", [P, 1])
        ri, ra, ry = A.sb("ri", [P, 2], I32), A.sb("ra", [P, 24]), A.sb("ry", [P, 4])
        nx, real, d0 = (A.sb(n, [P, 1], I32) for n in ("nx", "real", "d0"))
        copied, ends_in, compared, worst_out, flag_set, passed = (
            A.sem(n) for n in ("copied", "ends_in", "compared", "worst_out", "flag_set", "passed"))
        prepared, keys_set, tri_set, ranked_moves, ranked_ops, back_moves, back_ops = (
            A.sem(n) for n in ("prepared", "keys_set", "tri_set", "ranked_moves", "ranked_ops", "back_moves", "back_ops"))
        sorted_i, sorted_a, sorted_y = (
            nc.dram_tensor(n, s, t, kind="Internal").ap() for n, s, t in (
                ("sorted_i", (E_pad + 1, 2), I32), ("sorted_a", (E_pad, 24), F32), ("sorted_y", (E_pad, 4), F32)))

        with nc.Block() as block:
            @block.sync
            def _(sp):
                sp.dma_start(ends[:, :, :], given["ends"]).then_inc(ends_in, 16)
                for n in given:
                    to, from_ = d[n], given[n]
                    if n in ("eint", "y"):
                        to, from_ = (t.rearrange("(p k) c -> p (k c)", p=P) for t in (to, from_))
                    sp.dma_start(to, from_).then_inc(copied, 16)
                sp.wait_ge(compared, 2)
                sp.dma_start(row[0:1, :], worst[:, 0:1], allow_slow_non_contiguous=True).then_inc(worst_out, 16)
                sp.wait_ge(copied, 16 * len(given))

            @block.vector
            def _(dve):
                dve.wait_ge(ends_in, 16)
                dve.tensor_tensor(gt[:, :], ends[:, :, 0], ends[:, :, 1], ALU.is_gt).then_inc(compared, 1)
                dve.wait_ge(compared, 1)
                dve.tensor_reduce(worst[:, :], gt[:, :], AX.X, ALU.max).then_inc(compared, 1)
                dve.wait_ge(worst_out, 16)
                dve.tensor_reduce(worst1[:, :], row[:, :], AX.X, ALU.max).then_inc(compared, 1)
                dve.wait_ge(compared, 3)
                dve.tensor_copy(flag[:, :], worst1[:, :]).then_inc(flag_set, 1)
                dve.wait_ge(flag_set, 1)
                unordered = dve.value_load(flag[0:1, 0:1], min_val=0, max_val=1)
                with dve.If(unordered != 0):
                    dve.wait_ge(prepared, 32)
                    dve.wait_ge(tri_set, 2)
                    dve.tensor_scalar(keys[:, :], keys[:, :], 2.0, 1.0, ALU.mult, ALU.add).then_inc(keys_set, 1)
                    dve.wait_ge(keys_set, 1)
                    ops = Tally(ranked_ops, OPS)
                    with dve.Fori(0, NT) as t:
                        ops.step(t)
                        apart(dve, ranked_moves, t * MOVES + 16 * LOADS, passed)
                        ops.add(dve.tensor_scalar(key[:, :], own[:, :], 2.0, 1.0, ALU.mult, ALU.add), 1)
                        ops.add(dve.tensor_scalar(ahead[:, :], own[:, :], 2.0, None, ALU.mult), 1)
                        ops.add(dve.tensor_scalar(dst2[:, :], dst[:, :], 2.0, 1.0, ALU.mult, ALU.add), 1)
                        ops.wait(dve, passed)
                        ops.add(dve.tensor_tensor(mixed[:, :], key[:, :], tri[:, :], ALU.subtract), 1)
                        apart(dve, ranked_moves, t * MOVES + 16 * LOADS + 16, passed)
                        for c in range(CHUNKS):
                            ops.add(dve.tensor_tensor(lower[:, :], keys[:, c * CH:(c + 1) * CH],
                                                      dst2[:, :].to_broadcast([P, CH]), ALU.is_lt), 1)
                            ops.wait(dve, passed)
                            ops.add(dve.tensor_reduce(part[:, c:c + 1], lower[:, :], AX.X, ALU.add), 1)
                            ops.wait(dve, passed)
                        ops.add(dve.tensor_reduce(rankf[:, :], part[:, :], AX.X, ALU.add), 1)
                        ops.wait(dve, passed)
                        ops.add(dve.tensor_copy(rank[:, :], rankf[:, :]), 1)
                    ops.done()
                    ops = Tally(back_ops, 2)
                    with dve.Fori(0, NT) as t:
                        ops.step(t)
                        apart(dve, back_moves, t * BACK + 64, passed)
                        ops.add(dve.tensor_scalar(real[:, :], ri[:, 1:2], float(N), None, ALU.not_equal), 1)
                        ops.wait(dve, passed)
                        ops.add(dve.tensor_tensor(d0[:, :], ri[:, 1:2], real[:, :], ALU.mult), 1)
                    ops.done()

            @block.gpsimd
            def _(pool):
                pool.wait_ge(flag_set, 1)
                unordered = pool.value_load(flag[0:1, 0:1], min_val=0, max_val=1)
                with pool.If(unordered != 0):
                    pool.wait_ge(copied, 16 * len(given))
                    pool.dma_start(keys[:, :], given["dst_row"][0:1, 1:E_pad + 1].partition_broadcast(P)).then_inc(prepared, 16)
                    pool.dma_start(sorted_i[E_pad:E_pad + 1, 1:2], given["dst_row"][0:1, E_pad + 1:E_pad + 2],
                                   allow_slow_non_contiguous=True).then_inc(prepared, 16)
                    pool.memset(all_ones[:, :], 1.0).then_inc(tri_set, 1)
                    pool.wait_ge(tri_set, 1)
                    pool.affine_select(out=tri[:, :], in_=all_ones[:, :], compare_op=ALU.is_gt, fill=0.0, base=0,
                                       pattern=[[-1, P]], channel_multiplier=1).then_inc(tri_set, 1)
                    pool.wait_ge(keys_set, 1)

                    top = pool.to_reg(E_pad - 1)
                    moves = Tally(ranked_moves, MOVES)
                    with pool.Fori(0, NT) as t:
                        moves.step(t)
                        at = t * P
                        moves.add(pool.dma_start(own[:, :], given["dst_row"][0:1, bass.ds(at + 1, P)].partition_broadcast(P)), 16)
                        moves.add(pool.dma_start(dst[:, :].unsqueeze(1), given["ends"][:, bass.ds(t, 1), 0:1],
                                                 allow_slow_non_contiguous=True), 16)
                        moves.add(pool.dma_start(ri[:, :], given["eint"][bass.ds(at, P), 0:2]), 16)
                        moves.add(pool.dma_start(ra[:, :], d["attr_rows"][bass.ds(at, P), :]), 16)
                        moves.add(pool.dma_start(ry[:, :], given["y"][bass.ds(at, P), :]), 16)
                        apart(pool, ranked_ops, t * OPS + 4, passed)
                        moves.add(pool.dma_start(keys[:, bass.ds(at, P)], mixed[:, :]), 16)
                        apart(pool, ranked_ops, t * OPS + OPS, passed)
                        moves.add(pool.dma_start(keys[:, bass.ds(at, P)], ahead[:, :]), 16)
                        for table, rows in ((sorted_i, ri), (sorted_a, ra), (sorted_y, ry)):
                            moves.add(pool.indirect_dma_start(
                                table, bass.IndirectOffsetOnAxis(ap=rank[:, 0:1], axis=0), rows[:, :], None,
                                bounds_check=top, oob_is_err=False), 16)
                        moves.wait(pool, passed)
                    moves.done()
                    moves = Tally(back_moves, BACK)
                    with pool.Fori(0, NT) as t:
                        moves.step(t)
                        at = t * P
                        rows = bass.ds(at, P)
                        moves.add(pool.dma_start(ri[:, :], sorted_i[rows, :]), 16)
                        moves.add(pool.dma_start(nx[:, :], sorted_i[bass.ds(at + 1, P), 1:2], allow_slow_non_contiguous=True), 16)
                        moves.add(pool.dma_start(ra[:, :], sorted_a[rows, :]), 16)
                        moves.add(pool.dma_start(ry[:, :], sorted_y[rows, :]), 16)
                        moves.wait(pool, passed)
                        apart(pool, back_ops, t * 2 + 2, passed)

                        def store(to, rows_):
                            moves.add(pool.dma_start(to, rows_, allow_slow_non_contiguous=True), 16)

                        store(d["eint"][rows, 0:2], ri[:, :])
                        store(d["eint"][rows, 2:3], nx[:, :])
                        store(d["eint"][rows, 3:4], d0[:, :])
                        store(d["ends"][:, bass.ds(t, 1), 0:1], ri[:, 1:2].unsqueeze(1))
                        store(d["ends"][:, bass.ds(t, 1), 1:2], nx[:, :].unsqueeze(1))
                        store(d["dst_row"][0:1, bass.ds(at + 1, P)].rearrange("o (p q) -> p o q", q=1), ri[:, 1:2].unsqueeze(1))
                        store(d["y"][rows, :], ry[:, :])
                        store(d["attr16"][0:16, rows].rearrange("r (p o) -> p r o", o=1), ra[:, 0:16].rearrange("p (r o) -> p r o", o=1))
                        store(d["attr8"][:, rows].rearrange("r (p o) -> p r o", o=1), ra[:, 16:24].rearrange("p (r o) -> p r o", o=1))
                        moves.wait(pool, passed)
                    moves.done()



def load_weights(nc, ctx, d):
    A = Alloc(nc, ctx, "w")
    w = {}
    loads, scales, colscales = [], [], []

    def tile(name, shape):
        w[name] = A.sb(name, shape)
        return w[name]

    def block(name, ws, wv, fs, fv, back=False):
        m = tile(name + "_m", [P, P])
        r = tile(name + "_r", [2 * CV, 2 * CV])
        loads.append((m[0:CS, 0:CS], d[ws]))
        loads.append((m[64:96, 64:96], d[wv]))
        loads.append((m[96:128, 96:128], d[wv]))
        loads.append((r[0:CV, 0:CV], d[wv]))
        loads.append((r[CV:2 * CV, CV:2 * CV], d[wv]))
        scales.append((r[:, :], fv))
        scales.append((m[0:CS, 0:CS], fs))
        scales.append((m[64:128, 64:128], fv))
        if back:
            n = tile(name + "_b_m", [P, P])
            loads.append((n[0:CV, 0:CV], d[wv]))
            loads.append((n[CV:64, CV:64], d[wv]))
            loads.append((n[64:P, 64:P], d[ws]))
            scales.append((n[64:P, 64:P], fs))
            scales.append((n[0:64, 0:64], fv))

    i8, i32 = 1 / 8.0, 1 / np.sqrt(32.0)
    block("sc1", "L1_gnn_Wsc0", "L1_gnn_Wsc1", i8, i32, back=True)
    block("sc2", "L2_gnn_Wsc0", "L2_gnn_Wsc1", i8, i32, back=True)
    block("sc3", "L3_gnn_L_s", "L3_gnn_L_v", i8, i32, back=True)
    block("f1", "L1_gnn_Wl1_0", "L1_gnn_Wl1_1", i8, i32)
    block("f2", "L2_gnn_Wl1_0", "L2_gnn_Wl1_1", i8, i32)
    src_m = tile("src_m", [P, P])
    loads.append((src_m[0:CS, 0:CS], d["L0_gnn_Ws_src"]))
    loads.append((src_m[64:96, 64:96], d["L0_gnn_Wv_src"]))
    loads.append((src_m[96:128, 96:128], d["L0_gnn_Wv_src"]))
    dst_m = tile("dst_m", [P, P])
    loads.append((dst_m[0:32, 96:128], d["L0_gnn_Wv_dst"]))
    loads.append((dst_m[32:64, 64:96], d["L0_gnn_Wv_dst"]))
    loads.append((dst_m[64:128, 0:CS], d["L0_gnn_Ws_dst"]))
    ends_r = tile("ends_r", [2 * CV + 1, C])
    loads.append((ends_r[0:CV, P:C], d["L0_gnn_Wv_src"]))
    loads.append((ends_r[CV:2 * CV, P:C], d["L0_gnn_Wv_dst"]))
    block("out0", "L0_gnn_Wps", "L0_gnn_Wpv", 1.0, 1.0)

    def plain(name, src, rows, cols, f=1.0):
        t = tile(name, [rows, cols])
        loads.append((t[:, :], d[src]))
        if f != 1.0:
            scales.append((t[:, :], f))
        return t

    plain("fc1_1", "L1_gnn_Wfc1", 8, 64)
    plain("fc1_2", "L1_gnn_Wfc2", 64, 64)
    t = plain("fc1_3", "L1_gnn_Wfc3", 64, 192)
    scales.append((t[:, 160:192], 1 / np.sqrt(3.0)))
    plain("fc2_1", "L2_gnn_Wfc1", 16, 64)
    t = plain("fc2_3", "L2_gnn_Wfc2", 64, 192)
    scales.append((t[:, 160:192], 1 / np.sqrt(3.0)))
    for l, f in ((1, 1 / np.sqrt(32.0) / np.sqrt(96.0)), (2, 1 / np.sqrt(96.0))):
        plain(f"ov{l}", f"L{l}_gnn_Wl2_v", W96, CV, f)
        t = tile(f"oa{l}", [W96 + 1, 2 + CS])
        loads.append((t[0:W96, 0:1], d[f"L{l}_gnn_Wa"]))
        loads.append((t[0:W96, 2:2 + CS], d[f"L{l}_gnn_Wl2_s"]))
        scales.append((t[0:W96, 0:1], f))
        scales.append((t[0:W96, 2:2 + CS], f))
    plain("rbf", "L0_gnn_W_rbf", 16, 224)
    scales.append((w["rbf"][:, 160:192], 1 / np.sqrt(3.0)))
    scales.append((w["rbf"][:, 192:224], 1 / np.sqrt(2.0)))
    va = tile("va", [W96, 160])
    loads.append((va[:, 0:64], d["L0_gnn_Ws_val"]))
    loads.append((va[:, 64:128], d["L0_gnn_W_alpha"]))
    plain("valT", "ws_valT", 64, W96)
    plain("wg", "L0_gnn_Wg", 64, CV)
    plain("wvval", "L0_gnn_Wv_val", P, CV)
    adot = tile("adot", [P, 64])
    loads.append((adot[:, :], d["L0_gnn_alpha_dot"].partition_broadcast(P)))
    hm = tile("h_m", [P, 224])
    hr = tile("h_r", [64, 128])
    loads.append((hm[0:64, 0:64], d["L0_gnn_Ws_vlin"][0:64, :]))
    loads.append((hm[0:64, 64:96], d["L0_gnn_Wv_vlin"][0:64, :]))
    for g in range(2):
        loads.append((hm[64 + 32 * g:96 + 32 * g, 96 + 64 * g:128 + 64 * g], d["L0_gnn_Wv_vlin"][64:96, :]))
        loads.append((hm[64 + 32 * g:96 + 32 * g, 128 + 64 * g:160 + 64 * g], d["L0_gnn_Wv_vlin"][96:128, :]))
    loads.append((hr[0:32, 0:32], d["L0_gnn_Wv_vlin"][64:96, :]))
    loads.append((hr[0:32, 32:64], d["L0_gnn_Wv_vlin"][96:128, :]))
    loads.append((hr[32:64, 64:128], d["L0_gnn_Ws_vlin"][64:96, :]))
    cols = tile("cols", [P, 12])

    def col(c, at, src, n):
        loads.append((cols[at:at + n, c:c + 1], d[src]))

    col(0, 0, "L0_gnn_w2_ss", 64)
    col(1, 0, "L0_gnn_w2_sv", 64)
    for at in (64, 96):
        col(2, at, "L0_gnn_w2_vs", 32)
        col(3, at, "L0_gnn_w2_vv1", 32)
    col(4, 0, "L0_gnn_w2_vs", 32)
    col(5, 0, "L0_gnn_w2_vv1", 32)
    col(6, 32, "L0_gnn_w2_vv0", 32)
    col(7, 0, "L0_gnn_gamma_s", 64)
    col(7, 64, "L0_gnn_gamma_v", 32)
    col(7, 96, "L0_gnn_gamma_v", 32)
    col(8, 0, "L0_gnn_gamma_v", 32)
    col(8, 32, "L0_gnn_gamma_v", 32)
    col(8, 64, "L0_gnn_gamma_s", 64)
    col(9, 0, "L0_gnn_beta_s", 64)
    colscales += [(hm[0:64, 0:64], cols[0:64, 0:1], 1.0), (hm[0:64, 64:96], cols[0:64, 1:2], 1.0)]
    for g in range(2):
        a, b = 64 + 32 * g, 96 + 32 * g
        colscales.append((hm[a:b, 96 + 64 * g:128 + 64 * g], cols[a:b, 2:3], 1.0))
        colscales.append((hm[a:b, 128 + 64 * g:160 + 64 * g], cols[a:b, 3:4], 1 / np.sqrt(2.0)))
    colscales.append((hr[0:32, 0:32], cols[0:32, 4:5], 1.0))
    colscales.append((hr[0:32, 32:64], cols[0:32, 5:6], 1 / np.sqrt(2.0)))
    colscales.append((hr[32:64, 64:128], cols[32:64, 6:7], 1 / np.sqrt(3.0)))
    raw_src, raw_dst = plain("ws_src", "L0_gnn_Ws_src", 64, 64), plain("ws_dst", "L0_gnn_Ws_dst", 64, 64)
    colscales.append((w["src_m"][:, :], cols[:, 7:8], 1.0))
    colscales.append((dst_m[:, :], cols[:, 8:9], 1.0))
    colscales.append((ends_r[0:2 * CV, P:C], cols[0:2 * CV, 8:9], 1.0))
    g_m, g_r = tile("g_m", [P, 288]), tile("g_r", [CV, W96])
    i2, i3 = 1 / np.sqrt(2.0), 1 / np.sqrt(3.0)
    loads.append((g_m[0:64, 0:64], d["L3_gnn_W_ss"]))
    loads.append((g_m[0:64, 64:96], d["L3_gnn_W_sv"]))
    scales += [(g_m[0:64, 0:64], i2 * i8), (g_m[0:64, 64:96], i2 * i3 * i8)]
    for g in range(2):
        a, c = 64 + 32 * g, 96 * (g + 1)
        loads.append((g_m[a:a + 32, c:c + 64], d["L3_gnn_W_vv"]))
        loads.append((g_m[a:a + 32, c + 64:c + 96], d["L3_gnn_W_vs"]))
        scales.append((g_m[a:a + 32, c:c + 96], i2 * i3 * i32))
    loads.append((g_r[:, 0:64], d["L3_gnn_W_vv"]))
    loads.append((g_r[:, 64:96], d["L3_gnn_W_vs"]))
    scales.append((g_r[:, :], i2 * i3 * i32))
    plain("rad", "w_rad_ext", 17, C)
    ident = tile("ident", [P, P])
    eps = tile("eps", [P, 5])
    big = [w[n] for n in w if n.endswith("_m") or n.endswith("_r")]
    with phase(nc) as pctx:
        A = Alloc(nc, pctx, "setup")
        N = d["xa"].shape[0]
        slots = A.sb("slots", [P, (N + P - 1) // P], I32)
        pw = A.ps("pw", [W96, 512])

        zeroed, ident_done, weights_in = A.sem("zeroed"), A.sem("ident_done"), A.sem("weights_in")
        scaled, products, slots_set = A.sem("scaled"), A.sem("products"), A.sem("slots_set")
        slots_out = A.sem("slots_out")
        with nc.Block() as block:
            @block.gpsimd
            def _(pool):
                for t in big:
                    last = pool.memset(t[:, :], 0.0)
                last.then_inc(zeroed, 1)
                pool.memset(ident[:, :], 0.0).then_inc(ident_done, 1)
                pool.wait_ge(ident_done, 1)
                pool.affine_select(out=ident[:, :], in_=ident[:, :], compare_op=ALU.not_equal, fill=1.0,
                                   base=0, pattern=[[-1, P]], channel_multiplier=1).then_inc(ident_done, 1)
                pool.wait_ge(ident_done, 2)

            @block.sync
            def _(sp):
                sp.wait_ge(zeroed, 1)
                for dst, src in loads:
                    sp.dma_start(dst, src).then_inc(weights_in, 16)
                sp.wait_ge(slots_set, 1)
                full = slots.shape[1]
                rows = N // full
                sp.dma_start(d["slot"][0:rows * full, :].rearrange("(p k) c -> p (k c)", k=full),
                             slots[0:rows, :]).then_inc(slots_out, 16)
                if N % full:
                    sp.dma_start(d["slot"][rows * full:N, :].rearrange("(p k) c -> p (k c)", p=1),
                                 slots[0:1, 0:N % full]).then_inc(slots_out, 16)
                    sp.wait_ge(slots_out, 32)
                else:
                    sp.wait_ge(slots_out, 16)

            @block.vector
            def _(dve):
                dve.memset(slots[:, :], d["E_pad"] + 1).then_inc(slots_set, 1)
                dve.memset(eps[:, 0:1], EPS)
                for k in range(1, 5):
                    dve.memset(eps[:, k:k + 1], EPS ** k / 4)
                for l in (1, 2):
                    dve.memset(w[f"oa{l}"][0:W96, 1:2], 0.0)
                    dve.memset(w[f"oa{l}"][W96:W96 + 1, 0:1], 0.0)
                    dve.memset(w[f"oa{l}"][W96:W96 + 1, 1:2], 1.0)
                    dve.memset(w[f"oa{l}"][W96:W96 + 1, 2:2 + CS], 0.0)
                dve.wait_ge(weights_in, 16 * len(loads))
                for k, (ap, f) in enumerate(scales):
                    dve.tensor_scalar(ap, ap, float(f), None, ALU.mult).then_inc(scaled, 1)
                dve.wait_ge(scaled, len(scales))
                for ap, c, f in colscales:
                    dve.tensor_scalar(ap, ap, c, float(f), ALU.mult, ALU.mult).then_inc(scaled, 1)
                dve.wait_ge(scaled, len(scales) + len(colscales))
                dve.wait_ge(products, 1)
                dve.tensor_copy(w["va"][:, 128:160], pw[:, 0:CV]).then_inc(scaled, 1)
                dve.tensor_copy(ends_r[2 * CV:2 * CV + 1, 0:CS], pw[0:1, 128:128 + CS]).then_inc(scaled, 1)
                dve.wait_ge(scaled, len(scales) + len(colscales) + 2)

            @block.tensor
            def _(pe):
                pe.wait_ge(weights_in, 16 * len(loads))
                pe.matmul(pw[:, 0:CV], w["valT"][:, :], w["wg"][:, :], start=True, stop=True)
                pe.matmul(pw[0:1, 128:192], cols[0:64, 9:10], raw_src[:, :], start=True, stop=False)
                pe.matmul(pw[0:1, 128:192], cols[0:64, 9:10], raw_dst[:, :], start=False, stop=True).then_inc(products, 1)
    return w



def tiles_of(ap, at, g):
    return ap[bass.ds(at, g * P), :].rearrange("(g p) c -> p g c", p=P)


def last_edges(dve, out, ends, flag, big, done, value):
    dve.tensor_tensor(flag, ends[:, :, 0], ends[:, :, 1], ALU.not_equal).then_inc(done, 1)
    dve.wait_ge(done, value + 1)
    dve.scalar_tensor_tensor(flag, ends[:, :, 0], float(-big), flag, ALU.add, ALU.mult).then_inc(done, 1)
    dve.wait_ge(done, value + 2)
    return dve.tensor_scalar(out, flag, float(big), None, ALU.add)


def chain(nc, w, d, name, NB, iters, sources):
    N, NT = d["xa"].shape[0], d["NT"]
    G = PAIR
    step_rows = NB * G * P
    slots = 3 if NB % 3 == 0 else 4
    groups = [(b, b + 1) for b in range(0, NB, 2)]
    layers = 2 if sources else 3
    L = layers + 1
    big = 2 * N
    with phase(nc) as ctx:
        A = Alloc(nc, ctx, name, NB)
        xin, ac = A.sbs("xin", [P, G, C + 1]), A.sbs("ac", [P, G])
        st, mv = A.sbs("st", [P, G, 6]), A.sb("mv", [P, L, NB, G, 2])
        z = [A.sbs(f"z{l + 1}", [P, G, C]) for l in range(layers)]
        pre = A.sbs("pre", [P, G, C])
        tm, tr = A.sbs("tm", [P, G * P]), A.sbs("tr", [G * CV, P])
        terms = (1, 2, 3) if sources else (4,)
        n_s = len(terms)
        wt = A.sb("wt", [P, n_s, L, NB, G])
        va, vs, sd, rs, nb = (A.sb(n, [P, n_s] + s) for n, s in (
            ("va", [L, NB, G]), ("vs", [NB, G]), ("sd", [NB, G]), ("rs", [NB, G]), ("nb", [NB, G])))
        b_t = [A.ps(f"b_t{s}", [P, 512]) for s in range(slots)]
        b_y = [A.ps(f"b_y{s}", [P, 512])[:, 0:G * C].rearrange("p (k c) -> p k c", k=G) for s in range(slots)]

        x_in, taken = A.sems("x_in"), A.sems("taken")
        stats, aggr, z_ready = A.sems("stats"), A.sems("aggr"), [A.sems(f"z{l + 1}_ready") for l in range(layers)]
        turned, turned_out, y_done, pre_done = (A.sems(n) for n in ("turned", "turned_out", "y_done", "pre_done"))
        entry = A.sb("entry", [P, NB, G, 2])
        st0 = A.sbs("st0", [P, G, 6])
        stats0, aggr0 = A.sems("stats0"), A.sems("aggr0")
        settled = [A.sem(f"settled{q}") for q in range(len(groups))]
        weighted, summed, roots, inverse, shift = (
            [A.sem(f"{n}{q}") for q in range(len(groups))] for n in ("weighted", "summed", "roots", "inverse", "shift"))
        passed, start = A.sem("passed"), A.sem("start")
        out_ready, stored = A.sems("out_ready"), A.sems("stored")
        if sources:
            meta, eint, yin = A.sbs("meta", [P, G, MW]), A.sbs("eint", [P, G, 4], I32), A.sbs("yin", [P, G, 4])
            xl = [A.sbs(f"x{l}", [P, G, C]) for l in (1, 2, 3)]
            nrs, lst, rep = A.sb("nrs", [P, 2, NB, G]), A.sbs("lst", [P, G]), A.sbs("rep", [P, G], I32)
            e_in, rep_in, meta_set, lst_done, entered = (
                A.sems(n) for n in ("e_in", "rep_in", "meta_set", "lst_done", "entered"))
        else:
            ob = A.sbs("ob", [P, G, C])
            ids, ends = A.sb("ids", [P, NT, 2], I32), A.sb("ends", [P, NT, 2], I32)
            endf = A.sb("endf", [P, NT])
            RING = 8
            scatter_steps = NT // RING
            both = min(iters, scatter_steps)
            ring = A.sb("ring", [P, RING, 2], I32)
            ends_in, ids_done = A.sem("ends_in"), A.sem("ids_done")
            ring_in, ring_used = A.sem("ring_in"), A.sem("ring_used")

        def slot_free(eng, sems, r, b):
            if b >= slots:
                eng.wait_ge(sems[b - slots], r + 1)
            else:
                free(eng, sems[b + NB - slots], r)

        def parts(row, k):
            if k == 0:
                return row[:, 0:CS], vec(row[:, CS:C])
            return row[:, C - CS:C], vec(row[:, 0:C - CS])[:, ::-1, :]

        def centre(eng, b):
            for k in range(G):
                mean = entry[:, b, k, 0:1]
                s_part, v_part = parts(z[0][b][:, k, :], k)
                eng.tensor_scalar(s_part, xin[b][:, k, 0:CS], mean, None, ALU.subtract)
                ins = eng.tensor_scalar(v_part, cm(xin[b][:, k, CS:C]), mean, None, ALU.subtract)
            ins.then_inc(z_ready[0][b], 1)

        with nc.Block() as block:
            @block.sync
            def _(sp):
                if sources:
                    def loads(i):
                        for b in range(NB):
                            at = (NB * i + b) * G * P
                            free(sp, meta_set[b], i)
                            sp.dma_start(eint[b][:, :, :], tiles_of(d["eint"], at, G)).then_inc(e_in[b], 16)
                            sp.dma_start(yin[b][:, :, :], tiles_of(d["y"], at, G)).then_inc(e_in[b], 16)

                    def entries(i):
                        for b in range(NB):
                            at = (NB * i + b) * G * P
                            ready(sp, meta_set, i, b)
                            ready(sp, z_ready[0], i, b)
                            sp.dma_start(tiles_of(d["meta"], at, G), meta[b][:, :, :]).then_inc(entered[b], 16)
                            sp.dma_start(tiles_of(d["B0"], at, G), xin[b][:, :, :]).then_inc(entered[b], 16)

                    def stores(i):
                        for b in range(NB):
                            at = (NB * i + b) * G * P
                            ready(sp, out_ready, i, b)
                            for l in range(3):
                                sp.dma_start(tiles_of(d[f"B{l + 1}"], at, G), xl[l][b][:, :, :]).then_inc(stored[b], 16)

                    loads(0)
                    entries(0)
                    loads(1)
                    with sp.Fori(1, iters - 1) as i:
                        entries(i)
                        loads(i + 1)
                        stores(i - 1)
                    entries(iters - 1)
                    stores(iters - 2)
                    stores(iters - 1)
                    for b in range(NB):
                        sp.wait_ge(entered[b], 32 * iters)
                        sp.wait_ge(stored[b], 48 * iters)
                    return

                sp.dma_start(ends[:, :, :], d["ends"]).then_inc(ends_in, 16)
                sp.dma_start(ids[:, :, :], d["edge_ids"]).then_inc(ends_in, 16)

                def nodes(i, row):
                    for b in range(NB):
                        free(sp, z_ready[0][b], i)
                        free(sp, taken[b], i)
                        sp.dma_start(xin[b][:, :, :], d["xa"][bass.ds(row + b * G * P, G * P), :]
                                     .rearrange("(p g) c -> p g c", g=G)).then_inc(x_in[b], 16)

                def outs(i, row):
                    for b in range(NB):
                        ready(sp, out_ready, i, b)
                        sp.dma_start(d["out"][bass.ds(row + b * G * P, G * P), :]
                                     .rearrange("(p g) c -> p g c", g=G), ob[b][:, :, :]).then_inc(stored[b], 16)

                nodes(0, 0)
                with sp.Fori(1, iters - 1) as i:
                    nodes(i, i * step_rows)
                    outs(i - 1, (i - 1) * step_rows)
                nodes(iters - 1, N - step_rows)
                outs(iters - 2, (iters - 2) * step_rows)
                for b in range(NB):
                    sp.wait_ge(stored[b], 16 * (iters - 1))
                outs(iters - 1, N - step_rows)
                for b in range(NB):
                    sp.wait_ge(stored[b], 16 * iters)

            @block.gpsimd
            def _(pool):
                top = pool.to_reg(N - 1)

                def gathers(i):
                    for b in range(NB):
                        free(pool, entered[b], 32 * i)
                        apart(pool, e_in[b], 32 * i + 32, passed)
                        for k in range(G):
                            pool.indirect_dma_start(
                                xin[b][:, k, :], None, d["xa"],
                                bass.IndirectOffsetOnAxis(ap=eint[b][:, k, 0:1], axis=0),
                                bounds_check=top, oob_is_err=False).then_inc(x_in[b], 16)
                            pool.indirect_dma_start(
                                rep[b][:, k:k + 1], None, d["slot"],
                                bass.IndirectOffsetOnAxis(ap=eint[b][:, k, 0:1], axis=0),
                                bounds_check=top, oob_is_err=False).then_inc(rep_in[b], 16)

                def ids_load(i):
                    free(pool, ring_used, 16 * RING * i)
                    pool.dma_start(ring[:, :, :], ids[:, bass.ds(RING * i, RING), :]).then_inc(ring_in, 16)

                def scatters(i):
                    apart(pool, ring_in, 16 * i + 16, passed)
                    for r in range(RING):
                        pool.indirect_dma_start(
                            d["slot"], bass.IndirectOffsetOnAxis(ap=ring[:, r, 0:1], axis=0),
                            ring[:, r, 1:2], None, bounds_check=top,
                            oob_is_err=False).then_inc(ring_used, 16)

                def centres(i):
                    for b in range(NB):
                        apart(pool, aggr0[b], i + 1, passed)
                        centre(pool, b)

                if sources:
                    gathers(0)
                    with pool.Fori(1, iters) as i:
                        gathers(i)
                else:
                    centres(0)
                    pool.wait_ge(ids_done, 3)
                    ids_load(0)
                    scatters(0)
                    with pool.Fori(1, both) as i:
                        ids_load(i)
                        centres(i)
                        scatters(i)
                    if both < iters:
                        with pool.Fori(both, iters) as i:
                            centres(i)
                    if both < scatter_steps:
                        with pool.Fori(both, scatter_steps) as i:
                            ids_load(i)
                            scatters(i)
                    pool.wait_ge(ring_used, 16 * RING * scatter_steps)

            @block.vector
            def _(dve):
                for k in range(n_s):
                    for l in range(L):
                        ins = dve.memset(wt[:, k, l, :, :], float(EPS) ** (terms[k] - 1 - l) if l < terms[k] else 0.0)
                ins.then_inc(start, 1)
                dve.wait_ge(start, 1)
                if not sources:
                    dve.wait_ge(ends_in, 32)
                    last_edges(dve, ids[:, :, 0], ends, endf[:, :], big, ids_done, 0).then_inc(ids_done, 1)

                def statistics(n, src, group, st_, to, stats_, aggr_):
                    for b in group:
                        for k in range(G):
                            ins = dve.bn_stats(st_[b][:, k, :], src[b][:, k, 0:C])
                        ins.then_inc(stats_[b], 1)
                    for b in group:
                        apart(dve, stats_[b], n, passed)
                        for k in range(G):
                            ins = dve.bn_aggr(to(b, k), st_[b][:, k, :])
                        ins.then_inc(aggr_[b], 1)

                def describe(i, b):
                    dve.wait_ge(e_in[b], 32 * i + 32)
                    dve.wait_ge(rep_in[b], 16 * G * (i + 1))
                    dve.tensor_tensor(meta[b][:, :, M_YA:M_YA + 4], yin[b][:, :, :],
                                      xin[b][:, :, C:C + 1].to_broadcast([P, G, 4]), ALU.mult)
                    dve.tensor_copy(meta[b][:, :, M_Y:M_Y + 4], yin[b][:, :, :])
                    dve.tensor_copy(meta[b][:, :, M_Y + 4:M_Y + 6], yin[b][:, :, 1:3])
                    mint = meta[b][:, :, :].bitcast(I32)
                    dve.tensor_copy(mint[:, :, M_DST:M_DST + 1], eint[b][:, :, 1:2])
                    dve.tensor_copy(mint[:, :, M_REP], rep[b][:, :])
                    last_edges(dve, mint[:, :, M_LAST], eint[b][:, :, 1:3], lst[b][:, :], big,
                               lst_done[b], 2 * i).then_inc(meta_set[b], 1)

                def enter(i, group):
                    for b in group:
                        dve.wait_ge(x_in[b], 16 * (G if sources else 1) * (i + 1))
                    statistics(i + 1, xin, group, st0, lambda b, k: entry[:, b, k, :], stats0, aggr0)
                    for b in group:
                        dve.tensor_copy(ac[b][:, :], xin[b][:, :, C]).then_inc(taken[b], 1)
                        if sources:
                            describe(i, b)
                    if sources:
                        for b in group:
                            dve.wait_ge(aggr0[b], i + 1)
                            free(dve, out_ready[b], i)
                            centre(dve, b)

                def advance(i, l, group):
                    for b in group:
                        s = b % slots
                        dve.wait_ge(y_done[b], i * layers + l + 1)
                        for k in range(G):
                            if l < 2:
                                ins = dve.scalar_tensor_tensor(pre[b][:, k, :], b_y[s][:, k, 0:C],
                                                               ac[b][:, k:k + 1], z[l][b][:, k, :],
                                                               ALU.mult, ALU.add)
                            else:
                                ins = dve.tensor_tensor(pre[b][:, k, :], b_y[s][:, k, 0:C],
                                                        z[l][b][:, k, :], ALU.add)
                        ins.then_inc(pre_done[b], 1)
                    for b in group:
                        dve.wait_ge(pre_done[b], i * layers + l + 1)
                    statistics(i * layers + l + 1, pre, group, st, lambda b, k: mv[:, l + 1, b, k, :], stats, aggr)

                def deviations(i, q):
                    bs = slice(groups[q][0], groups[q][-1] + 1)
                    for b in groups[q]:
                        dve.wait_ge(aggr[b], (i + 1) * layers)
                    dve.wait_ge(settled[q], i + 1)
                    for k, n in enumerate(terms):
                        ins = dve.tensor_tensor(va[:, k, 0:n, bs, :].rearrange("p l b g -> p l (b g)"),
                                                mv[:, 0:n, bs, :, 1].rearrange("p l b g -> p l (b g)"),
                                                wt[:, k, 0:n, bs, :].rearrange("p l b g -> p l (b g)"), ALU.mult)
                    ins.then_inc(weighted[q], 1)
                    dve.wait_ge(weighted[q], i + 1)
                    for k, n in enumerate(terms):
                        ins = dve.tensor_reduce(vs[:, k, bs, :].rearrange("p b g -> p (b g)"),
                                                va[:, k, 0:n, bs, :].rearrange("p l b g -> p (b g) l"), AX.X, ALU.add)
                    ins.then_inc(summed[q], 1)

                def inverses(i, q):
                    bs = slice(groups[q][0], groups[q][-1] + 1)
                    dve.wait_ge(roots[q], i + 1)
                    dve.reciprocal(rs[:, :, bs, :], sd[:, :, bs, :]).then_inc(inverse[q], 1)
                    dve.wait_ge(inverse[q], i + 1)
                    if sources:
                        dve.tensor_scalar(nrs[:, :, bs, :], rs[:, 1:3, bs, :], -1.0, None, ALU.mult)
                    dve.scalar_tensor_tensor(nb[:, 0, bs, :], mv[:, layers, bs, :, 0], 1.0 if sources else -1.0,
                                             rs[:, n_s - 1, bs, :], ALU.mult, ALU.mult).then_inc(shift[q], 1)

                def settle(i, q):
                    bs = slice(groups[q][0], groups[q][-1] + 1)
                    for b in groups[q]:
                        dve.wait_ge(aggr0[b], i + 1)
                    dve.tensor_copy(mv[:, 0, bs, :, :], entry[:, bs, :, :]).then_inc(settled[q], 1)

                def body(i, more=True):
                    for l in range(layers - 1):
                        for group in groups:
                            advance(i, l, group)
                    for q, group in enumerate(groups):
                        advance(i, layers - 1, group)
                        deviations(i, q)
                        if q:
                            inverses(i, q - 1)
                            if more:
                                enter(i + 1, groups[q - 1])
                                settle(i + 1, q - 1)
                    inverses(i, len(groups) - 1)
                    if more:
                        enter(i + 1, groups[-1])
                        settle(i + 1, len(groups) - 1)

                for q, group in enumerate(groups):
                    enter(0, group)
                    settle(0, q)
                body(0)
                with dve.Fori(1, iters - 1) as i:
                    body(i)
                body(iters - 1, more=False)

            @block.scalar
            def _(act):
                def turn_out(i, l, group):
                    if l:
                        for b in group:
                            act.wait_ge(aggr[b], i * layers + l)
                            for k in range(G):
                                ins = act.activation(z[l][b][:, k, :], pre[b][:, k, :], ACT.Identity,
                                                     bias=mv[:, l, b, k, 0:1], scale=-1.0)
                            ins.then_inc(z_ready[l][b], 1)
                    for b in group:
                        s = b % slots
                        act.wait_ge(turned[b], i * layers + l + 1)
                        act.activation(tm[b][:, :], b_t[s][:, 0:G * P], ACT.Copy)
                        act.activation(tr[b][:, :], b_t[s][0:G * CV, G * P:G * P + P], ACT.Copy).then_inc(turned_out[b], 1)

                def deviations(i, q):
                    bs = slice(groups[q][0], groups[q][-1] + 1)
                    act.wait_ge(summed[q], i + 1)
                    for k, n in enumerate(terms):
                        ins = act.activation(sd[:, k, bs, :], vs[:, k, bs, :], ACT.Sqrt, bias=w["eps"][:, n:n + 1])
                    ins.then_inc(roots[q], 1)

                def results(i, q):
                    act.wait_ge(shift[q], i + 1)
                    for b in groups[q]:
                        free(act, stored[b], (48 if sources else 16) * i)
                        for k in range(G):
                            if sources:
                                for l, (from_, scale) in enumerate(((z[0], rs[:, 0, b, k:k + 1]), (z[1], nrs[:, 0, b, k:k + 1]),
                                                                    (pre, nrs[:, 1, b, k:k + 1]))):
                                    f, bias = (ACT.Identity, nb[:, 0, b, k:k + 1]) if l == 2 else (ACT.Copy, 0.0)
                                    to, row = xl[l][b][:, k, :], from_[b][:, k, :]
                                    if k == 0:
                                        ins = act.activation(to, row, f, bias=bias, scale=scale)
                                    else:
                                        s_part, v_part = parts(row, k)
                                        act.activation(to[:, 0:CS], s_part, f, bias=bias, scale=scale)
                                        ins = act.activation(vec(to[:, CS:C]), v_part, f, bias=bias, scale=scale)
                            else:
                                sc, bi = rs[:, 0, b, k:k + 1], nb[:, 0, b, k:k + 1]
                                s_part, v_part = parts(pre[b][:, k, :], k)
                                act.activation(ob[b][:, k, 0:CS], s_part, ACT.Identity, bias=bi, scale=sc)
                                ins = act.activation(cm(ob[b][:, k, CS:C]), v_part, ACT.Identity, bias=bi, scale=sc)
                        ins.then_inc(out_ready[b], 1)

                def body(i, more=True):
                    for l in range(1, layers - 1):
                        for group in groups:
                            turn_out(i, l, group)
                    Q = len(groups)
                    late = 1 if sources else 2
                    for q in range(Q):
                        turn_out(i, layers - 1, groups[q])
                        if q >= late:
                            deviations(i, q - late)
                            if q > late:
                                results(i, q - late - 1)
                    for q in range(Q - late, Q):
                        deviations(i, q)
                        if q < Q - 1 and q:
                            results(i, q - 1)
                    for q in range(Q):
                        if q >= Q - 2:
                            results(i, q)
                        if more:
                            turn_out(i + 1, 0, groups[q])

                for group in groups:
                    turn_out(0, 0, group)
                body(0)
                with act.Fori(1, iters - 1) as i:
                    body(i)
                body(iters - 1, more=False)

            @block.tensor
            def _(pe):
                def body(i):
                    for l in range(layers):
                        wm, wr = (w[f"sc{l + 1}_m"], w[f"sc{l + 1}_b_m"]), w[f"sc{l + 1}_r"]
                        r = i * layers + l
                        for group in groups:
                            for b in group:
                                s = b % slots
                                ready(pe, z_ready[l], i, b)
                                slot_free(pe, turned_out, r, b)
                                zz = z[l][b][:, :, :].rearrange("p k c -> p (k c)")
                                pe.transpose(b_t[s][:, 0:P], zz[:, 0:P], w["ident"][:, :])
                                pe.transpose(b_t[s][:, P:2 * P], zz[:, G * C - P:G * C], w["ident"][:, :])
                                ins = pe.transpose(b_t[s][0:G * CV, 2 * P:3 * P], zz[:, P:G * C - P], w["ident"][:, :])
                                ins.then_inc(turned[b], 1)
                            for b in group:
                                s = b % slots
                                pe.wait_ge(turned_out[b], r + 1)
                                slot_free(pe, pre_done, r, b)
                                yy = b_y[s].rearrange("p k c -> p (k c)")
                                pe.matmul(yy[:, 0:P], tm[b][:, 0:P], wm[0][:, :], start=True, stop=True)
                                pe.matmul(yy[:, G * C - P:G * C], tm[b][:, P:2 * P], wm[1][:, :], start=True, stop=True)
                                ins = pe.matmul(yy[:, P:G * C - P], tr[b][:, :], wr[:, :], start=True, stop=True)
                                ins.then_inc(y_done[b], 1)

                body(0)
                with pe.Fori(1, iters) as i:
                    body(i)



def vecs(ap):
    return ap.rearrange("p k (c u) -> p k c u", c=3)


def edge_rows(nc, ap, at, n):
    return ap[:, bass.ds(at, n)]


def attend0(nc, w, d):
    NT, N = d["NT"], d["xa"].shape[0]
    iters = NT // BODY
    K = PAIR
    with phase(nc) as ctx:
        A = Alloc(nc, ctx, "att", PLACES)
        xr = A.sbs("xr", [P, 2 * K, C + 1])
        meta, eint = A.sbs("meta", [P, K, MW]), A.sbs("eint", [P, K, 4], I32)
        attr, drow = A.sbs("attr", [16, K * P]), A.sbs("drow", [4, K * P + 2], I32)
        st, sq = A.sbs("st", [P, 2 * K, 6]), A.sbs("sq", [P, 2 * K, 96])
        mvs, sss = A.sb("mv", [P, PLACES, 2 * K, 2]), A.sb("ss", [P, PLACES, 2 * K])
        sds, rss = A.sb("sd", [P, 2, PLACES, 2 * K]), A.sb("rs", [P, 2, PLACES, 2 * K])
        xn = A.sbs("xn", [P, K, 2 * C])
        tm, tr = A.sbs("tm", [P, 2 * K * P]), A.sbs("tr", [2 * CV + 1, K * P])
        msg = A.sbs("msg", [P, K, CS + 5 * CV])
        ws, t1, t2, q = A.sbs("ws", [P, K, 128]), A.sbs("t1", [P, K, 96]), A.sbs("t2", [P, K, 96]), A.sbs("q", [P, K, 96])
        wv, cr, dt = A.sbs("wv", [P, K, CV]), A.sbs("cr", [P, K, 96]), A.sbs("dt", [P, K, CV])
        m1 = A.sbs("m1", [P, K, 480])
        m1t = A.sbs("m1t", [P, K, 512])
        val, gate, al = A.sbs("val", [P, K, 192]), A.sbs("gate", [P, K, CV]), A.sbs("al", [P, K, 64])
        la, lb, q2, sc = A.sbs("la", [P, K, 64]), A.sbs("lb", [P, K, 64]), A.sbs("q2", [P, K, 96]), A.sbs("sc", [P, K, 4])
        vt, vr, at4 = A.sbs("vt", [P, K * P]), A.sbs("vr", [64, K * P]), A.sbs("at4", [4, K * P])
        e5 = A.sbs("e5", [P, K, 160])
        h1, c1, p1, e1, e2, c2, e3 = (A.sbs(n, [P, K, 64 if n == "h1" else 96])
                                      for n in ("h1", "c1", "p1", "e1", "e2", "c2", "e3"))
        h = A.sbs("h", [P, K, C])
        pen, pen2, mrun = A.sbs("pen", [4, K * P]), A.sbs("pen2", [4, K * P]), A.sbs("mrun", [4, K * P])

        banks = A.ps("banks", [P, 8, 512])
        halves = [banks[:, k, :].rearrange("p (k e) -> p k e", k=K) for k in range(8)]
        b_t, b_r = (banks[:, 0, :], banks[:, 2, :]), (banks[:, 1, :], banks[:, 3, :])
        b_m, b_w = (halves[4], halves[5]), (halves[6], halves[7])
        b_u = (banks[:, 0:2, :], banks[:, 2:4, :])
        b_vt, b_vr = (banks[:, 4, :], banks[:, 0, :]), (banks[:, 5, :], banks[:, 1, :])
        b_h = (banks[:, 2:4, :], banks[:, 4:6, :])

        in_, meta_in, d_in, d0_out = (A.sems(n) for n in ("in", "meta_in", "d_in", "d0_out"))
        stats, squares, aggr = (A.sems(n) for n in ("stats", "squares", "aggr"))
        roots, scl = A.sem("roots"), A.sem("scl")
        xn_s, xn_v, turned, turned_out = (A.sems(n) for n in ("xn_s", "xn_v", "turned", "turned_out"))
        msg_done, msg_out, p_a, p_b, m1_ready = (A.sems(n) for n in ("msg_done", "msg_out", "p_a", "p_b", "m1_ready"))
        m1_turned, m1_out, va_done, acts = (A.sems(n) for n in ("m1_turned", "m1_out", "va_done", "acts"))
        c_a, c_b, c_ready, v_turned, v_out = (A.sems(n) for n in ("c_a", "c_b", "c_ready", "v_turned", "v_out"))
        h_done, e_out, d_a, d_b, h_ready, stored = (A.sems(n) for n in ("h_done", "e_out", "d_a", "d_b", "h_ready", "stored"))
        start, passed = A.sem("start"), A.sem("passed")

        def pos(i, b):
            return (PLACES * i + b) * K * P

        with nc.Block() as block:
            @block.sync
            def _(sp):
                def row_loads(i):
                    for b in range(PLACES):
                        free(sp, xn_s[b], i)
                        free(sp, xn_v[b], i)
                        free(sp, msg_done[b], i)
                        at = pos(i, b)
                        sp.dma_start(xr[b][:, 0:K, :], tiles_of(d["B0"], at, K)).then_inc(in_[b], 16)
                        sp.dma_start(eint[b][:, :, :], tiles_of(d["eint"], at, K)).then_inc(in_[b], 16)
                        sp.dma_start(attr[b][:, :], d["attr16"][0:16, bass.ds(at, K * P)]).then_inc(in_[b], 16)

                def edge_loads(i):
                    for b in range(PLACES):
                        free(sp, h_ready[b], i)
                        sp.dma_start(meta[b][:, :, :], tiles_of(d["meta"], pos(i, b), K)).then_inc(meta_in[b], 16)
                        sp.dma_start(drow[b][:, :], d["dst_row"][0:1, bass.ds(pos(i, b), K * P + 2)]
                                     .partition_broadcast(4)).then_inc(meta_in[b], 16)

                def stores(i):
                    for b in range(PLACES):
                        ready(sp, h_ready, i, b)
                        at = pos(i, b)
                        sp.dma_start(tiles_of(d["H0"], at, K), h[b][:, :, :]).then_inc(stored[b], 16)
                        sp.dma_start(d["A0"][:, bass.ds(at, K * P)], at4[b][:, :]).then_inc(stored[b], 16)
                        sp.dma_start(d["R0"][:, bass.ds(at, K * P)], mrun[b][:, :]).then_inc(stored[b], 16)

                row_loads(0)
                edge_loads(0)
                row_loads(1)
                with sp.Fori(1, iters - 1) as i:
                    edge_loads(i)
                    stores(i - 1)
                    row_loads(i + 1)
                edge_loads(iters - 1)
                stores(iters - 2)
                stores(iters - 1)
                for b in range(PLACES):
                    sp.wait_ge(stored[b], 48 * iters)

            @block.gpsimd
            def _(pool):
                top = pool.to_reg(N - 1)
                def body(i):
                    for b in range(PLACES):
                        free(pool, d0_out[b], 16 * i)
                        apart(pool, in_[b], 48 * i + 48, passed)
                        for k in range(K):
                            pool.indirect_dma_start(
                                xr[b][:, K + k, :], None, d["xa"],
                                bass.IndirectOffsetOnAxis(ap=eint[b][:, k, 3:4], axis=0),
                                bounds_check=top, oob_is_err=False).then_inc(d_in[b], 16)

                body(0)
                with pool.Fori(1, iters) as i:
                    body(i)

            @block.vector
            def _(dve):
                for b in range(PLACES):
                    dve.memset(tr[b][2 * CV:2 * CV + 1, :], 1.0)
                dve.memset(mrun[-1][:, :], NEG).then_inc(start, 1)
                dve.wait_ge(start, 1)
                def statistics(i):
                    n = i + 1
                    for b in range(PLACES):
                        dve.wait_ge(in_[b], 48 * n)
                        dve.wait_ge(d_in[b], 32 * n)
                        for k in range(2 * K):
                            ins = dve.bn_stats(st[b][:, k, :], xr[b][:, k, 0:CS])
                        ins.then_inc(stats[b], 1)
                    for b in range(PLACES):
                        apart(dve, stats[b], n, passed)
                        for k in range(2 * K):
                            ins = dve.bn_aggr(mvs[:, b, k, :], st[b][:, k, :])
                        ins.then_inc(aggr[b], 1)

                def inverses(i):
                    dve.wait_ge(roots, i + 1)
                    dve.reciprocal(rss[:, :, :, :], sds[:, :, :, :]).then_inc(scl, 1)
                    dve.wait_ge(scl, i + 1)

                def normalise(b):
                    for k in range(2 * K):
                        to = xn[b][:, k, 0:CS] if k < K else xn[b][:, k - K, 2 * C - CS:2 * C]
                        ins = dve.tensor_scalar(to, xr[b][:, k, 0:CS], mvs[:, b, k, 0:1],
                                                rss[:, 0, b, k:k + 1], ALU.subtract, ALU.mult)
                    ins.then_inc(xn_s[b], 1)

                def products(i):
                    n = i + 1
                    for b in range(PLACES):
                        dve.wait_ge(meta_in[b], 32 * n)
                        dve.wait_ge(msg_done[b], n)
                        dve.wait_ge(msg_out[b], n)
                        y, W, m = meta[b], b_w[b % 2], msg[b]
                        S3, S64 = [P, K, 3, CV], [P, K, 3, CS]
                        y0, yx = y[:, :, M_Y:M_Y + 1], y[:, :, M_Y + 1:M_Y + 4]
                        yx1, yx2 = y[:, :, M_Y + 2:M_Y + 5], y[:, :, M_Y + 3:M_Y + 6]

                        def over(ap, shape):
                            return ap.unsqueeze(3).to_broadcast(shape)

                        dve.tensor_tensor(ws[b][:, :, :].rearrange("p k (a u) -> p k a u", a=2),
                                          W[:, :, 0:128].rearrange("p k (a u) -> p k a u", a=2),
                                          m[:, :, 0:CS].unsqueeze(2).to_broadcast([P, K, 2, CS]), ALU.mult)
                        dve.tensor_tensor(vecs(t1[b][:, :, :]), vecs(m[:, :, 96:192]), over(yx2, S3), ALU.mult)
                        dve.tensor_tensor(vecs(t2[b][:, :, :]), vecs(m[:, :, 128:224]), over(yx1, S3), ALU.mult)
                        dve.tensor_tensor(vecs(q[b][:, :, :]), vecs(m[:, :, 64:160]), over(yx, S3), ALU.mult)
                        dve.tensor_tensor(wv[b][:, :, :], W[:, :, 128:160], y0.to_broadcast([P, K, CV]),
                                          ALU.mult).then_inc(p_a[b], 1)
                        dve.wait_ge(p_a[b], n)
                        dve.tensor_tensor(m1[b][:, :, 0:CS], ws[b][:, :, 0:CS], y0.to_broadcast([P, K, CS]), ALU.mult)
                        mx = m1[b][:, :, 96:480].rearrange("p k (c u) -> p k c u", c=3)
                        dve.tensor_tensor(mx[:, :, :, 0:CS], ws[b][:, :, 64:128].unsqueeze(2).to_broadcast(S64),
                                          over(yx, S64), ALU.mult)
                        dve.tensor_tensor(cr[b][:, :, :], t1[b][:, :, :], t2[b][:, :, :], ALU.subtract)
                        dve.tensor_tensor(mx[:, :, :, 64:96], vecs(m[:, :, 64:160]),
                                          wv[b][:, :, :].unsqueeze(2).to_broadcast(S3), ALU.mult)
                        dve.tensor_reduce(dt[b][:, :, :], q[b][:, :, :].rearrange("p k (c u) -> p k u c", c=3),
                                          AX.X, ALU.add).then_inc(p_b[b], 1)
                        dve.wait_ge(p_b[b], n)
                        dve.tensor_tensor(m1[b][:, :, CS:96], W[:, :, 160:192], dt[b][:, :, :], ALU.mult)
                        dve.tensor_tensor(mx[:, :, :, 96:128], W[:, :, 192:224].unsqueeze(2).to_broadcast(S3),
                                          vecs(cr[b][:, :, :]), ALU.mult).then_inc(m1_ready[b], 1)

                def values(i):
                    n = i + 1
                    for b in range(PLACES):
                        y, W = meta[b], b_w[b % 2]
                        S3 = [P, K, 3, CV]
                        yx = y[:, :, M_Y + 1:M_Y + 4]
                        dve.wait_ge(va_done[b], n)
                        dve.wait_ge(acts[b], n)
                        dve.tensor_tensor(vecs(val[b][:, :, 64:160]), vecs(W[:, :, 160:256]),
                                          gate[b][:, :, :].unsqueeze(2).to_broadcast(S3), ALU.mult)
                        dve.scalar_tensor_tensor(la[b][:, :, :], al[b][:, :, :], 0.2, al[b][:, :, :],
                                                 ALU.mult, ALU.max).then_inc(c_a[b], 1)
                        dve.wait_ge(c_a[b], n)
                        dve.tensor_tensor(vecs(q2[b][:, :, :]), vecs(val[b][:, :, 64:160]),
                                          yx.unsqueeze(3).to_broadcast(S3), ALU.mult)
                        dve.tensor_tensor(lb[b][:, :, :], la[b][:, :, :],
                                          w["adot"][:, :].unsqueeze(1).to_broadcast([P, K, 64]), ALU.mult).then_inc(c_b[b], 1)
                        dve.wait_ge(c_b[b], n)
                        dve.tensor_reduce(val[b][:, :, 160:192], q2[b][:, :, :].rearrange("p k (c u) -> p k u c", c=3),
                                          AX.X, ALU.add)
                        dve.tensor_reduce(sc[b][:, :, :], lb[b][:, :, :].rearrange("p k (h u) -> p k h u", h=4),
                                          AX.X, ALU.add).then_inc(c_ready[b], 1)

                def messages(i, b):
                    n = i + 1
                    y = meta[b]
                    S3 = [P, K, 3, CV]
                    y0, yx = y[:, :, M_Y:M_Y + 1], y[:, :, M_Y + 1:M_Y + 4].unsqueeze(3).to_broadcast(S3)
                    yx1 = y[:, :, M_Y + 2:M_Y + 5].unsqueeze(3).to_broadcast(S3)
                    yx2 = y[:, :, M_Y + 3:M_Y + 6].unsqueeze(3).to_broadcast(S3)
                    dve.wait_ge(h_done[b], n)
                    dve.wait_ge(e_out[b], n)
                    free(dve, stored[b], 48 * i)
                    dve.tensor_tensor(h1[b][:, :, :], b_h[b % 2][:, :, 0:CS], y0.to_broadcast([P, K, CS]), ALU.mult)
                    dve.tensor_tensor(vecs(c1[b][:, :, :]), b_h[b % 2][:, :, 64:96].unsqueeze(2).to_broadcast(S3), yx, ALU.mult)
                    de = b_h[b % 2][:, :, 96:288].rearrange("p k (c u) -> p k c u", c=3)
                    dve.tensor_tensor(vecs(p1[b][:, :, :]), de[:, :, :, 0:CV],
                                      y0.unsqueeze(3).to_broadcast(S3), ALU.mult)
                    dve.tensor_tensor(vecs(e1[b][:, :, :]), vecs(e5[b][:, :, 32:128]), yx2, ALU.mult)
                    dve.tensor_tensor(vecs(e2[b][:, :, :]), vecs(e5[b][:, :, 64:160]), yx1, ALU.mult)
                    dve.tensor_tensor(pen[b][:, :], drow[b][:, 1:K * P + 1], drow[b][:, 0:K * P],
                                      ALU.not_equal).then_inc(d_a[b], 1)
                    dve.wait_ge(d_a[b], n)
                    dve.tensor_tensor(h[b][:, :, 0:CS], b_h[b % 2][:, :, 288:352], h1[b][:, :, :], ALU.add)
                    dve.tensor_tensor(c2[b][:, :, :], c1[b][:, :, :], p1[b][:, :, :], ALU.add)
                    dve.tensor_tensor(e3[b][:, :, :], e1[b][:, :, :], e2[b][:, :, :], ALU.subtract)
                    dve.tensor_scalar(pen2[b][:, :], pen[b][:, :], NEG, None, ALU.mult).then_inc(d_b[b], 1)
                    dve.wait_ge(d_b[b], n)
                    if b:
                        dve.wait_ge(h_ready[b - 1], n)
                    dve.tensor_tensor(h[b][:, :, CS:C], c2[b][:, :, :], e3[b][:, :, :], ALU.add)
                    dve.tensor_tensor_scan(mrun[b][:, :], pen2[b][:, :], at4[b][:, :],
                                           mrun[b - 1][:, K * P - 1:K * P], ALU.add, ALU.max).then_inc(h_ready[b], 1)

                def body(i, more=True):
                    products(i)
                    if more:
                        statistics(i + 1)
                    values(i)
                    for b in range(PLACES):
                        messages(i, b)
                        if more and b in (1, 2):
                            if b == 1:
                                inverses(i + 1)
                            normalise(2 * b - 2)
                            normalise(2 * b - 1)
                    dve.wait_ge(h_ready[-1], i + 1)

                statistics(0)
                inverses(0)
                for b in range(PLACES):
                    normalise(b)
                body(0)
                with dve.Fori(1, iters - 1) as i:
                    body(i)
                body(iters - 1, more=False)

            @block.scalar
            def _(act):
                def squared(i, b):
                    n = i + 1
                    act.wait_ge(in_[b], 48 * n)
                    act.wait_ge(d_in[b], 32 * n)
                    act.dma_start(tiles_of(d["D0"], pos(i, b), K), xr[b][:, K:2 * K, :]).then_inc(d0_out[b], 16)
                    for k in range(2 * K):
                        ins = act.activation(sq[b][:, k, :], xr[b][:, k, CS:C], ACT.Square, accum_out=sss[:, b, k:k + 1])
                    ins.then_inc(squares[b], 1)

                def deviations(i):
                    n = i + 1
                    for b in range(PLACES):
                        act.wait_ge(squares[b], n)
                        act.wait_ge(aggr[b], n)
                    act.activation(sds[:, 1, :, :], sss[:, :, :], ACT.Sqrt, bias=w["eps"][:, 0:1], scale=1.0 / CV)
                    act.activation(sds[:, 0, :, :], mvs[:, :, :, 1], ACT.Sqrt, bias=w["eps"][:, 0:1]).then_inc(roots, 1)

                def normalise(i, b):
                    act.wait_ge(scl, i + 1)
                    for k in range(2 * K):
                        to = vec(xn[b][:, k, CS:C]) if k < K else vec(xn[b][:, k - K, C:2 * C - CS])[:, ::-1, :]
                        ins = act.activation(to, cm(xr[b][:, k, CS:C]), ACT.Copy, scale=rss[:, 1, b, k:k + 1])
                    ins.then_inc(xn_v[b], 1)

                def products(i):
                    n = i + 1
                    for b in range(PLACES):
                        act.wait_ge(turned[b], n)
                        act.activation(tm[b][:, :], b_t[b % 2], ACT.Copy)
                        act.activation(tr[b][0:2 * CV, :], b_r[b % 2][0:2 * CV, 0:K * P], ACT.Copy).then_inc(turned_out[b], 1)
                    for b in range(PLACES):
                        act.wait_ge(msg_done[b], n)
                        act.activation(msg[b][:, :, 0:C], b_m[b % 2][:, :, 0:C], ACT.Copy)
                        act.activation(msg[b][:, :, C:C + 64], b_m[b % 2][:, :, CS:CS + 64], ACT.Copy).then_inc(msg_out[b], 1)
                    for b in range(PLACES):
                        act.wait_ge(m1_turned[b], n)
                        for k in range(K):
                            act.activation(m1t[b][0:96, k, 0:128], b_u[b % 2][0:96, k, 0:128], ACT.Copy)
                            ins = act.activation(m1t[b][:, k, 128:512], b_u[b % 2][:, k, 128:512], ACT.Copy)
                        ins.then_inc(m1_out[b], 1)

                def gates(i, b):
                    act.wait_ge(va_done[b], i + 1)
                    act.activation(val[b][:, :, 0:CS], b_w[b % 2][:, :, 0:CS], ACT.Sigmoid)
                    act.activation(gate[b][:, :, :], b_w[b % 2][:, :, 128:160], ACT.Sigmoid)
                    act.activation(al[b][:, :, :], b_w[b % 2][:, :, 64:128], ACT.Copy).then_inc(acts[b], 1)

                def values(i):
                    n = i + 1
                    for b in range(PLACES):
                        act.wait_ge(v_turned[b], n)
                        free(act, stored[b], 48 * i)
                        act.activation(vt[b][:, :], b_vt[b % 2][:, 0:K * P], ACT.Copy)
                        act.activation(vr[b][:, :], b_vr[b % 2][0:64, 0:K * P], ACT.Copy)
                        act.activation(at4[b][:, :], b_vr[b % 2][0:4, K * P:2 * K * P], ACT.Copy).then_inc(v_out[b], 1)

                def last_products(i, b):
                    act.wait_ge(h_done[b], i + 1)
                    de = b_h[b % 2][:, :, 96:288].rearrange("p k (c u) -> p k c u", c=3)
                    act.activation(vecs(e5[b][:, :, 0:96]), de[:, :, :, CV:2 * CV], ACT.Copy)
                    act.activation(e5[b][:, :, 96:160].rearrange("p k (c u) -> p k c u", c=2), de[:, :, 0:2, CV:2 * CV],
                                   ACT.Copy).then_inc(e_out[b], 1)

                def body(i, more=True):
                    products(i)
                    for b in range(PLACES):
                        gates(i, b)
                        if more and b:
                            squared(i + 1, b - 1)
                    if more:
                        squared(i + 1, PLACES - 1)
                    values(i)
                    if more:
                        deviations(i + 1)
                    for b in range(PLACES):
                        last_products(i, b)
                        if more and b in (1, 2):
                            normalise(i + 1, 2 * b - 2)
                            normalise(i + 1, 2 * b - 1)

                for b in range(PLACES):
                    squared(0, b)
                deviations(0)
                for b in range(PLACES):
                    normalise(0, b)
                body(0)
                with act.Fori(1, iters - 1) as i:
                    body(i)
                body(iters - 1, more=False)
                for b in range(PLACES):
                    act.wait_ge(d0_out[b], 16 * iters)

            @block.tensor
            def _(pe):
                ident = w["ident"]
                def products(i):
                    n = i + 1
                    for b in range(PLACES):
                        pe.wait_ge(xn_s[b], n)
                        pe.wait_ge(xn_v[b], n)
                        if b >= 2:
                            pe.wait_ge(turned_out[b - 2], n)
                        elif b:
                            free(pe, h_ready[2], i)
                        for k in range(K):
                            pe.transpose(b_t[b % 2][:, k * P:(k + 1) * P], xn[b][:, k, 0:P], ident[:, :])
                            pe.transpose(b_t[b % 2][:, (K + k) * P:(K + k + 1) * P], xn[b][:, k, 2 * C - P:2 * C], ident[:, :])
                            ins = pe.transpose(b_r[b % 2][0:2 * CV, k * P:(k + 1) * P], xn[b][:, k, P:2 * C - P], ident[:, :])
                        ins.then_inc(turned[b], 1)
                    for b in range(PLACES):
                        pe.wait_ge(turned_out[b], n)
                        pe.wait_ge(in_[b], 48 * n)
                        if b >= 2:
                            pe.wait_ge(msg_out[b - 2], n)
                            pe.wait_ge(m1_ready[b - 2], n)
                        elif b == 0:
                            free(pe, h_ready[3], i)
                        for k in range(K):
                            s, t = slice(k * P, (k + 1) * P), slice((K + k) * P, (K + k + 1) * P)
                            pe.matmul(b_m[b % 2][:, k, 0:C], tr[b][:, s], w["ends_r"][:, :], start=True, stop=False)
                            pe.matmul(b_m[b % 2][:, k, 0:P], tm[b][:, s], w["src_m"][:, :], start=False, stop=False)
                            pe.matmul(b_m[b % 2][:, k, 0:P], tm[b][:, t], w["dst_m"][:, :], start=False, stop=True)
                            ins = pe.matmul(b_w[b % 2][:, k, 0:224], attr[b][:, s], w["rbf"][:, :], start=True, stop=True)
                        ins.then_inc(msg_done[b], 1)
                    for b in range(PLACES):
                        pe.wait_ge(m1_ready[b], n)
                        if b >= 2:
                            pe.wait_ge(m1_out[b - 2], n)
                        for k in range(K):
                            pe.transpose(b_u[b % 2][0:96, k, 0:P], m1[b][:, k, 0:96], ident[:, :])
                            for c in range(3):
                                ins = pe.transpose(b_u[b % 2][:, k, P * (c + 1):P * (c + 2)],
                                                   m1[b][:, k, 96 + P * c:96 + P * (c + 1)], ident[:, :])
                        ins.then_inc(m1_turned[b], 1)

                def values(i):
                    n = i + 1
                    for b in range(PLACES):
                        pe.wait_ge(m1_out[b], n)
                        if b >= 2:
                            pe.wait_ge(acts[b - 2], n)
                            pe.wait_ge(c_a[b - 2], n)
                        for k in range(K):
                            pe.matmul(b_w[b % 2][:, k, 0:C], m1t[b][0:96, k, 0:P], w["va"][:, :], start=True, stop=True)
                            for c in range(3):
                                ins = pe.matmul(b_w[b % 2][:, k, C + 32 * c:C + 32 * c + 32],
                                                m1t[b][:, k, P * (c + 1):P * (c + 2)], w["wvval"][:, :],
                                                start=True, stop=True)
                        ins.then_inc(va_done[b], 1)
                    for b in range(PLACES):
                        pe.wait_ge(c_ready[b], n)
                        if b >= 2:
                            pe.wait_ge(v_out[b - 2], n)
                        for k in range(K):
                            s = slice(k * P, (k + 1) * P)
                            pe.transpose(b_vt[b % 2][:, s], val[b][:, k, 0:P], ident[:, :])
                            pe.transpose(b_vr[b % 2][0:64, s], val[b][:, k, P:192], ident[:, :])
                            ins = pe.transpose(b_vr[b % 2][0:4, (K + k) * P:(K + k + 1) * P], sc[b][:, k, :], ident[:, :])
                        ins.then_inc(v_turned[b], 1)
                    for b in range(PLACES):
                        pe.wait_ge(v_out[b], n)
                        if b >= 2:
                            pe.wait_ge(h_ready[b - 2], n)
                        elif b:
                            pe.wait_ge(v_out[2], n)
                        for k in range(K):
                            s = slice(k * P, (k + 1) * P)
                            pe.matmul(b_h[b % 2][:, k, 0:224], vt[b][:, s], w["h_m"][:, :], start=True, stop=True)
                            ins = pe.matmul(b_h[b % 2][:, k, 224:352], vr[b][:, s], w["h_r"][:, :], start=True, stop=True)
                        ins.then_inc(h_done[b], 1)

                def body(i):
                    products(i)
                    values(i)

                body(0)
                with pe.Fori(1, iters) as i:
                    body(i)


def soften0(nc, d):
    E_pad = d["E_pad"]
    CH = max(c for c in range(1, min(2048, E_pad // 4) + 1) if E_pad % (2 * c) == 0)
    iters = E_pad // (2 * CH)
    with phase(nc) as ctx:
        A = Alloc(nc, ctx, "soft")
        a, m, dr = A.sbs("a", [4, CH]), A.sbs("m", [4, CH]), A.sbs("dr", [4, CH + 1], I32)
        same, pen, top = A.sbs("same", [4, CH]), A.sbs("pen", [4, CH]), A.sbs("top", [4, CH])
        dif, ex, bs = A.sbs("dif", [4, CH]), A.sbs("ex", [4, CH]), A.sbs("bs", [4, CH])
        in_, same_done, pen_done, top_done, dif_done, ex_done, bs_done, stored = (
            A.sems(n) for n in ("in", "same", "pen", "top", "dif", "ex", "bs", "stored"))
        start = A.sem("start")

        def at(i, b):
            return i * (-2 * CH) + (E_pad - (b + 1) * CH)

        with nc.Block() as block:
            @block.sync
            def _(sp):
                def loads(i):
                    for b in range(2):
                        free(sp, bs_done[b], i)
                        sp.dma_start(a[b][:, :], edge_rows(nc, d["A0"], at(i, b), CH)).then_inc(in_[b], 16)
                        sp.dma_start(m[b][:, :], edge_rows(nc, d["R0"], at(i, b), CH)).then_inc(in_[b], 16)
                        sp.dma_start(dr[b][:, :], d["dst_row"][0:1, bass.ds(at(i, b) + 1, CH + 1)]
                                     .partition_broadcast(4)).then_inc(in_[b], 16)

                def stores(i):
                    for b in range(2):
                        ready(sp, bs_done, i, b)
                        sp.dma_start(edge_rows(nc, d["X0"], at(i, b), CH), ex[b][:, :]).then_inc(stored[b], 16)
                        sp.dma_start(edge_rows(nc, d["S0"], at(i, b), CH), bs[b][:, :]).then_inc(stored[b], 16)

                loads(0)
                if iters > 1:
                    with sp.Fori(1, iters) as i:
                        loads(i)
                        stores(i - 1)
                stores(iters - 1)
                for b in range(2):
                    sp.wait_ge(stored[b], 32 * iters)

            @block.vector
            def _(dve):
                dve.memset(top[1][:, :], NEG)
                dve.memset(bs[1][:, :], 0.0).then_inc(start, 1)
                dve.wait_ge(start, 1)
                def body(i):
                    n = i + 1
                    for b in range(2):
                        dve.wait_ge(in_[b], 48 * n)
                        dve.tensor_tensor(same[b][:, :], dr[b][:, 0:CH], dr[b][:, 1:CH + 1], ALU.is_equal).then_inc(same_done[b], 1)
                    for b in range(2):
                        dve.wait_ge(same_done[b], n)
                        dve.tensor_scalar(pen[b][:, :], same[b][:, :], -NEG, NEG, ALU.mult, ALU.add).then_inc(pen_done[b], 1)
                    for b in range(2):
                        dve.wait_ge(pen_done[b], n)
                        if b:
                            dve.wait_ge(top_done[0], n)
                        else:
                            free(dve, top_done[1], i)
                        dve.tensor_tensor_scan(top[b][:, ::-1], pen[b][:, ::-1], m[b][:, ::-1], top[1 - b][:, 0:1],
                                               ALU.add, ALU.max).then_inc(top_done[b], 1)
                    for b in range(2):
                        dve.wait_ge(top_done[b], n)
                        dve.tensor_tensor(dif[b][:, :], a[b][:, :], top[b][:, :], ALU.subtract).then_inc(dif_done[b], 1)
                    for b in range(2):
                        dve.wait_ge(ex_done[b], n)
                        free(dve, stored[b], 32 * i)
                        if b:
                            dve.wait_ge(bs_done[0], n)
                        else:
                            free(dve, bs_done[1], i)
                        dve.tensor_tensor_scan(bs[b][:, ::-1], same[b][:, ::-1], ex[b][:, ::-1], bs[1 - b][:, 0:1],
                                               ALU.mult, ALU.add).then_inc(bs_done[b], 1)

                body(0)
                with dve.Fori(1, iters) as i:
                    body(i)

            @block.scalar
            def _(act):
                def body(i):
                    for b in range(2):
                        ready(act, dif_done, i, b)
                        free(act, stored[b], 32 * i)
                        act.activation(ex[b][:, :], dif[b][:, :], ACT.Exp).then_inc(ex_done[b], 1)

                body(0)
                with act.Fori(1, iters) as i:
                    body(i)


class Runs:

    def __init__(self, A):
        self.row = A.sbs("row", [P, PAIR * P + 1], I32)
        self.eq, self.ind = A.sbs("eq", [P, PAIR, P]), A.sbs("ind", [P, PAIR, P])
        self.done = A.sems("runs")

    def load(self, sp, d, at, b, sem):
        sp.dma_start(self.row[b][:, :], d["dst_row"][0:1, bass.ds(at, PAIR * P + 1)]
                     .partition_broadcast(P)).then_inc(sem, 16)

    def matrices(self, eng, b, dst_col):
        rows = self.row[b][:, 1:PAIR * P + 1].rearrange("p (k e) -> p k e", k=PAIR)
        before_ = self.row[b][:, 0:PAIR * P].rearrange("p (k e) -> p k e", k=PAIR)[:, :, 0:1]
        eng.tensor_tensor(self.eq[b][:, :, :], rows, dst_col.to_broadcast([P, PAIR, P]), ALU.is_equal)
        eng.tensor_tensor(self.ind[b][:, :, :], rows, before_.to_broadcast([P, PAIR, P]),
                          ALU.is_equal).then_inc(self.done[b], 1)


class Norm:

    def __init__(self, A):
        K = PAIR
        self.st, self.mv = A.sbs("n_st", [P, K, 6]), A.sbs("n_mv", [P, K, 2])
        self.sd, self.rs, self.nb = A.sbs("n_sd", [P, K]), A.sbs("n_rs", [P, K]), A.sbs("n_nb", [P, K])
        self.stats, self.aggr, self.roots, self.scl, self.nbd = (
            A.sems("n_" + x) for x in ("stats", "aggr", "roots", "scl", "nbd"))
        self.passed = A.sem("n_passed")

    def vector(self, dve, n, pre, pre_ready):
        for b in range(PLACES):
            dve.wait_ge(pre_ready[b], n)
            for k in range(PAIR):
                ins = dve.bn_stats(self.st[b][:, k, :], pre[b][:, k, :])
            ins.then_inc(self.stats[b], 1)
        for b in range(PLACES):
            apart(dve, self.stats[b], n, self.passed)
            for k in range(PAIR):
                ins = dve.bn_aggr(self.mv[b][:, k, :], self.st[b][:, k, :])
            ins.then_inc(self.aggr[b], 1)
        for b in range(PLACES):
            dve.wait_ge(self.roots[b], n)
            dve.reciprocal(self.rs[b][:, :], self.sd[b][:, :]).then_inc(self.scl[b], 1)
        for b in range(PLACES):
            dve.wait_ge(self.scl[b], n)
            dve.scalar_tensor_tensor(self.nb[b][:, :], self.mv[b][:, :, 0], -1.0, self.rs[b][:, :],
                                     ALU.mult, ALU.mult).then_inc(self.nbd[b], 1)

    def scalar_roots(self, act, n, eps):
        for b in range(PLACES):
            act.wait_ge(self.aggr[b], n)
            act.activation(self.sd[b][:, :], self.mv[b][:, :, 1], ACT.Sqrt, bias=eps).then_inc(self.roots[b], 1)

    def scalar_apply(self, act, b, k, out, pre):
        return act.activation(out, pre, ACT.Identity, bias=self.nb[b][:, k:k + 1], scale=self.rs[b][:, k:k + 1])


def update0(nc, w, d):
    NT = d["NT"]
    iters, K = NT // BODY, PAIR
    with phase(nc) as ctx:
        A = Alloc(nc, ctx, "upd", PLACES)
        h, x0, eint = A.sbs("h", [P, K, C]), A.sbs("x0", [P, K, C + 1]), A.sbs("eint", [P, K, 4], I32)
        ex, bs, same = A.sbs("ex", [4, K * P]), A.sbs("bs", [4, K * P]), A.sbs("same", [4, K * P])
        den = A.sbs("den", [4, K * P])
        de2, rden, alpha = (A.sbs(n, [P, K, 4]) for n in ("de2", "rden", "alpha"))
        ha, gm, gr = A.sbs("ha", [P, K, C]), A.sbs("gm", [P, K, P]), A.sbs("gr", [CV, K, P])
        pre, x1 = A.sbs("pre", [P, K, C]), A.sbs("x1", [P, K, ROW])
        runs, norm = Runs(A), Norm(A)
        b_al = [A.ps(f"b_al{b}", [P, 512]) for b in range(2)]
        b_s, b_y = [A.ps(f"b_s{b}", [P, K, 256]) for b in range(2)], [A.ps(f"b_y{b}", [P, K, 256]) for b in range(2)]
        in_, x_in, same_done, den_done, de2_done, rden_done, alpha_done = (
            A.sems(n) for n in ("in", "x_in", "same", "den", "de2", "rden", "alpha"))
        al_done, ha_done, seg_done, g_done, y_done, pre_done, x1_s, x1_v, stored = (
            A.sems(n) for n in ("al", "ha", "seg", "g", "y", "pre", "x1_s", "x1_v", "stored"))
        h_in = A.sems("h_in")
        g_half, start, passed = A.sems("g_half"), A.sem("start"), A.sem("passed")

        def pos(i, b):
            return (PLACES * i + b) * K * P

        with nc.Block() as block:
            @block.sync
            def _(sp):
                def early(i):
                    for b in range(PLACES):
                        free(sp, al_done[b], i)
                        free(sp, runs.done[b], i)
                        at = pos(i, b)
                        sp.dma_start(eint[b][:, :, :], tiles_of(d["eint"], at, K)).then_inc(in_[b], 16)
                        sp.dma_start(ex[b][:, :], d["X0"][:, bass.ds(at, K * P)]).then_inc(in_[b], 16)
                        sp.dma_start(bs[b][:, :], d["S0"][:, bass.ds(at, K * P)]).then_inc(in_[b], 16)
                        runs.load(sp, d, at, b, in_[b])

                def messages(i):
                    for b in range(PLACES):
                        free(sp, ha_done[b], i)
                        sp.dma_start(h[b][:, :, :], tiles_of(d["H0"], pos(i, b), K)).then_inc(h_in[b], 16)

                def late(i):
                    for b in range(PLACES):
                        free(sp, x1_v[b], i)
                        sp.dma_start(x0[b][:, :, :], tiles_of(d["D0"], pos(i, b), K)).then_inc(x_in[b], 16)

                def stores(i):
                    for b in range(PLACES):
                        ready(sp, x1_s, i, b)
                        ready(sp, x1_v, i, b)
                        sp.dma_start(tiles_of(d["D1"], pos(i, b), K), x1[b][:, :, :]).then_inc(stored[b], 16)

                early(0)
                messages(0)
                late(0)
                early(1)
                with sp.Fori(1, iters - 1) as i:
                    messages(i)
                    early(i + 1)
                    stores(i - 1)
                    late(i)
                messages(iters - 1)
                stores(iters - 2)
                late(iters - 1)
                stores(iters - 1)
                for b in range(PLACES):
                    sp.wait_ge(stored[b], 16 * iters)

            @block.vector
            def _(dve):
                dve.memset(den[-1][:, :], 0.0)
                dve.memset(gm[-1][:, :, :], 0.0)
                dve.memset(gr[-1][:, :, :], 0.0).then_inc(start, 1)
                dve.wait_ge(start, 1)
                def sums(i):
                    n = i + 1
                    for b in range(PLACES):
                        free(dve, g_done[b], i)
                        dve.wait_ge(in_[b], 64 * n)
                        row = runs.row[b]
                        dve.tensor_tensor(same[b][:, :], row[0:4, 1:K * P + 1], row[0:4, 0:K * P],
                                          ALU.is_equal).then_inc(same_done[b], 1)
                        runs.matrices(dve, b, eint[b][:, :, 1:2])
                    for b in range(PLACES):
                        dve.wait_ge(same_done[b], n)
                        if b:
                            dve.wait_ge(den_done[b - 1], n)
                        else:
                            free(dve, den_done[-1], i)
                        dve.tensor_tensor_scan(den[b][:, :], same[b][:, :], bs[b][:, :], den[b - 1][:, K * P - 1:K * P],
                                               ALU.mult, ALU.max).then_inc(den_done[b], 1)

                def messages(i):
                    n = i + 1
                    for b in range(PLACES):
                        dve.wait_ge(al_done[b], n)
                        dve.tensor_scalar(de2[b][:, :, :], b_al[b % 2][:, 8:16].rearrange("p (k h) -> p k h", k=K),
                                          1e-16, None, ALU.add).then_inc(de2_done[b], 1)
                        dve.wait_ge(de2_done[b], n)
                        dve.reciprocal(rden[b][:, :, :], de2[b][:, :, :]).then_inc(rden_done[b], 1)
                        dve.wait_ge(rden_done[b], n)
                        dve.tensor_tensor(alpha[b][:, :, :], b_al[b % 2][:, 0:8].rearrange("p (k h) -> p k h", k=K),
                                          rden[b][:, :, :], ALU.mult).then_inc(alpha_done[b], 1)
                    for b in range(PLACES):
                        dve.wait_ge(alpha_done[b], n)
                        dve.wait_ge(h_in[b], 16 * n)
                        al = alpha[b][:, :, :]
                        dve.tensor_tensor(ha[b][:, :, 0:CS].rearrange("p k (h u) -> p k h u", h=4),
                                          h[b][:, :, 0:CS].rearrange("p k (h u) -> p k h u", h=4),
                                          al.unsqueeze(3).to_broadcast([P, K, 4, 16]), ALU.mult)
                        for k in range(K):
                            ins = dve.tensor_tensor(ha[b][:, k, CS:C].rearrange("p (c h u) -> p c h u", c=3, h=4),
                                                    h[b][:, k, CS:C].rearrange("p (c h u) -> p c h u", c=3, h=4),
                                                    al[:, k, :].unsqueeze(1).unsqueeze(3).to_broadcast([P, 3, 4, 8]), ALU.mult)
                        ins.then_inc(ha_done[b], 1)
                    for b in range(PLACES):
                        dve.wait_ge(seg_done[b], n)
                        for k in range(K):
                            if k:
                                dve.wait_ge(g_half[b], n)
                            elif b:
                                dve.wait_ge(g_done[b - 1], n)
                            else:
                                free(dve, g_done[-1], i)
                            pb, pk = (b, 0) if k else (b - 1, K - 1)
                            dve.scalar_tensor_tensor(gm[b][:, k, :], runs.ind[b][:, k, :], gm[pb][:, pk, P - 1:P],
                                                     b_s[b % 2][:, k, 0:P], ALU.mult, ALU.add)
                            dve.scalar_tensor_tensor(gr[b][:, k, :], runs.ind[b][0:CV, k, :], gr[pb][:, pk, P - 1:P],
                                                     b_s[b % 2][0:CV, k, P:2 * P], ALU.mult,
                                                     ALU.add).then_inc((g_done if k else g_half)[b], 1)

                def update(i):
                    n = i + 1
                    for b in range(PLACES):
                        dve.wait_ge(y_done[b], n)
                        dve.wait_ge(x_in[b], 16 * n)
                        dve.scalar_tensor_tensor(pre[b][:, :, 0:CS], x0[b][:, :, 0:CS], 2.0, b_y[b % 2][:, :, 0:CS],
                                                 ALU.mult, ALU.add)
                        for k in range(K):
                            ins = dve.scalar_tensor_tensor(pre[b][:, k, CS:C].rearrange("p (c u) -> p c u", c=3),
                                                           cm(x0[b][:, k, CS:C]), 2.0,
                                                           b_y[b % 2][:, k, CS:C].rearrange("p (c u) -> p c u", c=3),
                                                           ALU.mult, ALU.add)
                        ins.then_inc(pre_done[b], 1)
                    norm.vector(dve, n, pre, pre_done)
                    for b in range(PLACES):
                        free(dve, stored[b], 16 * i)
                        dve.tensor_copy(x1[b][:, :, C:C + 1], x0[b][:, :, C:C + 1])
                        dve.tensor_tensor(x1[b][:, :, C + 1:C + 2], x0[b][:, :, C:C + 1], x0[b][:, :, C:C + 1],
                                          ALU.mult).then_inc(x1_v[b], 1)

                staged(dve, iters, sums, update, messages)

            @block.scalar
            def _(act):
                def body(i):
                    norm.scalar_roots(act, i + 1, w["eps"][:, 0:1])
                    for b in range(PLACES):
                        act.wait_ge(norm.nbd[b], i + 1)
                        free(act, stored[b], 16 * i)
                        for k in range(K):
                            ins = norm.scalar_apply(act, b, k, x1[b][:, k, 0:C], pre[b][:, k, :])
                        ins.then_inc(x1_s[b], 1)

                body(0)
                with act.Fori(1, iters) as i:
                    body(i)

            @block.tensor
            def _(pe):
                def body(i):
                    n = i + 1
                    for b in range(PLACES):
                        if b >= 2:
                            pe.wait_ge(alpha_done[b - 2], n)
                        apart(pe, den_done[b], n, passed)
                        for k in range(K):
                            s = slice(k * P, (k + 1) * P)
                            pe.transpose(b_al[b % 2][:, 4 * k:4 * k + 4], ex[b][:, s], w["ident"][0:4, 0:4])
                            ins = pe.transpose(b_al[b % 2][:, 8 + 4 * k:8 + 4 * k + 4], den[b][:, s], w["ident"][0:4, 0:4])
                        ins.then_inc(al_done[b], 1)
                    for b in range(PLACES):
                        pe.wait_ge(ha_done[b], n)
                        pe.wait_ge(runs.done[b], n)
                        if b >= 2:
                            pe.wait_ge(g_done[b - 2], n)
                        for k in range(K):
                            pe.matmul(b_s[b % 2][:, k, 0:P], ha[b][:, k, 0:P], runs.eq[b][:, k, :], start=True, stop=True)
                            ins = pe.matmul(b_s[b % 2][0:CV, k, P:2 * P], ha[b][:, k, P:C], runs.eq[b][:, k, :],
                                            start=True, stop=True)
                        ins.then_inc(seg_done[b], 1)
                    for b in range(PLACES):
                        pe.wait_ge(g_done[b], n)
                        if b >= 2:
                            pe.wait_ge(pre_done[b - 2], n)
                        else:
                            free(pe, pre_done[b - 2], i)
                        for k in range(K):
                            pe.matmul(b_y[b % 2][:, k, 0:P], gm[b][:, k, :], w["out0_m"][:, :], start=True, stop=True)
                            ins = pe.matmul(b_y[b % 2][:, k, P:C], gr[b][:, k, :], w["out0_r"][0:CV, 0:CV], start=True, stop=True)
                        ins.then_inc(y_done[b], 1)

                body(0)
                with pe.Fori(1, iters) as i:
                    body(i)


def source_rows(pool, d, l, b, xs, meta, sem, top):
    for k in range(PAIR):
        pool.indirect_dma_start(xs[b][:, k, :], None, d[f"D{l}"],
                                bass.IndirectOffsetOnAxis(ap=meta[b][:, k, M_REP:M_REP + 1].bitcast(I32), axis=0),
                                bounds_check=top, oob_is_err=False).then_inc(sem[b], 16)


def conv(nc, w, d, l):
    NT, E_pad = d["NT"], d["E_pad"]
    iters, K = NT // BODY, PAIR
    FIN = 8 if l == 1 else 16
    S3, S64 = [P, K, 3, CV], [P, K, 3, CS]
    with phase(nc) as ctx:
        A = Alloc(nc, ctx, f"l{l}", PLACES)
        xs, meta, attr = A.sbs("xs", [P, K, ROW]), A.sbs("meta", [P, K, MW]), A.sbs("attr", [FIN, K * P])
        slot = A.sbs("slot", [P, K, MW])
        xd = A.sbs("xd", [P, K, ROW])
        sm, sr = A.sbs("sm", [P, K * P]), A.sbs("sr", [CV, K * P])
        dm, dr = A.sbs("dm", [P, K * P]), A.sbs("dr", [CV, K * P])
        g1, g2, we = A.sbs("g1", [64, K * P]), A.sbs("g2", [64, K * P]), A.sbs("we", [P, K, 192])
        p1, p2, q, dt = A.sbs("p1", [P, K, 128]), A.sbs("p2", [P, K, 96]), A.sbs("q", [P, K, 96]), A.sbs("dt", [P, K, CV])
        M1 = W96 + 1
        mid = A.sbs("mid", [P, K, M1 + 3 * W96])
        g = A.sbs("g", [M1, K, 512])
        cn, rc, rc2, ta, qq = (A.sbs(n, [P, K]) for n in ("cn", "rc", "rc2", "ta", "qq"))
        s1, pre, xo = A.sbs("s1", [P, K, C]), A.sbs("pre", [P, K, C]), A.sbs("xo", [P, K, ROW])
        runs, norm = Runs(A), Norm(A)
        bank = [A.ps(f"bank{k}", [P, 512]) for k in range(8)]
        halves = [t[:, :].rearrange("p (k e) -> p k e", k=K) for t in bank]
        b_t, b_d, b_h = (bank[0], bank[6]), (bank[0], bank[4]), (bank[1], bank[7])
        b_f, b_w = (halves[2], halves[6]), (halves[3], halves[7])
        b_s, b_y, b_c = ((bank[4], bank[5]), (bank[2], bank[3])), (halves[6], halves[2]), (halves[7], halves[3])
        in_, src_in, row_in, xd_in, stored = A.sems("in"), A.sems("src_in"), A.sems("row_in"), A.sems("xd_in"), A.sems("stored")
        hid1, act1, hid2, act2, w_done, w_out = (A.sems(n) for n in ("hid1", "act1", "hid2", "act2", "w_done", "w_out"))
        s_turned, s_out, f_done, f_used, mid_a, mid_ready = (
            A.sems(n) for n in ("s_turned", "s_out", "f_done", "f_used", "mid_a", "mid_ready"))
        seg_done, g_half, g_done, c_done = (A.sems(n) for n in ("seg", "g_half", "g_done", "c_done"))
        d_turned, d_out, y_done, s1_done, pre_done, xo_s, xo_v = (
            A.sems(n) for n in ("d_turned", "d_out", "y_done", "s1", "pre", "xo_s", "xo_v"))
        q_sem, start, passed = A.sems("q_sem"), A.sem("start"), A.sem("passed")

        def pos(i, b):
            return (PLACES * i + b) * K * P

        with nc.Block() as block:
            @block.sync
            def _(sp):
                def source_loads(i):
                    for b in range(PLACES):
                        free(sp, s_turned[b], i)
                        free(sp, hid1[b], i)
                        at = pos(i, b)
                        sp.dma_start(slot[b][:, :, :], tiles_of(d["meta"], at, K)).then_inc(src_in[b], 16)
                        sp.dma_start(xs[b][:, :, 0:C], tiles_of(d[f"B{l}"], at, K)).then_inc(src_in[b], 16)
                        sp.dma_start(attr[b][:, :], d["attr8" if l == 1 else "attr16"][0:FIN, bass.ds(at, K * P)]).then_inc(src_in[b], 16)

                def edge_loads(i):
                    for b in range(PLACES):
                        free(sp, seg_done[b], i)
                        free(sp, g_done[b], i)
                        at = pos(i, b)
                        sp.dma_start(meta[b][:, :, :], tiles_of(d["meta"], at, K)).then_inc(in_[b], 16)
                        runs.load(sp, d, at, b, in_[b])

                def late(i):
                    for b in range(PLACES):
                        free(sp, xo_v[b], i)
                        sp.dma_start(xd[b][:, :, :], tiles_of(d[f"D{l}"], pos(i, b), K)).then_inc(xd_in[b], 16)

                def stores(i):
                    for b in range(PLACES):
                        ready(sp, xo_s, i, b)
                        ready(sp, xo_v, i, b)
                        sp.dma_start(tiles_of(d[f"D{l + 1}"], pos(i, b), K), xo[b][:, :, :]).then_inc(stored[b], 16)

                source_loads(0)
                edge_loads(0)
                late(0)
                source_loads(1)
                with sp.Fori(1, iters - 1) as i:
                    edge_loads(i)
                    source_loads(i + 1)
                    stores(i - 1)
                    late(i)
                edge_loads(iters - 1)
                stores(iters - 2)
                late(iters - 1)
                stores(iters - 1)
                for b in range(PLACES):
                    sp.wait_ge(stored[b], 16 * iters)

            @block.gpsimd
            def _(pool):
                top = pool.to_reg(E_pad - 1)
                def body(i):
                    for b in range(PLACES):
                        apart(pool, src_in[b], 48 * i + 48, passed)
                        source_rows(pool, d, l, b, xs, slot, row_in, top)

                body(0)
                with pool.Fori(1, iters) as i:
                    body(i)

            @block.vector
            def _(dve):
                for b in range(PLACES):
                    dve.memset(mid[b][:, :, W96:M1], 1.0)
                dve.memset(g[-1][:, :, :], 0.0).then_inc(start, 1)
                dve.wait_ge(start, 1)
                def matrices(i):
                    n = i + 1
                    for b in range(PLACES):
                        dve.wait_ge(in_[b], 32 * n)
                        runs.matrices(dve, b, meta[b][:, :, M_DST:M_DST + 1].bitcast(I32))

                def messages(i):
                    n = i + 1
                    for b in range(PLACES):
                        y, F, W = meta[b], b_f[b % 2], we[b]
                        y0, yx = y[:, :, M_YA:M_YA + 1], y[:, :, M_YA + 1:M_YA + 4]
                        gv = F[:, :, CS:C].rearrange("p k (c u) -> p k c u", c=3)
                        dve.wait_ge(f_done[b], n)
                        dve.wait_ge(w_out[b], n)
                        dve.tensor_tensor(p1[b][:, :, :].rearrange("p k (a u) -> p k a u", a=2),
                                          W[:, :, 0:128].rearrange("p k (a u) -> p k a u", a=2),
                                          F[:, :, 0:CS].unsqueeze(2).to_broadcast([P, K, 2, CS]), ALU.mult)
                        dve.tensor_tensor(vecs(p2[b][:, :, :]), gv, W[:, :, 128:160].unsqueeze(2).to_broadcast(S3), ALU.mult)
                        dve.tensor_tensor(vecs(q[b][:, :, :]), gv, yx.unsqueeze(3).to_broadcast(S3), ALU.mult).then_inc(f_used[b], 1)
                        dve.wait_ge(f_used[b], n)
                        mx = mid[b][:, :, M1:].rearrange("p k (c u) -> p k c u", c=3)
                        dve.tensor_reduce(dt[b][:, :, :], q[b][:, :, :].rearrange("p k (c u) -> p k u c", c=3),
                                          AX.X, ALU.add).then_inc(mid_a[b], 1)
                        dve.tensor_tensor(mid[b][:, :, 0:CS], p1[b][:, :, 0:CS], y0.to_broadcast([P, K, CS]), ALU.mult)
                        dve.tensor_tensor(mx[:, :, :, 0:CS], p1[b][:, :, 64:128].unsqueeze(2).to_broadcast(S64),
                                          yx.unsqueeze(3).to_broadcast(S64), ALU.mult)
                        dve.tensor_tensor(mx[:, :, :, CS:W96], vecs(p2[b][:, :, :]), y0.unsqueeze(3).to_broadcast(S3), ALU.mult)
                        dve.wait_ge(mid_a[b], n)
                        dve.tensor_tensor(mid[b][:, :, CS:W96], W[:, :, 160:192], dt[b][:, :, :], ALU.mult).then_inc(mid_ready[b], 1)
                    for b in range(PLACES):
                        dve.wait_ge(seg_done[b], n)
                        for k in range(K):
                            if k:
                                dve.wait_ge(g_half[b], n)
                            elif b:
                                dve.wait_ge(g_done[b - 1], n)
                            else:
                                free(dve, g_done[-1], i)
                            pb, pk = (b, 0) if k else (b - 1, K - 1)
                            for c in range(4):
                                R = M1 if c == 0 else W96
                                ins = dve.scalar_tensor_tensor(
                                    g[b][0:R, k, P * c:P * (c + 1)], runs.ind[b][0:R, k, :],
                                    g[pb][0:R, pk, P * (c + 1) - 1:P * (c + 1)], b_s[b % 2][k][0:R, P * c:P * (c + 1)],
                                    ALU.mult, ALU.add)
                            ins.then_inc((g_done if k else g_half)[b], 1)

                def update(i):
                    n = i + 1
                    for b in range(PLACES):
                        x = xd[b]
                        dve.wait_ge(xd_in[b], 16 * n)
                        dve.wait_ge(c_done[b], n)
                        dve.tensor_tensor(ta[b][:, :], b_c[b % 2][:, :, 0], x[:, :, C + 1], ALU.mult)
                        dve.tensor_scalar(cn[b][:, :], b_c[b % 2][:, :, 1], 1.0, None, ALU.max).then_inc(q_sem[b], 1)
                        if l == 2:
                            dve.wait_ge(q_sem[b], 4 * i + 1)
                            dve.reciprocal(rc[b][:, :], cn[b][:, :]).then_inc(q_sem[b], 1)
                            dve.wait_ge(q_sem[b], 4 * i + 2)
                            dve.tensor_tensor(rc2[b][:, :], rc[b][:, :], rc[b][:, :], ALU.mult).then_inc(q_sem[b], 1)
                            dve.wait_ge(q_sem[b], 4 * i + 3)
                            dve.tensor_tensor(qq[b][:, :], ta[b][:, :], rc2[b][:, :], ALU.mult).then_inc(q_sem[b], 1)
                        dve.wait_ge(y_done[b], n)
                        for k in range(K):
                            ins = dve.scalar_tensor_tensor(s1[b][:, k, :], b_y[b % 2][:, k, 0:C], x[:, k, C:C + 1],
                                                           x[:, k, 0:C], ALU.mult, ALU.add)
                        ins.then_inc(s1_done[b], 1)
                        dve.wait_ge(s1_done[b], n)
                        f = qq if l == 2 else ta
                        for k in range(K):
                            ins = dve.scalar_tensor_tensor(pre[b][:, k, :], b_c[b % 2][:, k, 2:2 + C], f[b][:, k:k + 1],
                                                           s1[b][:, k, :], ALU.mult, ALU.add)
                        ins.then_inc(pre_done[b], 1)
                    norm.vector(dve, n, pre, pre_done)
                    for b in range(PLACES):
                        free(dve, stored[b], 16 * i)
                        dve.tensor_copy(xo[b][:, :, C:ROW], xd[b][:, :, C:ROW]).then_inc(xo_v[b], 1)

                staged(dve, iters, matrices, update, messages)

            @block.scalar
            def _(act):
                def hidden(i):
                    n = i + 1
                    for group in ((0, 1), (2, 3)):
                        for b in group:
                            act.wait_ge(hid1[b], n)
                            act.activation(g1[b][:, :], b_h[b % 2][0:64, 0:K * P], ACT.Gelu_apprx_tanh if l == 1 else ACT.Silu,
                                           scale=float(FIN) ** -0.5).then_inc(act1[b], 1)
                        for b in group:
                            act.wait_ge(s_turned[b], n)
                            act.activation(sm[b][:, :], b_t[b % 2][:, 0:K * P], ACT.Copy)
                            act.activation(sr[b][:, :], b_t[b % 2][0:CV, K * P:2 * K * P], ACT.Copy).then_inc(s_out[b], 1)
                            if l == 1:
                                act.wait_ge(hid2[b], n)
                                act.activation(g2[b][:, :], b_h[b % 2][0:64, 0:K * P], ACT.Gelu_apprx_tanh,
                                               scale=0.125).then_inc(act2[b], 1)

                def weights(i):
                    n = i + 1
                    for b in range(PLACES):
                        act.wait_ge(w_done[b], n)
                        act.activation(we[b][:, :, :], b_w[b % 2][:, :, 0:192], ACT.Copy, scale=0.125).then_inc(w_out[b], 1)
                    for b in range(PLACES):
                        act.wait_ge(d_turned[b], n)
                        act.activation(dm[b][:, :], b_d[b % 2][:, 0:K * P], ACT.Copy)
                        act.activation(dr[b][:, :], b_d[b % 2][0:CV, K * P:2 * K * P], ACT.Copy).then_inc(d_out[b], 1)

                def results(i):
                    n = i + 1
                    norm.scalar_roots(act, n, w["eps"][:, 0:1])
                    for b in range(PLACES):
                        act.wait_ge(norm.nbd[b], n)
                        free(act, stored[b], 16 * i)
                        for k in range(K):
                            ins = norm.scalar_apply(act, b, k, xo[b][:, k, 0:C], pre[b][:, k, :])
                        ins.then_inc(xo_s[b], 1)

                staged(act, iters, hidden, results, weights)

            @block.tensor
            def _(pe):
                ident = w["ident"]
                act_last = act2 if l == 1 else act1

                def turn(rows, bank_):
                    for k in range(K):
                        s = slice(k * P, (k + 1) * P)
                        pe.transpose(bank_[:, s], rows[:, k, 0:P], ident[:, :])
                        ins = pe.transpose(bank_[0:CV, K * P + k * P:K * P + (k + 1) * P], rows[:, k, P:C], ident[:, :])
                    return ins

                def hidden(i):
                    n = i + 1
                    for group in ((0, 1), (2, 3)):
                        for b in group:
                            pe.wait_ge(src_in[b], 48 * n)
                            if b >= 2:
                                pe.wait_ge(act_last[b - 2], n)
                            pe.matmul(b_h[b % 2][0:64, 0:K * P], w[f"fc{l}_1"][:, :], attr[b][:, :], start=True, stop=True).then_inc(hid1[b], 1)
                        for b in group:
                            pe.wait_ge(row_in[b], 32 * n)
                            if b >= 2:
                                pe.wait_ge(s_out[b - 2], n)
                            turn(xs[b], b_t[b % 2]).then_inc(s_turned[b], 1)
                            if l == 1:
                                apart(pe, act1[b], n, passed)
                                pe.matmul(b_h[b % 2][0:64, 0:K * P], w["fc1_2"][:, :], g1[b][:, :], start=True, stop=True).then_inc(hid2[b], 1)

                def messages(i):
                    n = i + 1
                    for b in range(PLACES):
                        hid = g2 if l == 1 else g1
                        pe.wait_ge(act_last[b], n)
                        if b >= 2:
                            pe.wait_ge(w_out[b - 2], n)
                        elif b:
                            pe.wait_ge(act_last[-1], n)
                            pe.wait_ge(s_out[-1], n)
                        else:
                            free(pe, pre_done[-1], i)
                        for k in range(K):
                            ins = pe.matmul(b_w[b % 2][:, k, 0:192], hid[b][:, k * P:(k + 1) * P], w[f"fc{l}_3"][:, :], start=True, stop=True)
                        ins.then_inc(w_done[b], 1)
                        pe.wait_ge(s_out[b], n)
                        if b >= 2:
                            pe.wait_ge(f_used[b - 2], n)
                        for k in range(K):
                            s = slice(k * P, (k + 1) * P)
                            pe.matmul(b_f[b % 2][:, k, 0:P], sm[b][:, s], w[f"f{l}_m"][:, :], start=True, stop=True)
                            ins = pe.matmul(b_f[b % 2][:, k, P:C], sr[b][:, s], w[f"f{l}_r"][0:CV, 0:CV], start=True, stop=True)
                        ins.then_inc(f_done[b], 1)
                    for b in range(PLACES):
                        pe.wait_ge(xd_in[b], 16 * n)
                        if b >= 2:
                            pe.wait_ge(d_out[b - 2], n)
                        turn(xd[b], b_d[b % 2]).then_inc(d_turned[b], 1)
                    for b in range(PLACES):
                        pe.wait_ge(mid_ready[b], n)
                        pe.wait_ge(runs.done[b], n)
                        if b >= 2:
                            pe.wait_ge(g_done[b - 2], n)
                        elif b:
                            pe.wait_ge(f_used[-1], n)
                            pe.wait_ge(w_out[-1], n)
                        else:
                            pe.wait_ge(d_out[-1], n)
                        for k in range(K):
                            pe.matmul(b_s[b % 2][k][0:M1, 0:P], mid[b][:, k, 0:M1], runs.eq[b][:, k, :], start=True, stop=True)
                            for c in range(3):
                                ins = pe.matmul(b_s[b % 2][k][0:W96, P * (c + 1):P * (c + 2)],
                                                mid[b][:, k, M1 + W96 * c:M1 + W96 * (c + 1)], runs.eq[b][:, k, :],
                                                start=True, stop=True)
                        ins.then_inc(seg_done[b], 1)

                def update(i, fronts=None):
                    n = i + 1
                    fronts = i + 2 if fronts is None else fronts
                    for b in range(PLACES):
                        pe.wait_ge(d_out[b], n)
                        if b >= 2:
                            pe.wait_ge(pre_done[b - 2], n)
                        elif b:
                            pe.wait_ge(g_done[-1], n)
                        else:
                            pe.wait_ge(s_out[-1], fronts)
                            pe.wait_ge(act_last[-1], fronts)
                        for k in range(K):
                            s = slice(k * P, (k + 1) * P)
                            pe.matmul(b_y[b % 2][:, k, 0:P], dm[b][:, s], w[f"sc{l}_m"][:, :], start=True, stop=True)
                            ins = pe.matmul(b_y[b % 2][:, k, P:C], dr[b][:, s], w[f"sc{l}_r"][0:CV, 0:CV], start=True, stop=True)
                        ins.then_inc(y_done[b], 1)
                        pe.wait_ge(g_done[b], n)
                        for k in range(K):
                            pe.matmul(b_c[b % 2][:, k, 0:2 + CS], g[b][:, k, 0:P], w[f"oa{l}"][:, :], start=True, stop=True)
                            for c in range(3):
                                ins = pe.matmul(b_c[b % 2][:, k, 2 + CS + CV * c:2 + CS + CV * (c + 1)],
                                                g[b][0:W96, k, P * (c + 1):P * (c + 2)], w[f"ov{l}"][:, :],
                                                start=True, stop=True)
                        ins.then_inc(c_done[b], 1)

                staged(pe, iters, hidden, update, messages, last_tail=lambda i: update(i, iters))


def conv3(nc, w, d):
    NT, E_pad, N = d["NT"], d["E_pad"], d["xa"].shape[0]
    iters, K = NT // BODY, PAIR
    S3, S64 = [P, K, 3, CV], [P, K, 3, CS]
    with phase(nc) as ctx:
        A = Alloc(nc, ctx, "l3", PLACES)
        xs, meta, attr = A.sbs("xs", [P, K, ROW]), A.sbs("meta", [P, K, MW]), A.sbs("attr", [17, K * P])
        slot = A.sbs("slot", [P, K, MW])
        xd, last = A.sbs("xd", [P, K, ROW]), A.sbs("last", [P, K, MW])
        sm, sr = A.sbs("sm", [P, K * P]), A.sbs("sr", [CV, K * P])
        dm, dr = A.sbs("dm", [P, K * P]), A.sbs("dr", [CV, K * P])
        gate = A.sbs("gate", [P, K, C])
        h1, hq, hs, qv = A.sbs("h1", [P, K, CS]), A.sbs("hq", [P, K, CS]), A.sbs("hs", [P, K, CS]), A.sbs("qv", [P, K, 192])
        c1, p1, c2 = A.sbs("c1", [P, K, 96]), A.sbs("p1", [P, K, 96]), A.sbs("c2", [P, K, 96])
        mid, gm, gr = A.sbs("mid", [P, K, C]), A.sbs("gm", [P, K, P]), A.sbs("gr", [CV, K, P])
        pre, xo = A.sbs("pre", [P, K, C]), A.sbs("xo", [P, K, C])
        runs, norm = Runs(A), Norm(A)
        banks = A.ps("banks", [P, 8, 512])
        half = [banks[:, k, :].rearrange("p (k e) -> p k e", k=K) for k in range(8)]
        b_t, b_g, b_f = (banks[:, 0, :], banks[:, 2, :]), (half[1], half[3]), (banks[:, 2:4, :], banks[:, 6:8, :])
        b_d = banks[:, 0, :], banks[:, 1, :]
        b_s, b_y = (half[4], half[5]), (half[6], half[7])
        in_, src_in, row_in, xd_in, stored = A.sems("in"), A.sems("src_in"), A.sems("row_in"), A.sems("xd_in"), A.sems("stored")
        s_turned, s_out, f_done, f_used, gt_done, gt_out = (
            A.sems(n) for n in ("s_turned", "s_out", "f_done", "f_used", "gt_done", "gt_out"))
        mid_a, mid_b, mid_ready = A.sems("mid_a"), A.sems("mid_b"), A.sems("mid_ready")
        seg_done, g_half, g_done = A.sems("seg"), A.sems("g_half"), A.sems("g_done")
        d_turned, d_out, y_done, pre_done, xo_done = (A.sems(n) for n in ("d_turned", "d_out", "y", "pre", "xo"))
        start, passed = A.sem("start"), A.sem("passed")

        def pos(i, b):
            return (PLACES * i + b) * K * P

        with nc.Block() as block:
            @block.sync
            def _(sp):
                def source_loads(i):
                    for b in range(PLACES):
                        free(sp, s_turned[b], i)
                        free(sp, gt_done[b], i)
                        at = pos(i, b)
                        sp.dma_start(slot[b][:, :, :], tiles_of(d["meta"], at, K)).then_inc(src_in[b], 16)
                        sp.dma_start(xs[b][:, :, 0:C], tiles_of(d["B3"], at, K)).then_inc(src_in[b], 16)
                        sp.dma_start(attr[b][:, :], d["attr16"][:, bass.ds(at, K * P)]).then_inc(src_in[b], 16)

                def edge_loads(i):
                    for b in range(PLACES):
                        free(sp, mid_ready[b], i)
                        free(sp, runs.done[b], i)
                        at = pos(i, b)
                        sp.dma_start(meta[b][:, :, :], tiles_of(d["meta"], at, K)).then_inc(in_[b], 16)
                        runs.load(sp, d, at, b, in_[b])

                def late(i):
                    for b in range(PLACES):
                        free(sp, stored[b], 32 * i)
                        free(sp, pre_done[b], i)
                        at = pos(i, b)
                        sp.dma_start(xd[b][:, :, :], tiles_of(d["D3"], at, K)).then_inc(xd_in[b], 16)
                        sp.dma_start(last[b][:, :, :], tiles_of(d["meta"], at, K)).then_inc(xd_in[b], 16)

                source_loads(0)
                edge_loads(0)
                late(0)
                source_loads(1)
                with sp.Fori(1, iters - 1) as i:
                    edge_loads(i)
                    source_loads(i + 1)
                    late(i)
                edge_loads(iters - 1)
                late(iters - 1)

            @block.gpsimd
            def _(pool):
                top, top_node = pool.to_reg(E_pad - 1), pool.to_reg(N - 1)

                def gathers(i):
                    for b in range(PLACES):
                        apart(pool, src_in[b], 48 * i + 48, passed)
                        source_rows(pool, d, 3, b, xs, slot, row_in, top)

                def scatters(i):
                    for b in range(PLACES):
                        pool.wait_ge(xd_in[b], 32 * i + 32)
                        apart(pool, xo_done[b], i + 1, passed)
                        for k in range(K):
                            pool.indirect_dma_start(
                                d["out"], bass.IndirectOffsetOnAxis(
                                    ap=last[b][:, k, M_LAST:M_LAST + 1].bitcast(I32), axis=0),
                                xo[b][:, k, :], None, bounds_check=top_node, oob_is_err=False).then_inc(stored[b], 16)

                gathers(0)
                with pool.Fori(1, iters) as i:
                    gathers(i)
                    scatters(i - 1)
                scatters(iters - 1)
                for b in range(PLACES):
                    pool.wait_ge(stored[b], 32 * iters)

            @block.vector
            def _(dve):
                dve.memset(gm[-1][:, :, :], 0.0)
                dve.memset(gr[-1][:, :, :], 0.0).then_inc(start, 1)
                dve.wait_ge(start, 1)
                def matrices(i):
                    n = i + 1
                    for b in range(PLACES):
                        free(dve, g_done[b], i)
                        dve.wait_ge(in_[b], 32 * n)
                        runs.matrices(dve, b, meta[b][:, :, M_DST:M_DST + 1].bitcast(I32))

                def messages(i):
                    n = i + 1
                    for b in range(PLACES):
                        y = meta[b]
                        y0, yx = y[:, :, M_Y:M_Y + 1], y[:, :, M_Y + 1:M_Y + 4].unsqueeze(3)
                        fx = b_f[b % 2][:, :, 96:384].rearrange("p k (c u) -> p k c u", c=3)
                        dve.wait_ge(f_done[b], n)
                        dve.tensor_tensor(h1[b][:, :, :], b_f[b % 2][:, :, 0:CS], y0.to_broadcast([P, K, CS]), ALU.mult)
                        dve.tensor_tensor(vecs(qv[b][:, :, :]), fx[:, :, :, 0:CS], yx.to_broadcast(S64), ALU.mult)
                        dve.tensor_tensor(vecs(c1[b][:, :, :]), b_f[b % 2][:, :, CS:W96].unsqueeze(2).to_broadcast(S3),
                                          yx.to_broadcast(S3), ALU.mult)
                        dve.tensor_tensor(vecs(p1[b][:, :, :]), fx[:, :, :, CS:W96],
                                          y0.unsqueeze(3).to_broadcast(S3), ALU.mult).then_inc(f_used[b], 1)
                        dve.wait_ge(f_used[b], n)
                        dve.tensor_reduce(hq[b][:, :, :], qv[b][:, :, :].rearrange("p k (c u) -> p k u c", c=3), AX.X, ALU.add)
                        dve.tensor_tensor(c2[b][:, :, :], c1[b][:, :, :], p1[b][:, :, :], ALU.add).then_inc(mid_a[b], 1)
                        dve.wait_ge(mid_a[b], n)
                        dve.wait_ge(gt_out[b], n)
                        dve.tensor_tensor(hs[b][:, :, :], h1[b][:, :, :], hq[b][:, :, :], ALU.add).then_inc(mid_b[b], 1)
                        dve.tensor_tensor(mid[b][:, :, CS:C], c2[b][:, :, :], gate[b][:, :, CS:C], ALU.mult)
                        dve.wait_ge(mid_b[b], n)
                        dve.tensor_tensor(mid[b][:, :, 0:CS], hs[b][:, :, :], gate[b][:, :, 0:CS], ALU.mult).then_inc(mid_ready[b], 1)
                    for b in range(PLACES):
                        dve.wait_ge(seg_done[b], n)
                        for k in range(K):
                            if k:
                                dve.wait_ge(g_half[b], n)
                            elif b:
                                dve.wait_ge(g_done[b - 1], n)
                            else:
                                free(dve, g_done[-1], i)
                            pb, pk = (b, 0) if k else (b - 1, K - 1)
                            dve.scalar_tensor_tensor(gm[b][:, k, :], runs.ind[b][:, k, :], gm[pb][:, pk, P - 1:P],
                                                     b_s[b % 2][:, k, 0:P], ALU.mult, ALU.add)
                            dve.scalar_tensor_tensor(gr[b][:, k, :], runs.ind[b][0:CV, k, :], gr[pb][:, pk, P - 1:P],
                                                     b_s[b % 2][0:CV, k, P:2 * P], ALU.mult,
                                                     ALU.add).then_inc((g_done if k else g_half)[b], 1)

                def update(i):
                    n = i + 1
                    for b in range(PLACES):
                        dve.wait_ge(y_done[b], n)
                        dve.wait_ge(xd_in[b], 32 * n)
                        dve.tensor_tensor(pre[b][:, :, :], b_y[b % 2][:, :, 0:C], xd[b][:, :, 0:C], ALU.add).then_inc(pre_done[b], 1)
                    norm.vector(dve, n, pre, pre_done)

                staged(dve, iters, matrices, update, messages)

            @block.scalar
            def _(act):
                def sources(i):
                    n = i + 1
                    for b in range(PLACES):
                        act.wait_ge(s_turned[b], n)
                        act.activation(sm[b][:, :], b_t[b % 2][:, 0:K * P], ACT.Copy)
                        act.activation(sr[b][:, :], b_t[b % 2][0:CV, K * P:2 * K * P], ACT.Copy).then_inc(s_out[b], 1)
                        act.wait_ge(gt_done[b], n)
                        act.activation(gate[b][:, :, :], b_g[b % 2][:, :, 0:C], ACT.Sigmoid).then_inc(gt_out[b], 1)

                def destinations(i):
                    n = i + 1
                    for b in range(PLACES):
                        act.wait_ge(d_turned[b], n)
                        act.activation(dm[b][:, :], b_d[b % 2][:, 0:K * P], ACT.Copy)
                        act.activation(dr[b][:, :], b_d[b % 2][0:CV, K * P:2 * K * P], ACT.Copy).then_inc(d_out[b], 1)

                def results(i):
                    n = i + 1
                    norm.scalar_roots(act, n, w["eps"][:, 0:1])
                    for b in range(PLACES):
                        act.wait_ge(norm.nbd[b], n)
                        free(act, stored[b], 32 * i)
                        for k in range(K):
                            norm.scalar_apply(act, b, k, xo[b][:, k, 0:CS], pre[b][:, k, 0:CS])
                            ins = norm.scalar_apply(act, b, k, cm(xo[b][:, k, CS:C]), vec(pre[b][:, k, CS:C]))
                        ins.then_inc(xo_done[b], 1)

                staged(act, iters, sources, results, destinations)

            @block.tensor
            def _(pe):
                ident = w["ident"]

                def turn(rows, b_t):
                    for k in range(K):
                        s = slice(k * P, (k + 1) * P)
                        pe.transpose(b_t[:, s], rows[:, k, 0:P], ident[:, :])
                        ins = pe.transpose(b_t[0:CV, K * P + k * P:K * P + (k + 1) * P], rows[:, k, P:C], ident[:, :])
                    return ins

                def body(i):
                    n = i + 1
                    for b in range(PLACES):
                        pe.wait_ge(src_in[b], 48 * n)
                        pe.wait_ge(row_in[b], 32 * n)
                        if b >= 2:
                            pe.wait_ge(s_out[b - 2], n)
                        turn(xs[b], b_t[b % 2]).then_inc(s_turned[b], 1)
                        if b >= 2:
                            pe.wait_ge(gt_out[b - 2], n)
                        for k in range(K):
                            ins = pe.matmul(b_g[b % 2][:, k, 0:C], attr[b][:, k * P:(k + 1) * P], w["rad"][:, :], start=True, stop=True)
                        ins.then_inc(gt_done[b], 1)
                    pe.wait_ge(gt_out[-1], n)
                    for b in range(PLACES):
                        pe.wait_ge(s_out[b], n)
                        if b >= 2:
                            pe.wait_ge(f_used[b - 2], n)
                        elif b:
                            free(pe, pre_done[-1], i)
                        for k in range(K):
                            s = slice(k * P, (k + 1) * P)
                            pe.matmul(b_f[b % 2][:, k, 0:288], sm[b][:, s], w["g_m"][:, :], start=True, stop=True)
                            ins = pe.matmul(b_f[b % 2][:, k, 288:384], sr[b][:, s], w["g_r"][:, :], start=True, stop=True)
                        ins.then_inc(f_done[b], 1)
                    for b in range(PLACES):
                        pe.wait_ge(xd_in[b], 32 * n)
                        if b >= 2:
                            pe.wait_ge(d_out[b - 2], n)
                        turn(xd[b], b_d[b % 2]).then_inc(d_turned[b], 1)
                    for b in range(PLACES):
                        pe.wait_ge(mid_ready[b], n)
                        pe.wait_ge(runs.done[b], n)
                        if b >= 2:
                            pe.wait_ge(g_done[b - 2], n)
                        for k in range(K):
                            pe.matmul(b_s[b % 2][:, k, 0:P], mid[b][:, k, 0:P], runs.eq[b][:, k, :], start=True, stop=True)
                            ins = pe.matmul(b_s[b % 2][0:CV, k, P:2 * P], mid[b][:, k, P:C], runs.eq[b][:, k, :],
                                            start=True, stop=True)
                        ins.then_inc(seg_done[b], 1)
                    for b in range(PLACES):
                        pe.wait_ge(d_out[b], n)
                        pe.wait_ge(g_done[b], n)
                        pe.wait_ge(*((pre_done[b - 2], n) if b >= 2 else (f_used[-1], n)))
                        for k in range(K):
                            s = slice(k * P, (k + 1) * P)
                            pe.matmul(b_y[b % 2][:, k, 0:P], dm[b][:, s], w["sc3_m"][:, :], start=True, stop=False)
                            pe.matmul(b_y[b % 2][:, k, 0:P], gm[b][:, k, :], w["sc3_m"][:, :], start=False, stop=True)
                            pe.matmul(b_y[b % 2][:, k, P:C], dr[b][:, s], w["sc3_r"][0:CV, 0:CV], start=True, stop=False)
                            ins = pe.matmul(b_y[b % 2][:, k, P:C], gr[b][:, k, :], w["sc3_r"][0:CV, 0:CV], start=False, stop=True)
                        ins.then_inc(y_done[b], 1)

                body(0)
                with pe.Fori(1, iters) as i:
                    body(i)



def build(nc, ins, out):
    d = dict(ins)
    d["out"] = out
    NT = d["ends"].shape[1]
    E_pad = NT * P
    N = d["xa"].shape[0]
    d["NT"], d["E_pad"] = NT, E_pad

    def table(name, shape, dt=F32):
        d[name] = nc.dram_tensor(name, shape, dt, kind="Internal").ap()

    for n, dt in (("eint", I32), ("ends", I32), ("dst_row", I32), ("y", F32), ("attr16", F32), ("attr8", F32)):
        d["given_" + n] = d[n]
        table(n, d[n].shape, dt)
    table("slot", (N, 1), I32)
    table("meta", (E_pad, MW))
    table("B0", (E_pad, C + 1))
    for l in (1, 2, 3):
        table(f"B{l}", (E_pad, C))
    table("D0", (E_pad, C + 1))
    table("H0", (E_pad, C))
    for l in (1, 2, 3):
        table(f"D{l}", (E_pad, ROW))
    for n in ("A0", "R0", "X0", "S0"):
        table(n, (4, E_pad))
    order_edges(nc, d)
    with ExitStack() as ctx:
        w = load_weights(nc, ctx, d)
        chain(nc, w, d, "nodes", NODE_PLACES, -(-N // (NODE_PLACES * PAIR * P)), sources=False)
        chain(nc, w, d, "sources", PLACES, NT // BODY, sources=True)
        attend0(nc, w, d)
        soften0(nc, d)
        update0(nc, w, d)
        conv(nc, w, d, 1)
        conv(nc, w, d, 2)
        conv3(nc, w, d)


def layout(inputs):
    x = np.asarray(inputs["x"])
    N = x.shape[0]
    dst, src = np.asarray(inputs["dst"], np.int32), np.asarray(inputs["src"], np.int32)
    E = dst.shape[0]
    NT = -(-E // (BODY * P)) * BODY
    E_pad = NT * P

    def padded(a, fill):
        return np.concatenate([a, np.full((E_pad - E,) + a.shape[1:], fill, a.dtype)])

    def by_lane(a):
        return np.ascontiguousarray(a.reshape(NT, P, -1).transpose(1, 0, 2))

    d0, dp, sp = padded(dst, 0), padded(dst, N), padded(src, 0)
    nxt = np.concatenate([dp[1:], np.full(1, N + 1, np.int32)])
    a16, a8, a4 = (padded(np.asarray(inputs[k]), 0) for k in ("edge_attr_16", "edge_attr_8", "edge_attr_4"))
    order = np.concatenate([np.arange(CS), CS + np.arange(3 * CV).reshape(CV, 3).T.ravel()])
    out = {
        "xa": np.concatenate([x, np.asarray(inputs["node_vec1"])], 1),
        "ends": by_lane(np.stack([dp, nxt], 1)),
        "edge_ids": by_lane(np.repeat(np.arange(E_pad, dtype=np.int32)[:, None], 2, 1)),
        "eint": np.stack([sp, dp, nxt, d0], 1),
        "dst_row": np.concatenate([np.full(1, N + 1, np.int32), dp, np.full(1, N + 1, np.int32)])[None],
        "y": a4,
        "attr16": np.concatenate([a16.T, np.ones((1, E_pad), np.float32)]),
        "attr8": np.ascontiguousarray(a8.T),
        "attr_rows": np.concatenate([a16, a8], 1),
        "ws_valT": np.ascontiguousarray(np.asarray(inputs["L0_gnn_Ws_val"]).T),
        "w_rad_ext": np.concatenate([np.asarray(inputs["L3_gnn_W_rad"]).T,
                                     np.asarray(inputs["L3_gnn_b_rad"])[None]])[:, order],
    }
    for k, v in inputs.items():
        if k.startswith("L") and k not in ("L3_gnn_W_rad", "L3_gnn_b_rad"):
            v = np.asarray(v)
            out[k] = v.reshape(-1) if k == "L0_gnn_alpha_dot" else v.reshape(v.shape[0], -1)
    return {k: np.ascontiguousarray(v) for k, v in out.items()}


def kernel(**inputs):
    import concourse.bacc as bacc
    from concourse.bass_utils import run_bass_kernel_spmd as run

    nc = bacc.Bacc("TRN2", target_bir_lowering=False, num_devices=1)
    arrays = {f"in_{k}": v for k, v in layout(inputs).items()}
    ins = {k[3:]: nc.dram_tensor(k, v.shape, mybir.dt.from_np(v.dtype), kind="ExternalInput").ap()
           for k, v in arrays.items()}
    N = arrays["in_xa"].shape[0]
    out = nc.dram_tensor("out_x", (N, C), F32, kind="ExternalOutput").ap()
    build(nc, ins, out)
    r = run(nc, [arrays], core_ids=[0])
    return r.results[0]["out_x"]
```
